# Optimizing a Trainium2 kernel written in Bass

```python
import numpy as np
import jax
import jax.numpy as jnp

def _softmax(x, axis=-1):
    return jax.nn.softmax(x, axis=axis)

def _gelu(x):
    return jax.nn.gelu(x, approximate=True)

def _silu(x):
    return jax.nn.silu(x)

def _sigmoid(x):
    return jax.nn.sigmoid(x)

def _layernorm(x, axis=-1, eps=1e-05):
    m = jnp.mean(x, axis=axis, keepdims=True)
    v = jnp.var(x, axis=axis, keepdims=True)
    return (x - m) / jnp.sqrt(v + eps)

def _scatter_add(tgt, idx, src, axis=0):
    return tgt.at[idx].add(src)

def _segment_sum(src, seg, n):
    return jax.ops.segment_sum(src, seg, n)
kernel_name = 'mk_seq_preln_d2_jaxref_r8_9f075a'

def setup_inputs(seed: int=0):
    np.random.seed(seed)
    _w = jnp.asarray

    def _L0_attn_setup():
        import jax, jax.numpy as jnp
        import numpy as np
        H = 512
        D = H // 4
        key = jax.random.key(seed)
        k1, k2, k3, k4, k5 = jax.random.split(key, 5)
        x = jax.random.normal(k1, (4, 512, H), dtype=jnp.float32)
        s_in = 1.0 / np.sqrt(H)
        Wqkv = jax.random.normal(k2, (H, 3 * D), dtype=jnp.float32) * s_in
        bqkv = jax.random.normal(k3, (3 * D,), dtype=jnp.float32) * 0.01
        Wo = jax.random.normal(k4, (D, H), dtype=jnp.float32) * (1.0 / np.sqrt(D))
        bo = jax.random.normal(k5, (H,), dtype=jnp.float32) * 0.01
        return {'x': x, 'Wqkv': Wqkv, 'bqkv': bqkv, 'Wo': Wo, 'bo': bo}
    _L0_attn_in = _L0_attn_setup()

    def _L0_ffn_setup():
        import jax, jax.numpy as jnp
        import numpy as np
        HID, INTER = (512, 1792)
        B, S = (2, 256)

        def _binary_diff_weight(w, base):
            d = w - base
            coeff = jnp.mean(jnp.abs(d))
            return base + coeff * jnp.sign(d)
        key = jax.random.key(seed)
        ks = jax.random.split(key, 7)
        return {'hidden_states': jax.random.normal(ks[0], (B, S, HID), dtype=jnp.float32), 'w1': jax.random.normal(ks[1], (INTER, HID), dtype=jnp.float32) * 0.02, 'mean_w1': jax.random.normal(ks[2], (INTER, HID), dtype=jnp.float32) * 0.02, 'w2': jax.random.normal(ks[3], (HID, INTER), dtype=jnp.float32) * 0.02, 'mean_w2': jax.random.normal(ks[4], (HID, INTER), dtype=jnp.float32) * 0.02, 'w3': jax.random.normal(ks[5], (INTER, HID), dtype=jnp.float32) * 0.02, 'mean_w3': jax.random.normal(ks[6], (INTER, HID), dtype=jnp.float32) * 0.02}
    _L0_ffn_in = _L0_ffn_setup()

    def _L1_attn_setup():
        import jax, jax.numpy as jnp
        import numpy as np
        B, S, HID = (1, 256, 512)
        H, NOPE, ROPE, VD = (32, 128, 64, 128)
        QKD = NOPE + ROPE
        Q_RANK, KV_RANK = (192, 64)
        IDX_H, IDX_D, TOPK = (16, 128, 128)
        EPS, THETA = (1e-05, 10000.0)

        def rmsnorm(x, w):
            return x * jax.lax.rsqrt(jnp.mean(x * x, axis=-1, keepdims=True) + EPS) * w

        def rope_interleaved(x, pos):
            d = x.shape[-1]
            inv_freq = 1.0 / THETA ** (jnp.arange(0, d, 2, dtype=jnp.float32) / d)
            ang = pos[:, None] * inv_freq[None, :]
            cos, sin = (jnp.cos(ang), jnp.sin(ang))
            x2 = x.reshape(*x.shape[:-1], d // 2, 2)
            x0, x1 = (x2[..., 0], x2[..., 1])
            return jnp.stack([x0 * cos - x1 * sin, x1 * cos + x0 * sin], axis=-1).reshape(x.shape)
        key = jax.random.key(seed)
        ks = jax.random.split(key, 12)
        s = 0.02
        return {'hidden_states': jax.random.normal(ks[0], (B, S, HID), jnp.float32), 'q_a_w': jax.random.normal(ks[1], (HID, Q_RANK), jnp.float32) * s, 'q_a_norm_w': jnp.ones((Q_RANK,), jnp.float32), 'q_b_w': jax.random.normal(ks[2], (Q_RANK, H * QKD), jnp.float32) * s, 'kv_a_w': jax.random.normal(ks[3], (HID, KV_RANK + ROPE), jnp.float32) * s, 'kv_a_norm_w': jnp.ones((KV_RANK,), jnp.float32), 'kv_b_w': jax.random.normal(ks[4], (KV_RANK, H * (NOPE + VD)), jnp.float32) * s, 'o_w': jax.random.normal(ks[5], (H * VD, HID), jnp.float32) * s, 'idx_wq_w': jax.random.normal(ks[6], (HID, IDX_H * IDX_D), jnp.float32) * s, 'idx_wk_w': jax.random.normal(ks[7], (HID, IDX_D), jnp.float32) * s, 'idx_weights_w': jax.random.normal(ks[8], (HID, IDX_H), jnp.float32) * s}
    _L1_attn_in = _L1_attn_setup()

    def _L1_ffn_setup():
        import jax, jax.numpy as jnp
        import numpy as np
        B_, S, D_IN, D_OUT = (4, 256, 512, 512)
        N, RANK, ALPHA = (8, 16, 32)
        SCALE = ALPHA / RANK
        key = jax.random.key(seed)
        kx, ka, kb, kw, kbias = jax.random.split(key, 5)
        x = jax.random.normal(kx, (B_, S, D_IN), dtype=jnp.float32)
        lora_A = jax.random.normal(ka, (N, RANK, D_IN), dtype=jnp.float32) * (1.0 / np.sqrt(D_IN))
        lora_B = jax.random.normal(kb, (N, D_OUT, RANK), dtype=jnp.float32) * (1.0 / np.sqrt(RANK))
        W = jax.random.normal(kw, (D_OUT, D_IN), dtype=jnp.float32) * (1.0 / np.sqrt(D_IN))
        bias = jax.random.normal(kbias, (D_OUT,), dtype=jnp.float32) * 0.01
        lora_weights = jnp.full((N,), 1.0 / N, dtype=jnp.float32)
        return {'x': x, 'lora_A': lora_A, 'lora_B': lora_B, 'W': W, 'bias': bias, 'lora_weights': lora_weights}
    _L1_ffn_in = _L1_ffn_setup()
    _d = {'L0_attn_x': _L0_attn_in['x'], 'L0_attn_Wqkv': _L0_attn_in['Wqkv'], 'L0_attn_bqkv': _L0_attn_in['bqkv'], 'L0_attn_Wo': _L0_attn_in['Wo'], 'L0_attn_bo': _L0_attn_in['bo'], 'L0_ffn_w1': _L0_ffn_in['w1'], 'L0_ffn_mean_w1': _L0_ffn_in['mean_w1'], 'L0_ffn_w2': _L0_ffn_in['w2'], 'L0_ffn_mean_w2': _L0_ffn_in['mean_w2'], 'L0_ffn_w3': _L0_ffn_in['w3'], 'L0_ffn_mean_w3': _L0_ffn_in['mean_w3'], 'L1_attn_q_a_w': _L1_attn_in['q_a_w'], 'L1_attn_q_a_norm_w': _L1_attn_in['q_a_norm_w'], 'L1_attn_q_b_w': _L1_attn_in['q_b_w'], 'L1_attn_kv_a_w': _L1_attn_in['kv_a_w'], 'L1_attn_kv_a_norm_w': _L1_attn_in['kv_a_norm_w'], 'L1_attn_kv_b_w': _L1_attn_in['kv_b_w'], 'L1_attn_o_w': _L1_attn_in['o_w'], 'L1_attn_idx_wq_w': _L1_attn_in['idx_wq_w'], 'L1_attn_idx_wk_w': _L1_attn_in['idx_wk_w'], 'L1_attn_idx_weights_w': _L1_attn_in['idx_weights_w'], 'L1_ffn_lora_A': _L1_ffn_in['lora_A'], 'L1_ffn_lora_B': _L1_ffn_in['lora_B'], 'L1_ffn_W': _L1_ffn_in['W'], 'L1_ffn_bias': _L1_ffn_in['bias'], 'L1_ffn_lora_weights': _L1_ffn_in['lora_weights']}
    _x0 = _d['L0_attn_x']
    _d['L0_attn_x'] = jax.random.normal(jax.random.fold_in(jax.random.key(seed), 1), (1, 1024, 512), dtype=_x0.dtype)
    del _x0
    return _d

def reference(L0_attn_x, L0_attn_Wqkv, L0_attn_bqkv, L0_attn_Wo, L0_attn_bo, L0_ffn_w1, L0_ffn_mean_w1, L0_ffn_w2, L0_ffn_mean_w2, L0_ffn_w3, L0_ffn_mean_w3, L1_attn_q_a_w, L1_attn_q_a_norm_w, L1_attn_q_b_w, L1_attn_kv_a_w, L1_attn_kv_a_norm_w, L1_attn_kv_b_w, L1_attn_o_w, L1_attn_idx_wq_w, L1_attn_idx_wk_w, L1_attn_idx_weights_w, L1_ffn_lora_A, L1_ffn_lora_B, L1_ffn_W, L1_ffn_bias, L1_ffn_lora_weights):

    def _L0_attn_ref(x, Wqkv, bqkv, Wo, bo):
        import jax, jax.numpy as jnp
        import numpy as np
        H = 512
        D = H // 4
        B, S, C = x.shape
        d = C // 4
        qkv = jnp.einsum('bsc,cf->bsf', x, Wqkv) + bqkv
        qkv = qkv.reshape(B, S, 3, d)
        q, k, v = (qkv[:, :, 0], qkv[:, :, 1], qkv[:, :, 2])
        scale = 1.0 / jnp.sqrt(jnp.float32(d)).astype(x.dtype)
        attn = jnp.einsum('bqd,bkd->bqk', q, k) * scale
        attn = jax.nn.softmax(attn, axis=-1)
        out = jnp.einsum('bqk,bkd->bqd', attn, v)
        return jnp.einsum('bqd,dc->bqc', out, Wo) + bo

    def _L0_ffn_ref(hidden_states, w1, mean_w1, w2, mean_w2, w3, mean_w3):
        import jax, jax.numpy as jnp
        import numpy as np
        HID, INTER = (512, 1792)
        B, S = (2, 256)

        def _binary_diff_weight(w, base):
            d = w - base
            coeff = jnp.mean(jnp.abs(d))
            return base + coeff * jnp.sign(d)
        W1 = _binary_diff_weight(w1, mean_w1)
        W2 = _binary_diff_weight(w2, mean_w2)
        W3 = _binary_diff_weight(w3, mean_w3)
        gate = jnp.einsum('bsh,ih->bsi', hidden_states, W1)
        up = jnp.einsum('bsh,ih->bsi', hidden_states, W3)
        h = jax.nn.silu(gate) * up
        return jnp.einsum('bsi,hi->bsh', h, W2)

    def _L1_attn_ref(hidden_states, q_a_w, q_a_norm_w, q_b_w, kv_a_w, kv_a_norm_w, kv_b_w, o_w, idx_wq_w, idx_wk_w, idx_weights_w):
        import jax, jax.numpy as jnp
        import numpy as np
        B, S, HID = (1, 256, 512)
        H, NOPE, ROPE, VD = (32, 128, 64, 128)
        QKD = NOPE + ROPE
        Q_RANK, KV_RANK = (192, 64)
        IDX_H, IDX_D, TOPK = (16, 128, 128)
        EPS, THETA = (1e-05, 10000.0)

        def rmsnorm(x, w):
            return x * jax.lax.rsqrt(jnp.mean(x * x, axis=-1, keepdims=True) + EPS) * w

        def rope_interleaved(x, pos):
            d = x.shape[-1]
            inv_freq = 1.0 / THETA ** (jnp.arange(0, d, 2, dtype=jnp.float32) / d)
            ang = pos[:, None] * inv_freq[None, :]
            cos, sin = (jnp.cos(ang), jnp.sin(ang))
            x2 = x.reshape(*x.shape[:-1], d // 2, 2)
            x0, x1 = (x2[..., 0], x2[..., 1])
            return jnp.stack([x0 * cos - x1 * sin, x1 * cos + x0 * sin], axis=-1).reshape(x.shape)
        b, s, _ = hidden_states.shape
        pos = jnp.arange(s, dtype=jnp.float32)
        q_lat = rmsnorm(hidden_states @ q_a_w, q_a_norm_w)
        q = (q_lat @ q_b_w).reshape(b, s, H, QKD).transpose(0, 2, 1, 3)
        q_nope, q_pe = (q[..., :NOPE], q[..., NOPE:])
        ckv = hidden_states @ kv_a_w
        kv_lat, k_pe = (ckv[..., :KV_RANK], ckv[..., KV_RANK:])
        kv = (rmsnorm(kv_lat, kv_a_norm_w) @ kv_b_w).reshape(b, s, H, NOPE + VD).transpose(0, 2, 1, 3)
        k_nope, v = (kv[..., :NOPE], kv[..., NOPE:])
        q_pe = rope_interleaved(q_pe, pos)
        k_pe = rope_interleaved(k_pe[:, None, :, :], pos)
        scores = (jnp.einsum('bhqd,bhkd->bhqk', q_nope, k_nope) + jnp.einsum('bhqd,bhkd->bhqk', q_pe, k_pe)) * QKD ** (-0.5)
        iq = (hidden_states @ idx_wq_w).reshape(b, s, IDX_H, IDX_D)
        ik = hidden_states @ idx_wk_w
        iw = hidden_states @ idx_weights_w * IDX_H ** (-0.5)
        idx_scores = jnp.einsum('bqn,bnqk->bqk', iw, jax.nn.relu(jnp.einsum('bqnd,bkd->bnqk', iq, ik))) * IDX_D ** (-0.5)
        causal = pos[:, None] >= pos[None, :]
        idx_scores = jnp.where(causal, idx_scores, -jnp.inf)
        _, topk_idx = jax.lax.top_k(idx_scores, TOPK)
        bi = jnp.arange(b)[:, None, None]
        qi = jnp.arange(s)[None, :, None]
        topk_mask = jnp.zeros((b, s, s), bool).at[bi, qi, topk_idx].set(True)
        mask = topk_mask & causal
        scores = jnp.where(mask[:, None], scores, -jnp.inf)
        attn = jax.nn.softmax(scores, axis=-1)
        out = jnp.einsum('bhqk,bhkd->bqhd', attn, v).reshape(b, s, H * VD)
        return out @ o_w

    def _L1_ffn_ref(x, lora_A, lora_B, W, bias, lora_weights):
        import jax, jax.numpy as jnp
        import numpy as np
        B_, S, D_IN, D_OUT = (4, 256, 512, 512)
        N, RANK, ALPHA = (8, 16, 32)
        SCALE = ALPHA / RANK
        h = jnp.einsum('bsd,nrd->nbsr', x, lora_A)
        coef = (SCALE * lora_weights)[:, None, None]
        lora_out = jnp.einsum('nbsr,nor->bso', h, lora_B * coef)
        base = jnp.einsum('bsd,od->bso', x, W) + bias
        return base + lora_out
    x = L0_attn_x
    x = x + _L0_attn_ref(_layernorm(x, axis=-1), L0_attn_Wqkv, L0_attn_bqkv, L0_attn_Wo, L0_attn_bo)
    x = x + _L0_ffn_ref(_layernorm(x, axis=-1), L0_ffn_w1, L0_ffn_mean_w1, L0_ffn_w2, L0_ffn_mean_w2, L0_ffn_w3, L0_ffn_mean_w3)
    x = x + _L1_attn_ref(_layernorm(x, axis=-1), L1_attn_q_a_w, L1_attn_q_a_norm_w, L1_attn_q_b_w, L1_attn_kv_a_w, L1_attn_kv_a_norm_w, L1_attn_kv_b_w, L1_attn_o_w, L1_attn_idx_wq_w, L1_attn_idx_wk_w, L1_attn_idx_weights_w)
    x = x + _L1_ffn_ref(_layernorm(x, axis=-1), L1_ffn_lora_A, L1_ffn_lora_B, L1_ffn_W, L1_ffn_bias, L1_ffn_lora_weights)
    return x

_drawn_inputs = setup_inputs


def setup_inputs(seed=0):
    import zlib

    import numpy as np

    out = dict(_drawn_inputs(seed))
    spreads = {'L1_attn_q_a_norm_w': (1.0, 0.6),
     'L1_attn_kv_a_norm_w': (1.0, 0.6),
     'L1_ffn_lora_weights': (0.125, 0.2)}
    factors = {'L0_attn_bqkv': 4.53,
     'L0_attn_bo': 5.91,
     'L1_attn_q_a_w': 8.0,
     'L1_attn_q_b_w': 8.0,
     'L1_attn_idx_wq_w': 3.453,
     'L1_attn_idx_wk_w': 3.426,
     'L1_attn_idx_weights_w': 3.438,
     'L1_ffn_bias': 8.0}
    for name, (base, spread) in spreads.items():
        noise = np.random.default_rng([zlib.crc32(name.encode()), seed]).standard_normal(out[name].shape)
        drawn = base * np.exp(spread * noise) if base else spread * noise
        out[name] = jnp.asarray(drawn.astype(out[name].dtype))
    for name, factor in factors.items():
        out[name] = (out[name] * factor).astype(out[name].dtype)
    return out
```

```python
from contextlib import ExitStack

import numpy as np

import concourse.bass as bass
from concourse import mybir

F32 = mybir.dt.float32
F32R = mybir.dt.float32r
BF16 = mybir.dt.bfloat16
I8 = mybir.dt.int8
ALU = mybir.AluOpType
ACT = mybir.ActivationFunctionType
AXX = mybir.AxisListType.X

P = 128
S = 1024
HID = 512
NT = S // P
NK = HID // P
D0 = 128
INTER = 1792
NI = INTER // P
HEADS, NOPE, ROPE, VD = 32, 128, 64, 128
QKD = NOPE + ROPE
QR, KR = 192, 64
IDXH, IDXD, TOPK = 16, 128, 128
PAIRS = HEADS // 2
LATW = QR + KR + ROPE + IDXH
LORA_N, LORA_R, LORA_SCALE = 8, 16, 2.0
EPS = 1e-5
BIG = 1.0e30
FUTURE = -3.0e38
TAKEN = -3.3e38
WCHUNKS = 2 * NI + 16
TRI = [P * (t * (t + 1) // 2) for t in range(NT + 1)]


def ds(start, size):
    return bass.ds(start, size)


ATT_ORDER = [("S", 0), ("S", 1), ("T", 0), ("S", 2), ("T", 1), ("S", 3), ("T", 2), ("S", 4), ("T", 3), ("S", 5),
             ("O", 0), ("T", 4), ("Y", 0), ("Y", 1), ("Y", 2), ("Y", 3), ("S", 6), ("T", 5), ("S", 7), ("T", 6),
             ("T", 7), ("O", 1), ("Y", 4), ("Y", 5), ("Y", 6), ("Y", 7)]

HEAD_ORDER = []
for _i in range(16):
    HEAD_ORDER.append(("S", _i))
    if _i >= 7 and _i % 4 == 3:
        HEAD_ORDER.append(("V", _i // 4 - 1))
    if _i >= 3:
        HEAD_ORDER.append(("T", _i - 3))
HEAD_ORDER += [("Q", 0), ("T", 13), ("R", 0), ("T", 14), ("T", 15)] + [("Y", _t) for _t in range(4)]
HEAD_ORDER += [("V", 3), ("Q", 1), ("Y", 4), ("Y", 5), ("R", 1), ("Y", 6), ("Y", 7)]
EVAC_ORDER = list(HEAD_ORDER)
for _n in range(len(EVAC_ORDER) - 1):
    if EVAC_ORDER[_n][0] == "S" and EVAC_ORDER[_n + 1][0] == "T":
        EVAC_ORDER[_n:_n + 2] = EVAC_ORDER[_n + 1], EVAC_ORDER[_n]
Q_BANKS = ((2, 0, 1), (4, 3, 2))

GROUPS = []
for _i in range(16):
    GROUPS.append([])
    for _c in range(1 if _i % NT < 4 else 2):
        GROUPS[_i].append((_c, sum(map(len, GROUPS))))
NG = sum(map(len, GROUPS))


def build(nc, x_in, wqkv, bqkv, wo, bo, w1, m1, w2, m2, w3, m3, qa, qan, qb, kva, kvan, kvb, ow,
          iwq, iwk, iww, lA, lB, lW, lbias, lcoef, cos_q, sin_q, cos_k, sin_k, out,
          wabs_d, wabs_rem_d, wuvo_d):
    ctx = ExitStack()
    with ctx:
        def sem(name):
            return ctx.enter_context(nc.semaphore(name))

        def sbin(scope, name, shape, dt=F32):
            return scope.enter_context(nc.sbuf_tensor(name, shape, dt))

        def sb(name, shape, dt=F32):
            return sbin(ctx, name, shape, dt)

        x = sb("x", [P, NT * HID])
        xn_h = sb("xn_h", [P, NK, S], F32R)
        xn_l = sb("xn_l", [P, NK, S], F32R)
        ident = sb("ident", [P, P])
        ones = sb("ones", [P, P])
        stats = sb("stats", [P, NT * 6])
        mv = sb("mv", [P, NT, 2])
        rs_var = sb("rs_var", [P, 16])
        rs_sqrt = sb("rs_sqrt", [P, 16])
        rs_out = sb("rs_out", [P, 16])
        rs_tmp = sb("rs_tmp", [P, 16])
        row_bc = sb("row_bc", [P, HID])
        xn_t = sb("xn_t", [P, 2, HID])
        ps = ctx.enter_context(nc.psum_tensor("ps", [P, 8, 512], F32))

        pTx_h = xn_h[:].rearrange("p k s -> p (k s)").rearrange("p (b q) -> p b q", q=512)
        pTx_l = xn_l[:].rearrange("p k s -> p (k s)").rearrange("p (b q) -> p b q", q=512)

        w_scope = ExitStack()
        base = [sbin(w_scope, f"base{m}", [P, NI * 512]) for m in range(3)]
        sgn = [sbin(w_scope, f"sgn{m}", [P, NI * 512], I8) for m in range(3)]
        absum = sbin(w_scope, "absum", [P, WCHUNKS])
        coef = sbin(w_scope, "coef", [P, 3])
        a_scope = ExitStack()
        qkT_h = sbin(a_scope, "qkT_h", [P, 2, S], F32R)
        qkT_l = sbin(a_scope, "qkT_l", [P, 2, S], F32R)
        v_h = sbin(a_scope, "v_h", [P, NT, D0], F32R)
        v_l = sbin(a_scope, "v_l", [P, NT, D0], F32R)
        bq_col = sbin(a_scope, "bq_col", [P, 2])
        bv_bc = sbin(a_scope, "bv_bc", [P, D0])
        wo_h = sbin(a_scope, "wo_h", [P, HID], F32R)
        wo_l = sbin(a_scope, "wo_l", [P, HID], F32R)
        sm0 = sbin(a_scope, "sm0", [P, 4 * NT])
        wring = sbin(a_scope, "wring", [P, 3, 512])
        q_scope = ExitStack()
        wqkv_h = sbin(q_scope, "wqkv_h", [P, NK, 3 * D0], F32R)
        wqkv_l = sbin(q_scope, "wqkv_l", [P, NK, 3 * D0], F32R)
        q_scope.close()
        p0 = sbin(a_scope, "p0", [P, 2, S])
        oT_h = sbin(a_scope, "oT_h", [P, 512], F32R)
        oT_l = sbin(a_scope, "oT_l", [P, 512], F32R)
        a_scope.close()
        f_scope = ExitStack()
        weff = sbin(f_scope, "weff", [P, 3, 512])
        wc_h = sbin(f_scope, "wc_h", [P, 2, 3, 512], F32R)
        wc_l = sbin(f_scope, "wc_l", [P, 2, 3, 512], F32R)
        silu = sbin(f_scope, "silu", [P, 512])
        hf = sbin(f_scope, "hf", [P, 512])
        hT_h = sbin(f_scope, "hT_h", [P, 2, 512], F32R)
        hT_l = sbin(f_scope, "hT_l", [P, 2, 512], F32R)
        f_scope.close()
        w_scope.close()

        l_scope = ExitStack()
        latT_h = sbin(l_scope, "latT_h", [P, 4, S], F32R)
        latT_l = sbin(l_scope, "latT_l", [P, 4, S], F32R)
        v3 = sbin(l_scope, "v3", [P, NT, 3 * KR], F32R)
        mbias = sbin(l_scope, "mbias", [P, TRI[NT]], BF16)
        cosq = sbin(l_scope, "cosq", [P, S])
        sinq = sbin(l_scope, "sinq", [P, S])
        i_scope = ExitStack()
        iw = sbin(i_scope, "iw", [P, NT, IDXH])
        ikT_h = sbin(i_scope, "ikT_h", [P, S], F32R)
        ikT_l = sbin(i_scope, "ikT_l", [P, S], F32R)
        iqT_h = sbin(i_scope, "iqT_h", [P, S], F32R)
        iqT_l = sbin(i_scope, "iqT_l", [P, S], F32R)
        iwq_raw = sbin(i_scope, "iwq_raw", [P, NK, IDXD])
        iwq_h = sbin(i_scope, "iwq_h", [P, NK, IDXD], F32R)
        iwq_l = sbin(i_scope, "iwq_l", [P, NK, IDXD], F32R)
        relu = sbin(i_scope, "relu", [P, 2, S])
        acc = sbin(i_scope, "acc", [P, TRI[NT] - P])
        top8 = sbin(i_scope, "top8", [P, 8])
        t_scope = ExitStack()
        lat = sbin(t_scope, "lat", [P, NT, LATW])
        latn = sbin(t_scope, "latn", [P, NT, 384])
        lat_sq = sbin(t_scope, "lat_sq", [P, NT, QR])
        norm_bc = sbin(t_scope, "norm_bc", [P, QR + KR])
        cosk = sbin(t_scope, "cosk", [P, NT, ROPE // 2])
        sink = sbin(t_scope, "sink", [P, NT, ROPE // 2])
        rope_t = sbin(t_scope, "rope_t", [P, 2, NT, ROPE // 2])
        wlat_h = sbin(t_scope, "wlat_h", [P, NK, LATW], F32R)
        wlat_l = sbin(t_scope, "wlat_l", [P, NK, LATW], F32R)
        wlat_raw = sbin(t_scope, "wlat_raw", [P, NK, LATW])
        t_scope.close()
        r_scope = ExitStack()
        qb_raw = sbin(r_scope, "qb_raw", [P, 2, 2 * QKD])
        kvb_raw = sbin(r_scope, "kvb_raw", [KR, 512])
        ow_raw = sbin(r_scope, "ow_raw", [P, 2, HID])
        qbT = sbin(r_scope, "qbT", [P, 2, QR])
        kvbT = sbin(r_scope, "kvbT", [P, 4, KR])
        pr_out = sbin(r_scope, "pr_out", [P, 256 + 512])
        r_scope.close()
        i_scope.close()
        h_scope = ExitStack()
        wc_raw = sbin(h_scope, "wc_raw", [P, 2, 256])
        wq_h = sbin(h_scope, "wq_h", [P, 2, 384], F32R)
        wq_l = sbin(h_scope, "wq_l", [P, 2, 384], F32R)
        wuvo_raw = sbin(h_scope, "wuvo_raw", [P, HID])
        wuvo_h = sbin(h_scope, "wuvo_h", [P, HID], F32R)
        wuvo_l = sbin(h_scope, "wuvo_l", [P, HID], F32R)
        rop = sbin(h_scope, "rop", [P, 2, 512])
        qc_h = sbin(h_scope, "qc_h", [P, 2, S], F32R)
        qc_l = sbin(h_scope, "qc_l", [P, 2, S], F32R)
        pm = sbin(h_scope, "pm", [P, 4, S])
        smx = sbin(h_scope, "smx", [P, 48])
        ycp = sbin(h_scope, "ycp", [P, 4, HID])
        pTa_h = sbin(h_scope, "pTa_h", [P, 4, 512], F32R)
        pTa_l = sbin(h_scope, "pTa_l", [P, 4, 512], F32R)
        ol_half = sbin(h_scope, "ol_half", [P, 512])
        ol_f = sbin(h_scope, "ol_f", [P, 512])
        ol_h = sbin(h_scope, "ol_h", [P, S], F32R)
        ol_l = sbin(h_scope, "ol_l", [P, S], F32R)
        h_scope.close()
        l_scope.close()

        e_scope = ExitStack()
        lA_sb = sbin(e_scope, "lA_sb", [P, HID])
        lB_sb = sbin(e_scope, "lB_sb", [P, NK, P])
        lBT = sbin(e_scope, "lBT", [P, HID])
        lc_col = sbin(e_scope, "lc_col", [P, 1])
        lc2_col = sbin(e_scope, "lc2_col", [P, 1])
        lW_sb = sbin(e_scope, "lW_sb", [P, NK, HID])
        lWT = sbin(e_scope, "lWT", [P, NK, HID])
        wfin_f = sbin(e_scope, "wfin_f", [P, NK, HID])
        wfin_h = sbin(e_scope, "wfin_h", [P, NK, HID], F32R)
        wfin_l = sbin(e_scope, "wfin_l", [P, NK, HID], F32R)
        e_scope.close()

        def sems(prefix, names):
            return [sem(prefix + n) for n in names.split()]

        ld_x, ld_a, ld_l, ld_e = sems("ld_", "x a l e")
        ld_w = sems("ld_w", "0 1 2")
        consts, phase, st_out, passed = sem("consts"), sem("phase"), sem("st_out"), sem("passed")
        ln_xn, ln_tr, ln_hi, ln_lo = sems("ln_", "xn tr hi lo")
        rs_v, rs_s = sems("rs_", "v s")
        at_w, at_proj, at_q, at_qkv, at_v = sems("at_", "w proj q qkv v")
        at_s, at_max, at_exp, at_tr, at_hi, at_lo = sems("at_", "s max exp tr hi lo")
        at_o, at_ohi, at_ot, at_y, at_x = sems("at_", "o ohi ot y x")
        wt_d, wt_abs, wt_tot, wt_coef = sems("wt_", "d abs tot coef")
        ff_we, ff_tr, ff_hi, ff_lo = sems("ff_", "we tr hi lo")
        ff_gate, ff_up, ff_silu, ff_mul, ff_hhi, ff_h, ff_y, ff_x = sems("ff_", "gate up silu mul hhi h y x")
        lt_w, lt_mm, lt_ev, lt_norm, lt_tr, lt_hi, lt_lo = sems("lt_", "w mm ev norm tr hi lo")
        ix_ld, ix_w, ix_q, ix_qhi, ix_qlo, ix_s, ix_r, ix_acc, ix_mask = sems("ix_", "ld w q qhi qlo s r acc mask")
        pr_ldq, pr_ldo, pr_t, pr_tev, pr_mm, pr_st = sems("pr_", "ldq ldo t tev mm st")
        hd_ldq, hd_ldu, hd_wq, hd_wu, hd_q, hd_rot, hd_qhi, hd_qlo = sems("hd_", "ldq ldu wq wu q rot qhi qlo")
        hd_s, hd_max, hd_exp, hd_rec, hd_p, hd_tr, hd_hi, hd_lo = sems("hd_", "s max exp rec p tr hi lo")
        hd_o, hd_ocp, hd_of, hd_ohi, hd_olo = sems("hd_", "o ocp of ohi olo")
        hd_y, hd_x, hd_yc, hd_yx = sems("hd_", "y x yc yx")
        en_tb, en_tw, en_bt, en_wt, en_c, en_mm, en_w, en_y, en_o = sems("en_", "tb tw bt wt c mm w y o")

        block = ctx.enter_context(nc.Block())

        def meet(e, n):
            e.drain().then_inc(phase, 1)
            e.wait_ge(phase, 5 * n)

        def wait_apart(e, s, value):
            e.wait_ge(s, value)
            e.sem_inc(passed, 1)

        def f(ap):
            return ap.bitcast(F32)

        def mm3(pe, dst, lh, ll, rh, rl, start, stop):
            pe.matmul(dst, lh, rl, start=start, stop=False)
            pe.matmul(dst, ll, rh, start=False, stop=False)
            return pe.matmul(dst, lh, rh, start=False, stop=stop)

        def tile(t):
            return slice(t * P, (t + 1) * P)

        def xt(t):
            return x[:, t * HID:(t + 1) * HID]

        def two_banks(b, w=1024):
            return ps[:, b:b + 2, :].rearrange("p a n -> p (a n)")[:, 0:w]

        def wt_chunk(chunk):
            m = min(chunk // NI, 2)
            return m, chunk - NI * m, 512 if m < 2 else 448

        def row(v, n, parts=P):
            return v.rearrange("(a n) -> a n", a=1).broadcast_to([parts, n])

        @block.sync
        def _(sp):
            for t in range(NT):
                sp.dma_start(xt(t), x_in[0, tile(t), :]).then_inc(ld_x, 16)
            sp.dma_start(base[2][:, 0:NK * 3 * D0].rearrange("p (k n) -> p k n", k=NK),
                         wqkv.rearrange("(k p) n -> p k n", p=P)).then_inc(ld_a, 16)
            sp.dma_start(base[2][:, 2048:2048 + HID], wo).then_inc(ld_a, 16)
            with nc.allow_non_contiguous_dma(reason="a small bias column"):
                sp.dma_start(bq_col[:], bqkv[0:2 * D0].rearrange("(a p) -> p a", p=P)).then_inc(ld_a, 16)
            sp.dma_start(bv_bc[:], row(bqkv[2 * D0:3 * D0], D0)).then_inc(ld_a, 16)
            sp.dma_start(row_bc[:], row(bo, HID)).then_inc(ld_a, 16)
            pairs = ((w1, m1), (w3, m3), (w2, m2))
            for chunk in range(WCHUNKS):
                m, s, width = wt_chunk(chunk)
                rows, mrows = (a.rearrange("(c p) n -> p c n", p=P) for a in pairs[m])
                dst = base[m][:, s * width:(s + 1) * width]
                slot = wring[:, chunk % 3, 0:width]
                if m < 2:
                    ws, ms = rows[:, s, :], mrows[:, s, :]
                else:
                    c = slice((s % 4) * 448, (s % 4) * 448 + 448)
                    ws, ms = rows[:, s // 4, c], mrows[:, s // 4, c]
                if chunk == 2 * NI:
                    sp.wait_ge(at_w, 1)
                if chunk >= 3:
                    sp.wait_ge(wt_abs, chunk - 2)
                sp.dma_start(dst, ms).then_inc(ld_w[chunk % 3], 16)
                sp.dma_start(slot, ws).then_inc(ld_w[chunk % 3], 16)
            meet(sp, 1)
            meet(sp, 2)
            for k in range(NK):
                sp.dma_start(wlat_raw[:, k, 0:QR], qa[tile(k), :]).then_inc(ld_l, 16)
                sp.dma_start(wlat_raw[:, k, QR:QR + KR + ROPE], kva[tile(k), :]).then_inc(ld_l, 16)
                sp.dma_start(wlat_raw[:, k, QR + KR + ROPE:LATW], iww[tile(k), :]).then_inc(ld_l, 16)
            sp.dma_start(norm_bc[:, 0:QR], row(qan, QR)).then_inc(ld_l, 16)
            sp.dma_start(norm_bc[:, QR:QR + KR], row(kvan, KR)).then_inc(ld_l, 16)
            sp.dma_start(cosk[:], cos_k).then_inc(ld_l, 16)
            sp.dma_start(sink[:], sin_k).then_inc(ld_l, 16)
            sp.dma_start(cosq[:], cos_q).then_inc(ld_l, 16)
            sp.dma_start(sinq[:], sin_q).then_inc(ld_l, 16)
            sp.dma_start(iwq_raw[:], iwk.rearrange("(k p) n -> p k n", p=P)).then_inc(ix_ld, 16)
            with sp.Fori(0, IDXH) as n:
                sp.wait_ge(ix_w, n + 1)
                sp.dma_start(iwq_raw[:], iwq.rearrange("(k p) n -> p k n", p=P)[:, :, ds(n * IDXD, IDXD)])\
                    .then_inc(ix_ld, 16)
            sp.wait_ge(lt_lo, NT)
            with sp.Fori(0, PAIRS) as j:
                sp.wait_ge(pr_t, 2 * j + 1)
                sp.dma_start(qb_raw[:, 0, :], qb[0:P, ds(j * 2 * QKD, 2 * QKD)]).then_inc(pr_ldq, 16)
                sp.dma_start(qb_raw[0:QR - P, 1, :], qb[P:QR, ds(j * 2 * QKD, 2 * QKD)]).then_inc(pr_ldq, 16)
                sp.dma_start(kvb_raw[:], kvb[:, ds(j * 512, 512)]).then_inc(pr_ldq, 16)
                sp.wait_ge(pr_mm, j + 1)
                sp.dma_start(ow_raw[:], ow[ds(j * 256, 256), :].rearrange("(a p) n -> p a n", p=P)).then_inc(pr_ldo, 16)
            meet(sp, 3)

            def load_wc(j):
                sp.dma_start(wc_raw[:, 0, 0:P], wabs_d[:, ds(j * P, P)]).then_inc(hd_ldq, 16)
                sp.dma_start(wc_raw[0:QR - P, 1, 0:P], wabs_rem_d[:, ds(j * P, P)]).then_inc(hd_ldq, 16)
                for a in range(2):
                    c = slice(P + a * ROPE, P + (a + 1) * ROPE)
                    src = ds(j * 2 * QKD + (1 - a) * QKD + NOPE, ROPE)
                    sp.dma_start(wc_raw[:, 0, c], qb[0:P, src]).then_inc(hd_ldq, 16)
                    sp.dma_start(wc_raw[0:QR - P, 1, c], qb[P:QR, src]).then_inc(hd_ldq, 16)

            load_wc(0)
            sp.dma_start(wuvo_raw[:], wuvo_d[0:P, :]).then_inc(hd_ldu, 16)
            with sp.Fori(1, PAIRS) as j:
                sp.wait_ge(hd_wu, j)
                sp.dma_start(wuvo_raw[:], wuvo_d[ds(j * P, P), :]).then_inc(hd_ldu, 16)
                wait_apart(sp, hd_wq, j)
                load_wc(j)
            meet(sp, 4)
            sp.dma_start(lA_sb[:], lA.rearrange("n r d -> (n r) d")).then_inc(ld_e, 16)
            for k in range(NK):
                sp.dma_start(lB_sb[:, k, :].rearrange("p (n r) -> p n r", n=LORA_N),
                             lB[:, tile(k), :].rearrange("n p r -> p n r")).then_inc(ld_e, 16)
            for n in range(LORA_N):
                sp.dma_start(lc_col[n * LORA_R:(n + 1) * LORA_R, :], row(lcoef[n:n + 1], 1, LORA_R)).then_inc(ld_e, 16)
            sp.dma_start(lW_sb[:], lW.rearrange("(k p) n -> p k n", p=P)).then_inc(ld_e, 16)
            sp.dma_start(row_bc[:], row(lbias, HID)).then_inc(ld_e, 16)
            for t in range(NT):
                sp.wait_ge(en_o, t + 1)
                sp.dma_start(out[0, tile(t), :], xt(t)).then_inc(st_out, 16)
            sp.wait_ge(st_out, 16 * NT)

        @block.gpsimd
        def _(pool):
            pool.memset(ident[:], 0.0)
            pool.memset(ones[:], 1.0)
            pool.drain()
            pool.affine_select(out=ident[:], in_=ident[:], compare_op=ALU.not_equal, fill=1.0, base=0,
                               pattern=[[-1, P]], channel_multiplier=1)
            pool.drain().then_inc(consts, 1)
            for chunk in range(WCHUNKS):
                m, s, width = wt_chunk(chunk)
                slot = wring[:, chunk % 3, 0:width]
                pool.wait_ge(ld_w[chunk % 3], 32 * (chunk // 3 + 1))
                pool.tensor_tensor(slot, slot, base[m][:, s * width:(s + 1) * width], ALU.subtract).then_inc(wt_d, 1)
            meet(pool, 1)
            meet(pool, 2)
            pool.memset(mbias[:, 0:P], 0.0)
            pool.drain()
            pool.affine_select(out=mbias[:, 0:P], in_=mbias[:, 0:P], compare_op=ALU.is_ge, fill=BIG, base=0,
                               pattern=[[-1, P]], channel_multiplier=1).then_inc(ix_mask, 1)

            def split_index():
                pool.tensor_copy(iwq_h[:], iwq_raw[:])
                pool.drain()
                pool.tensor_tensor(iwq_l[:], iwq_raw[:], f(iwq_h[:]), ALU.subtract).then_inc(ix_w, 1)

            pool.wait_ge(ix_ld, 16)
            split_index()
            with pool.Fori(0, IDXH) as n:
                pool.drain()
                pool.wait_ge(ix_ld, 16 * n + 32)
                wait_apart(pool, ix_q, 2 * n + 2)
                split_index()
            pool.wait_ge(ix_acc, IDXH * (NT - 1) + 1)
            for t in range(1, NT):
                d = acc[:, TRI[t] - P + t * P:TRI[t] + t * P]
                pool.affine_select(out=d, in_=d, compare_op=ALU.is_ge, fill=FUTURE, base=0,
                                   pattern=[[-1, P]], channel_multiplier=1).then_inc(ix_mask, 1)
            meet(pool, 3)
            pool.memset(f(wq_h[QR - P:P, 1, :]), 0.0)
            pool.memset(f(wq_l[QR - P:P, 1, :]), 0.0)
            pool.drain()

            rem = slice(0, QR - P)
            parts = ((0, slice(0, P)), (1, rem))

            def split_hi():
                for k, r in parts:
                    pool.tensor_copy(wq_h[r, k, 0:256], wc_raw[r, k, :])
                pool.drain()

            def split_lo():
                for k, r in parts:
                    pool.tensor_tensor(wq_l[r, k, 0:256], wc_raw[r, k, :], f(wq_h[r, k, 0:256]), ALU.subtract)
                pool.drain()

            def swap_partners(part):
                for k, r in parts:
                    src = f(part[r, k, P:256]).rearrange("p (i two) -> p i two", two=2)
                    dst = part[r, k, 256:384].rearrange("p (i two) -> p i two", two=2)
                    for o in range(2):
                        pool.tensor_copy(dst[:, :, o:o + 1], src[:, :, 1 - o:2 - o])
                pool.drain()

            def scale_tile(j, i):
                w = (i % NT + 1) * P
                wait_apart(pool, hd_rec, 16 * j + i + 1)
                pool.tensor_scalar(pm[:, i % 4, 0:w], pm[:, i % 4, 0:w], smx[:, 32 + i:33 + i], 0.0,
                                   ALU.mult, ALU.add).then_inc(hd_p, 1)

            def pair(j, last):
                for i in range(16):
                    scale_tile(j, i)
                    if i == 3:
                        pool.wait_ge(hd_ldu, 16 * j + 16)
                        wait_apart(pool, hd_y, NT * j + 1)
                        pool.tensor_copy(wuvo_h[:], wuvo_raw[:])
                        pool.drain()
                    if i == 4:
                        pool.tensor_tensor(wuvo_l[:], wuvo_raw[:], f(wuvo_h[:]), ALU.subtract)
                        pool.drain().then_inc(hd_wu, 1)
                    if i == 6 and not last:
                        pool.wait_ge(hd_ldq, 96 * j + 192)
                        wait_apart(pool, hd_q, 6 * j + 6)
                        split_hi()
                    if i == 7 and not last:
                        split_lo()
                    if i == 8 and not last:
                        swap_partners(wq_h)
                    if i == 9 and not last:
                        swap_partners(wq_l)
                        pool.drain().then_inc(hd_wq, 1)
                for o in range(4):
                    t = 2 * o + 1
                    pool.wait_ge(hd_yc, 4 * j + o + 2)
                    pool.tensor_tensor(xt(t), xt(t), ycp[:, o, :], ALU.add).then_inc(hd_yx, 1)

            pool.wait_ge(hd_ldq, 96)
            split_hi()
            split_lo()
            swap_partners(wq_h)
            swap_partners(wq_l)
            pool.drain().then_inc(hd_wq, 1)
            with pool.Fori(0, PAIRS - 1) as j:
                pair(j, False)
            pair(PAIRS - 1, True)
            meet(pool, 4)

        @block.scalar
        def _(act):
            COPY = ACT.Copy

            def sqrt(k, n):
                act.wait_ge(rs_v, k + 1)
                act.activation(rs_sqrt[:, 0:n], rs_var[:, 0:n], ACT.Sqrt).then_inc(rs_s, 1)

            def norm_hi(l):
                for t in range(NT):
                    act.wait_ge(ln_tr, NT * l + t + 1)
                    act.activation(xn_h[:, :, tile(t)], ps[:, t % 2, :].rearrange("p (k s) -> p k s", k=NK),
                                   COPY).then_inc(ln_hi, 1)

            chunks = list(range(WCHUNKS))

            def weight_chunk():
                chunk = chunks.pop(0)
                m, s, width = wt_chunk(chunk)
                slot = wring[:, chunk % 3, 0:width]
                act.wait_ge(wt_d, chunk + 1)
                act.activation(sgn[m][:, s * width:(s + 1) * width], slot, ACT.Sign)
                act.drain()
                act.activation(slot, slot, ACT.Abs, accum_out=absum[:, chunk:chunk + 1])
                act.drain().then_inc(wt_abs, 1)

            sqrt(0, NT)
            norm_hi(0)
            for u in range(4):
                act.wait_ge(at_proj, u + 1)
                if u >= 2:
                    act.wait_ge(at_qkv, u - 1)
                act.activation(xn_t[:, u % 2, :], ps[:, u, :], ACT.Identity,
                               bias=bq_col[:, u // 2:u // 2 + 1]).then_inc(at_q, 1)
            for kind, i in ATT_ORDER:
                if kind == "S":
                    act.wait_ge(at_max, i + 1)
                    act.activation(p0[:, i % 2, :], two_banks(2 * (i % 2)), ACT.Exp,
                                   bias=sm0[:, NT + i:NT + i + 1], scale=float(D0) ** -0.5,
                                   accum_out=sm0[:, 2 * NT + i:2 * NT + i + 1])
                    act.drain().then_inc(at_exp, 1)
                    weight_chunk()
                elif kind == "T":
                    for c in range(2):
                        act.wait_ge(at_tr, 2 * i + c + 1)
                        act.activation(pTx_h[:, 4 * c:4 * c + 4, tile(i % 4)],
                                       ps[:, 4 + c, :].rearrange("p (k s) -> p k s", k=4), COPY).then_inc(at_hi, 1)
                elif kind == "O":
                    act.wait_ge(at_o, i + 1)
                    act.activation(oT_h[:], ps[:, 6, :], COPY).then_inc(at_ohi, 1)
            while chunks:
                weight_chunk()
            act.drain().then_inc(wt_tot, 1)
            sqrt(1, NT)
            norm_hi(1)
            meet(act, 1)

            def weight_hi(g, par, k):
                act.wait_ge(ff_tr, 3 * g + k + 1)
                act.activation(wc_h[:, par, k, :], ps[:, 6 + (3 * par + k) % 2, :], COPY).then_inc(ff_hi, 1)

            with act.Fori(0, 2) as half:
                for k in range(3):
                    weight_hi(half * NI, 0, k)

                def step(s, par, last=False):
                    g = half * NI + s
                    if not last:
                        weight_hi(g + 1, 1 - par, 0)
                        weight_hi(g + 1, 1 - par, 1)
                    act.wait_ge(ff_gate, g + 1)
                    act.wait_ge(ff_mul, g + 1)
                    act.activation(silu[:], ps[:, 4, :], ACT.Silu).then_inc(ff_silu, 1)
                    act.wait_ge(ff_mul, g + 2)
                    act.activation(hT_h[:, par, :], hf[:], COPY).then_inc(ff_hhi, 1)
                    if not last:
                        weight_hi(g + 1, 1 - par, 2)

                with act.Fori(0, NI - 2, 2) as s:
                    step(s, 0)
                    step(s + 1, 1)
                step(NI - 2, 0)
                step(NI - 1, 1, last=True)
            meet(act, 2)
            sqrt(2, NT)
            norm_hi(2)
            for t in range(NT):
                act.wait_ge(lt_mm, t + 1)
                act.activation(lat[:, t, :], ps[:, 2 + t % 2, 0:LATW], COPY).then_inc(lt_ev, 1)
            sqrt(3, 16)
            for t in range(NT):
                act.wait_ge(lt_tr, t + 1)
                src = ps[:, 4 + t % 2, :]
                act.activation(latT_h[:, 0, tile(t)], src[:, 0:P], COPY)
                act.activation(latT_h[0:QR - P, 1, tile(t)], ps[0:QR - P, 4 + t % 2, P:2 * P], COPY)
                act.activation(latT_h[:, 2:4, tile(t)], src[:, 2 * P:4 * P].rearrange("p (k s) -> p k s", k=2), COPY)
                act.drain().then_inc(lt_hi, 1)
            for b in range(2):
                act.wait_ge(ix_q, b + 1)
                act.activation(ikT_h[:, b * 512:(b + 1) * 512], ps[:, b, :], COPY).then_inc(ix_qhi, 1)
            with act.Fori(0, IDXH) as n:
                for b in range(2):
                    act.wait_ge(ix_q, 2 * n + b + 3)
                    act.activation(iqT_h[:, b * 512:(b + 1) * 512], ps[:, b, :], COPY).then_inc(ix_qhi, 1)
                for t in range(1, NT):
                    w = (t + 1) * P
                    act.wait_ge(ix_s, (NT - 1) * n + t)
                    act.wait_ge(ix_acc, (NT - 1) * n + max(t - 2, 0) + 1)
                    act.activation(relu[:, t % 2, 0:w], two_banks(2 + 2 * (t % 2), w), ACT.Relu).then_inc(ix_r, 1)
            act.wait_ge(lt_lo, NT)
            with act.Fori(0, PAIRS) as j:
                act.wait_ge(pr_t, 2 * j + 2)
                act.activation(kvbT[:].rearrange("p a n -> p (a n)"), ps[:, 0, 0:4 * KR], COPY).then_inc(pr_tev, 1)
                act.wait_ge(pr_t, 2 * j + 3)
                act.activation(qbT[:].rearrange("p a n -> p (a n)"), ps[:, 1, 0:2 * QR], COPY).then_inc(pr_tev, 1)
                act.wait_ge(pr_mm, j + 2)
                act.wait_ge(pr_st, 48 * j + 1)
                act.activation(pr_out[:, 0:P], ps[:, 6, 0:P], COPY, scale=-float(QKD) ** -0.5)
                act.activation(pr_out[0:QR - P, P:256], ps[0:QR - P, 6, P:256], COPY,
                               scale=-float(QKD) ** -0.5)
                act.activation(pr_out[:, 256:768], ps[:, 7, :], COPY)
                act.drain()
                act.dma_start(wabs_d[:, ds(j * P, P)], pr_out[:, 0:P]).then_inc(pr_st, 16)
                act.dma_start(wabs_rem_d[:, ds(j * P, P)], pr_out[0:QR - P, P:256]).then_inc(pr_st, 16)
                act.dma_start(wuvo_d[ds(j * P, P), :], pr_out[:, 256:768]).then_inc(pr_st, 16)
            act.wait_ge(pr_st, 48 * PAIRS + 1)
            meet(act, 3)

            def query_hi_abs(pair, n):
                c = slice(512 * n, 512 * n + 512)
                act.wait_ge(hd_q, 6 * pair + 3 * n + 3)
                act.activation(qc_h[0:KR, 0, c], ps[0:KR, Q_BANKS[n][0], :], COPY)
                act.activation(qc_h[KR:P, 1, c], ps[KR:P, Q_BANKS[n][0], :], COPY).then_inc(hd_qhi, 1)

            def query_hi_rope(pair, n):
                c = slice(512 * n, 512 * n + 512)
                act.wait_ge(hd_rot, 2 * pair + n + 1)
                act.activation(qc_h[KR:P, 0, c], rop[KR:P, 0, :], COPY)
                act.activation(qc_h[0:KR, 1, c], rop[0:KR, 0, :], COPY).then_inc(hd_qhi, 1)

            def pair_work(j, last):
                for kind, i in EVAC_ORDER:
                    if kind == "S":
                        w = (i % NT + 1) * P
                        act.wait_ge(hd_max, 16 * j + i + 1)
                        act.activation(pm[:, i % 4, 0:w], pm[:, i % 4, 0:w], ACT.Exp, bias=smx[:, i:i + 1],
                                       scale=-1.0, accum_out=smx[:, 16 + i:17 + i])
                        act.drain().then_inc(hd_exp, 1)
                    elif kind == "T":
                        t = i % NT
                        dst = pTa_h[:] if t < 4 else pTx_h
                        for c, g in GROUPS[i]:
                            nk = min(4, t + 1 - 4 * c)
                            act.wait_ge(hd_tr, NG * j + g + 1)
                            act.activation(dst[:, 4 * c:4 * c + nk, tile(t % 4)],
                                           ps[:, 4 + g % 2, 0:nk * P].rearrange("p (k s) -> p k s", k=nk),
                                           COPY).then_inc(hd_hi, 1)
                    elif kind == "V":
                        h, b = divmod(i, 2)
                        mine, other = slice(KR * h, KR * h + KR), slice(KR * (1 - h), KR * (1 - h) + KR)
                        act.wait_ge(hd_o, 4 * j + i + 1)
                        act.activation(ol_half[mine, :], ps[other, 6, :], COPY).then_inc(hd_ocp, 1)
                        act.wait_ge(hd_of, 4 * j + i + 2)
                        act.activation(ol_h[mine, 512 * b:512 * b + 512], ol_f[mine, :], COPY).then_inc(hd_ohi, 1)
                    elif kind == "Q":
                        if not last:
                            query_hi_abs(j + 1, i)
                    elif kind == "R":
                        if not last:
                            query_hi_rope(j + 1, i)
                    elif i % 2:
                        act.wait_ge(hd_y, NT * j + i + 2)
                        act.wait_ge(hd_yx, 4 * j + 1)
                        act.activation(ycp[:, i // 2, :], ps[:, 1, :], COPY).then_inc(hd_yc, 1)

            for n in range(2):
                query_hi_abs(0, n)
                query_hi_rope(0, n)
            with act.Fori(0, PAIRS - 1) as j:
                pair_work(j, False)
            pair_work(PAIRS - 1, True)
            meet(act, 4)
            sqrt(4, NT)
            norm_hi(3)
            act.wait_ge(en_tb, 1)
            act.wait_ge(en_c, 1)
            act.activation(lBT[:], ps[:, 0, :], ACT.Identity, scale=lc2_col[:]).then_inc(en_bt, 1)
            for k in range(NK):
                act.wait_ge(en_tw, k + 1)
                act.activation(lWT[:, k, :], ps[:, 1 + k, :], COPY).then_inc(en_wt, 1)

        @block.vector
        def _(dve):
            dve.drain().then_inc(ff_lo, 2)
            dve.drain().then_inc(ff_mul, 1)
            dve.drain().then_inc(ff_x, 1)
            dve.drain().then_inc(ix_acc, 1)
            dve.drain().then_inc(hd_lo, 2)
            dve.drain().then_inc(hd_of, 1)
            dve.drain().then_inc(hd_x, 1)

            def rsqrt(k, n):
                v, r, q = rs_var[:, 0:n], rs_out[:, 0:n], rs_tmp[:, 0:n]
                dve.drain().then_inc(rs_v, 1)
                dve.wait_ge(rs_s, k + 1)
                dve.reciprocal(r, rs_sqrt[:, 0:n])
                dve.drain()
                dve.tensor_tensor(q, r, r, ALU.mult)
                dve.drain()
                dve.tensor_tensor(q, q, v, ALU.mult)
                dve.drain()
                dve.tensor_scalar(q, q, -0.5, 1.5, ALU.mult, ALU.add)
                dve.drain()
                dve.tensor_tensor(r, r, q, ALU.mult)
                dve.drain()

            def split(hi, lo, src):
                dve.tensor_copy(hi, src)
                dve.drain()
                return dve.tensor_tensor(lo, src, f(hi), ALU.subtract)

            def norm(l, k):
                for t in range(NT):
                    if l == 0:
                        dve.wait_ge(ld_x, 16 * NT)
                    dve.bn_stats(stats[:, 6 * t:6 * t + 6], xt(t))
                dve.drain()
                for t in range(NT):
                    dve.bn_aggr(mv[:, t, :], stats[:, 6 * t:6 * t + 6])
                dve.drain()
                dve.tensor_scalar(rs_var[:, 0:NT], mv[:, :, 1], EPS, None, ALU.add)
                rsqrt(k, NT)

                def lo(t):
                    dve.wait_ge(ln_hi, NT * l + t + 1)
                    dve.tensor_tensor(xn_l[:, :, tile(t)], ps[:, t % 2, :].rearrange("p (k s) -> p k s", k=NK),
                                      f(xn_h[:, :, tile(t)]), ALU.subtract).then_inc(ln_lo, 1)

                for t in range(NT):
                    if t >= 2:
                        dve.wait_ge(ln_tr, NT * l + t - 1)
                    dve.tensor_scalar(xn_t[:, t % 2, :], xt(t), mv[:, t, 0:1], rs_out[:, t:t + 1],
                                      ALU.subtract, ALU.mult).then_inc(ln_xn, 1)
                    if t >= 1:
                        lo(t - 1)
                lo(NT - 1)
                dve.drain()

            norm(0, 0)
            dve.wait_ge(ld_a, 80)
            raw = base[2][:, 0:NK * 3 * D0].rearrange("p (k n) -> p k n", k=NK)
            split(wqkv_h[:], wqkv_l[:], raw)
            split(wo_h[:], wo_l[:], base[2][:, 2048:2048 + HID])
            dve.drain().then_inc(at_w, 1)
            for t in range(NT):
                dve.tensor_tensor(xt(t), xt(t), row_bc[:], ALU.add)
            for u in range(4):
                m, n = divmod(u, 2)
                c = slice(512 * n, 512 * n + 512)
                dve.wait_ge(at_q, u + 1)
                split(qkT_h[:, m, c], qkT_l[:, m, c], xn_t[:, u % 2, :])
                dve.drain().then_inc(at_qkv, 1)
            for b in range(2):
                dve.wait_ge(at_proj, 5 + b)
                tmp = xn_t[:, b, :].rearrange("p (k s) -> p k s", k=4)
                for i in range(4):
                    dve.tensor_tensor(tmp[:, i, :], ps[:, 4 + b, tile(i)], bv_bc[:], ALU.add)
                dve.drain()
                split(v_h[:, 4 * b:4 * b + 4, :], v_l[:, 4 * b:4 * b + 4, :], tmp)
                dve.drain().then_inc(at_v, 1)
            for kind, i in ATT_ORDER:
                if kind == "S":
                    dve.wait_ge(at_s, i + 1)
                    dve.tensor_reduce(sm0[:, i:i + 1], two_banks(2 * (i % 2)), AXX, ALU.max)
                    dve.drain()
                    dve.tensor_scalar(sm0[:, NT + i:NT + i + 1], sm0[:, i:i + 1], -float(D0) ** -0.5, None, ALU.mult)\
                        .then_inc(at_max, 1)
                elif kind == "T":
                    for c in range(2):
                        dve.wait_ge(at_hi, 2 * i + c + 1)
                        dst = (slice(None), slice(4 * c, 4 * c + 4), tile(i % 4))
                        dve.tensor_tensor(pTx_l[dst], ps[:, 4 + c, :].rearrange("p (k s) -> p k s", k=4),
                                          f(pTx_h[dst]), ALU.subtract).then_inc(at_lo, 1)
                elif kind == "O":
                    dve.wait_ge(at_ohi, i + 1)
                    dve.tensor_tensor(oT_l[:], ps[:, 6, :], f(oT_h[:]), ALU.subtract).then_inc(at_ot, 1)
                    dve.reciprocal(sm0[:, 3 * NT + 4 * i:3 * NT + 4 * i + 4], sm0[:, 2 * NT + 4 * i:2 * NT + 4 * i + 4])
                    dve.drain()
                else:
                    dve.wait_ge(at_y, i + 1)
                    dve.scalar_tensor_tensor(xt(i), ps[:, 7, :], sm0[:, 3 * NT + i:3 * NT + i + 1], xt(i),
                                             ALU.mult, ALU.add).then_inc(at_x, 1)
            dve.drain()
            norm(1, 1)
            dve.wait_ge(wt_tot, 2)
            for m, (a, b) in enumerate(((0, NI), (NI, 2 * NI), (2 * NI, WCHUNKS))):
                dve.tensor_reduce(coef[:, m:m + 1], ps[:, 7, a:b], AXX, ALU.add)
            dve.drain()
            dve.tensor_scalar(coef[:], coef[:], 1.0 / (INTER * HID), None, ALU.mult)
            meet(dve, 1)

            def effective(s, k):
                dst = weff[:, k, :]
                if k < 2:
                    sg, bs = sgn[k][:, ds(s * 512, 512)], base[k][:, ds(s * 512, 512)]
                else:
                    sg, bs = (a[:].rearrange("p (c n) -> p c n", c=NK)[:, :, ds(s * P, P)]
                              for a in (sgn[2], base[2]))
                    dst = dst.rearrange("p (c n) -> p c n", c=NK)
                dve.scalar_tensor_tensor(dst, sg, coef[:, k:k + 1], bs, ALU.mult, ALU.add).then_inc(ff_we, 1)

            def weight_lo(g, par, k):
                dve.wait_ge(ff_hi, 3 * g + k + 1)
                dve.tensor_tensor(wc_l[:, par, k, :], ps[:, 6 + (3 * par + k) % 2, :], f(wc_h[:, par, k, :]),
                                  ALU.subtract).then_inc(ff_lo, 1)

            with dve.Fori(0, 2) as half:
                for k in range(3):
                    effective(0, k)
                for k in range(3):
                    weight_lo(half * NI, 0, k)
                    effective(1, k)

                def step(s, par, ahead=True, last=False):
                    g = half * NI + s
                    for k in range(0 if last else 2):
                        weight_lo(g + 1, 1 - par, k)
                        if ahead:
                            effective(s + 2, k)
                    dve.wait_ge(ff_silu, g + 1)
                    dve.wait_ge(ff_up, g + 1)
                    dve.tensor_tensor(hf[:], ps[:, 5, :], silu[:], ALU.mult).then_inc(ff_mul, 1)
                    dve.drain()
                    dve.wait_ge(ff_hhi, g + 1)
                    dve.tensor_tensor(hT_l[:, par, :], hf[:], f(hT_h[:, par, :]), ALU.subtract).then_inc(ff_h, 1)
                    dve.drain()
                    if not last:
                        weight_lo(g + 1, 1 - par, 2)
                        if ahead:
                            effective(s + 2, 2)

                with dve.Fori(0, (NI - 2) // 2) as q:
                    step(2 * q, 0)
                    step(2 * q + 1, 1)
                step(NI - 2, 0, ahead=False)
                step(NI - 1, 1, last=True)
                for i in range(4):
                    xs = x[:, ds((half * 4 + i) * HID, HID)]
                    dve.wait_ge(ff_y, 4 * half + i + 1)
                    dve.tensor_tensor(xs, xs, ps[:, i, :], ALU.add).then_inc(ff_x, 1)
                dve.drain()
            meet(dve, 2)
            norm(2, 2)
            dve.memset(f(latT_h[QR - P:P, 1, :]), 0.0)
            dve.memset(f(latT_l[QR - P:P, 1, :]), 0.0)
            dve.memset(acc[:], 0.0)
            dve.wait_ge(ld_l, 16 * 18)
            split(wlat_h[:], wlat_l[:], wlat_raw[:])
            dve.drain().then_inc(lt_w, 1)
            dve.wait_ge(lt_ev, NT)
            for c, (a, w) in enumerate(((0, QR), (QR, KR))):
                sq = lat_sq[:, :, 0:w]
                dve.tensor_tensor(sq, lat[:, :, a:a + w], lat[:, :, a:a + w], ALU.mult)
                dve.drain()
                dve.tensor_reduce(rs_var[:, NT * c:NT * c + NT], sq, AXX, ALU.add)
                dve.drain()
                dve.tensor_scalar(rs_var[:, NT * c:NT * c + NT], rs_var[:, NT * c:NT * c + NT], 1.0 / w, EPS,
                                  ALU.mult, ALU.add)
                dve.drain()
            rsqrt(3, 16)
            for t in range(NT):
                for c, (a, w) in enumerate(((0, QR), (QR, KR))):
                    dve.scalar_tensor_tensor(latn[:, t, a:a + w], lat[:, t, a:a + w],
                                             rs_out[:, NT * c + t:NT * c + t + 1], norm_bc[:, a:a + w],
                                             ALU.mult, ALU.mult)
            kp = lat[:, :, QR + KR:QR + KR + ROPE].rearrange("p t (i two) -> p t i two", two=2)
            ko = latn[:, :, QR + KR:QR + KR + ROPE].rearrange("p t (i two) -> p t i two", two=2)
            for o in range(2):
                own, partner = kp[:, :, :, o], kp[:, :, :, 1 - o]
                dve.tensor_tensor(rope_t[:, 0], own, cosk[:], ALU.mult)
                dve.tensor_tensor(rope_t[:, 1], partner, sink[:], ALU.mult)
                dve.drain()
                dve.tensor_tensor(ko[:, :, :, o], rope_t[:, 0], rope_t[:, 1], ALU.add if o else ALU.subtract)
                dve.drain()
            lv = latn[:, :, QR:QR + KR]
            dve.tensor_copy(latn[:, :, QR + KR + ROPE:384], lv)
            dve.tensor_copy(v3[:, :, 0:KR], lv)
            dve.tensor_copy(v3[:, :, 2 * KR:3 * KR], lv)
            dve.drain()
            dve.tensor_tensor(v3[:, :, KR:2 * KR], lv, f(v3[:, :, 0:KR]), ALU.subtract)
            dve.tensor_scalar(iw[:], lat[:, :, QR + KR + ROPE:LATW], float(IDXH) ** -0.5 * float(IDXD) ** -0.5, None,
                              ALU.mult)
            dve.drain().then_inc(lt_norm, 1)
            for t in range(NT):
                dve.wait_ge(lt_hi, t + 1)
                src = ps[:, 4 + t % 2, :]
                dve.tensor_tensor(latT_l[:, 0, tile(t)], src[:, 0:P], f(latT_h[:, 0, tile(t)]), ALU.subtract)
                dve.tensor_tensor(latT_l[0:QR - P, 1, tile(t)], ps[0:QR - P, 4 + t % 2, P:2 * P],
                                  f(latT_h[0:QR - P, 1, tile(t)]), ALU.subtract)
                dve.tensor_tensor(latT_l[:, 2:4, tile(t)], src[:, 2 * P:4 * P].rearrange("p (k s) -> p k s", k=2),
                                  f(latT_h[:, 2:4, tile(t)]), ALU.subtract)
                dve.drain().then_inc(lt_lo, 1)

            def index_lo(hi, lo, b, count):
                c = slice(512 * b, 512 * b + 512)
                dve.wait_ge(ix_qhi, count)
                dve.tensor_tensor(lo[:, c], ps[:, b, :], f(hi[:, c]), ALU.subtract).then_inc(ix_qlo, 1)

            for b in range(2):
                index_lo(ikT_h, ikT_l, b, b + 1)
            with dve.Fori(0, IDXH) as n:
                for b in range(2):
                    index_lo(iqT_h, iqT_l, b, 2 * n + b + 3)
                dve.drain()
                for t in range(1, NT):
                    w = (t + 1) * P
                    at = acc[:, TRI[t] - P:TRI[t] - P + w]
                    dve.wait_ge(ix_r, (NT - 1) * n + t + 1)
                    dve.scalar_tensor_tensor(at, relu[:, t % 2, 0:w], iw[:, t, ds(n, 1)], at, ALU.mult, ALU.add)\
                        .then_inc(ix_acc, 1)
                dve.drain()
            for t in range(1, NT):
                at = acc[:, TRI[t] - P:TRI[t + 1] - P]
                dve.wait_ge(ix_mask, t + 1)
                with dve.Fori(0, TOPK // 8):
                    dve.max(top8[:], at)
                    dve.drain()
                    dve.match_replace(at, top8[:], at, TAKEN)
                    dve.drain()
                dve.tensor_scalar(mbias[:, TRI[t]:TRI[t + 1]], at, TAKEN, BIG, ALU.not_equal, ALU.mult)
            meet(dve, 3)

            def query_rotate(pair, n):
                c = slice(512 * n, 512 * n + 512)
                b_abs, b_own, b_partner = Q_BANKS[n]
                dve.wait_ge(hd_q, 6 * pair + 3 * n + 1)
                dve.tensor_tensor(rop[:, 0, :], ps[:, b_own, :], cosq[:, c], ALU.mult)
                dve.wait_ge(hd_q, 6 * pair + 3 * n + 2)
                dve.tensor_tensor(rop[:, 1, :], ps[:, b_partner, :], sinq[:, c], ALU.mult)
                dve.drain()
                dve.tensor_tensor(rop[:, 0, :], rop[:, 0, :], rop[:, 1, :], ALU.add)
                dve.drain().then_inc(hd_rot, 1)
                dve.wait_ge(hd_qhi, 4 * pair + 2 * n + 1)
                dve.tensor_tensor(qc_l[0:KR, 0, c], ps[0:KR, b_abs, :], f(qc_h[0:KR, 0, c]), ALU.subtract)
                dve.tensor_tensor(qc_l[KR:P, 1, c], ps[KR:P, b_abs, :], f(qc_h[KR:P, 1, c]), ALU.subtract)

            def query_lo(pair, n):
                c = slice(512 * n, 512 * n + 512)
                dve.wait_ge(hd_qhi, 4 * pair + 2 * n + 2)
                dve.tensor_tensor(qc_l[KR:P, 0, c], rop[KR:P, 0, :], f(qc_h[KR:P, 0, c]), ALU.subtract)
                dve.tensor_tensor(qc_l[0:KR, 1, c], rop[0:KR, 0, :], f(qc_h[0:KR, 1, c]), ALU.subtract)
                dve.drain().then_inc(hd_qlo, 1)

            def pair_work(j, last):
                def rec(i):
                    dve.wait_ge(hd_exp, 16 * j + i + 1)
                    dve.reciprocal(smx[:, 32 + i:33 + i], smx[:, 16 + i:17 + i]).then_inc(hd_rec, 1)

                for kind, i in HEAD_ORDER:
                    if kind == "S":
                        t = i % NT
                        w = (t + 1) * P
                        if i >= 4:
                            dve.wait_ge(hd_tr, NG * j + GROUPS[i - 4][-1][1] + 1)
                        wait_apart(dve, hd_s, 16 * j + i + 1)
                        dve.tensor_tensor_reduce(out=pm[:, i % 4, 0:w], in0=two_banks(2 * (i % 2), w),
                                                 in1=mbias[:, TRI[t]:TRI[t + 1]], scale=1.0, scalar=3.0 * BIG,
                                                 op0=ALU.add, op1=ALU.min, accum_out=smx[:, i:i + 1])
                        dve.drain().then_inc(hd_max, 1)
                        if i >= 1:
                            rec(i - 1)
                        if i == 15:
                            rec(15)
                    elif kind == "T":
                        t = i % NT
                        dh, dl = (pTa_h[:], pTa_l[:]) if t < 4 else (pTx_h, pTx_l)
                        for c, g in GROUPS[i]:
                            nk = min(4, t + 1 - 4 * c)
                            at = (slice(None), slice(4 * c, 4 * c + nk), tile(t % 4))
                            dve.wait_ge(hd_hi, NG * j + g + 1)
                            dve.tensor_tensor(dl[at], ps[:, 4 + g % 2, 0:nk * P].rearrange("p (k s) -> p k s", k=nk),
                                              f(dh[at]), ALU.subtract).then_inc(hd_lo, 1)
                    elif kind == "V":
                        h, b = divmod(i, 2)
                        r, c = slice(KR * h, KR * h + KR), slice(512 * b, 512 * b + 512)
                        dve.wait_ge(hd_ocp, 4 * j + i + 1)
                        dve.tensor_tensor(ol_f[r, :], ps[r, 6, :], ol_half[r, :], ALU.add).then_inc(hd_of, 1)
                        dve.drain()
                        dve.wait_ge(hd_ohi, 4 * j + i + 1)
                        dve.tensor_tensor(ol_l[r, c], ol_f[r, :], f(ol_h[r, c]), ALU.subtract).then_inc(hd_olo, 1)
                        dve.drain()
                    elif kind == "Q":
                        if not last:
                            query_rotate(j + 1, i)
                    elif kind == "R":
                        if not last:
                            query_lo(j + 1, i)
                    else:
                        if i % 2 == 0:
                            dve.wait_ge(hd_y, NT * j + i + 2)
                            dve.tensor_tensor(xt(i), xt(i), ps[:, 7, :], ALU.add).then_inc(hd_x, 1)
                dve.drain()

            for n in range(2):
                query_rotate(0, n)
                query_lo(0, n)
            with dve.Fori(0, PAIRS - 1) as j:
                pair_work(j, False)
            pair_work(PAIRS - 1, True)
            meet(dve, 4)
            norm(3, 4)
            dve.wait_ge(ld_e, 16 * (3 + NK + LORA_N))
            dve.tensor_scalar(lc2_col[:], lc_col[:], LORA_SCALE, None, ALU.mult).then_inc(en_c, 1)
            for t in range(NT):
                dve.tensor_tensor(xt(t), xt(t), row_bc[:], ALU.add)
            for k in range(NK):
                dve.wait_ge(en_wt, k + 1)
                dve.wait_ge(en_mm, k + 1)
                dve.tensor_tensor(wfin_f[:, k, :], ps[:, (5, 6, 7, 0)[k], :], lWT[:, k, :], ALU.add)
                dve.drain()
                split(wfin_h[:, k, :], wfin_l[:, k, :], wfin_f[:, k, :])
                dve.drain().then_inc(en_w, 1)
            for t in range(NT):
                dve.wait_ge(en_y, t + 1)
                dve.tensor_tensor(xt(t), xt(t), ps[:, 1 + t % 2, :], ALU.add).then_inc(en_o, 1)

        @block.tensor
        def _(pe):
            pe.drain().then_inc(ix_r, 1)
            pe.drain().then_inc(pr_t, 1)
            pe.drain().then_inc(pr_mm, 1)
            pe.drain().then_inc(pr_st, 1)
            pe.drain().then_inc(hd_y, 1)
            pe.drain().then_inc(hd_yc, 1)
            pe.drain().then_inc(hd_yx, 1)
            pe.wait_ge(consts, 1)

            def norm_tr(l):
                for t in range(NT):
                    pe.wait_ge(ln_xn, NT * l + t + 1)
                    if t >= 2:
                        pe.wait_ge(ln_lo, NT * l + t - 1)
                    for k in range(NK):
                        last = pe.transpose(ps[:, t % 2, tile(k)], xn_t[:, t % 2, tile(k)], ident[:])
                    last.then_inc(ln_tr, 1)
                pe.wait_ge(ln_lo, NT * l + NT)

            norm_tr(0)
            pe.wait_ge(at_w, 1)
            for u in range(4):
                m, n = divmod(u, 2)
                c = slice(512 * n, 512 * n + 512)
                for k in range(NK):
                    last = mm3(pe, ps[:, u, :], wqkv_h[:, k, tile(m)], wqkv_l[:, k, tile(m)],
                               xn_h[:, k, c], xn_l[:, k, c], k == 0, k == NK - 1)
                last.then_inc(at_proj, 1)
            for t in range(NT):
                for k in range(NK):
                    last = mm3(pe, ps[:, 4 + t // 4, tile(t % 4)], xn_h[:, k, tile(t)], xn_l[:, k, tile(t)],
                               wqkv_h[:, k, tile(2)], wqkv_l[:, k, tile(2)], k == 0, k == NK - 1)
                if t % 4 == 3:
                    last.then_inc(at_proj, 1)
            pe.wait_ge(at_qkv, 4)
            for kind, i in ATT_ORDER:
                if kind == "S":
                    if i >= 2:
                        pe.wait_ge(at_exp, i - 1)
                    for n in range(2):
                        c = slice(512 * n, 512 * n + 512)
                        last = mm3(pe, ps[:, 2 * (i % 2) + n, :], qkT_h[:, 0, tile(i)], qkT_l[:, 0, tile(i)],
                                   qkT_h[:, 1, c], qkT_l[:, 1, c], True, True)
                    last.then_inc(at_s, 1)
                elif kind == "T":
                    pe.wait_ge(at_exp, i + 1)
                    for c in range(2):
                        if i == 0:
                            pe.wait_ge(at_v, c + 1)
                        else:
                            pe.wait_ge(at_lo, 2 * i + c - 1)
                        for k in range(4):
                            last = pe.transpose(ps[:, 4 + c, tile(k)], p0[:, i % 2, tile(4 * c + k)], ident[:])
                        last.then_inc(at_tr, 1)
                elif kind == "O":
                    pe.wait_ge(at_lo, 8 * (i + 1))
                    if i:
                        pe.wait_ge(at_ot, i)
                    for k in range(NT):
                        last = mm3(pe, ps[:, 6, :], v_h[:, k, :], v_l[:, k, :], pTx_h[:, k, :], pTx_l[:, k, :],
                                   k == 0, k == NT - 1)
                    last.then_inc(at_o, 1)
                else:
                    pe.wait_ge(at_ot, i // 4 + 1)
                    if i:
                        pe.wait_ge(at_x, i)
                    mm3(pe, ps[:, 7, :], oT_h[:, tile(i % 4)], oT_l[:, tile(i % 4)], wo_h[:], wo_l[:],
                        True, True).then_inc(at_y, 1)
            norm_tr(1)
            pe.wait_ge(wt_tot, 1)
            pe.matmul(ps[:, 7, 0:WCHUNKS], ones[:], absum[:], start=True, stop=True).then_inc(wt_tot, 1)
            meet(pe, 1)

            with pe.Fori(0, 2) as half:
                tokens = ds(half * 512, 512)

                def transposes(g, par, k):
                    pe.wait_ge(ff_we, 3 * g + k + 1)
                    pe.wait_ge(ff_lo, 3 * g + k + 1)
                    for c in range(NK):
                        last = pe.transpose(ps[:, 6 + (3 * par + k) % 2, tile(c)], weff[:, k, tile(c)], ident[:])
                    last.then_inc(ff_tr, 1)

                def project(g, par, k, done):
                    pe.wait_ge(ff_lo, 3 * g + k + 3)
                    for c in range(NK):
                        last = mm3(pe, ps[:, 4 + k, :], wc_h[:, par, k, tile(c)], wc_l[:, par, k, tile(c)],
                                   xn_h[:, c, tokens], xn_l[:, c, tokens], c == 0, c == NK - 1)
                    last.then_inc(done, 1)

                def down(g, par, first=False, last=False):
                    pe.wait_ge(ff_h, g + 1)
                    pe.wait_ge(ff_lo, 3 * g + 5)
                    for i in range(4):
                        one = mm3(pe, ps[:, i, :], hT_h[:, par, tile(i)], hT_l[:, par, tile(i)],
                                  wc_h[:, par, 2, :], wc_l[:, par, 2, :], first, last)
                        if last:
                            one.then_inc(ff_y, 1)

                def step(s, par, before="run", last=False):
                    g = half * NI + s
                    if not last:
                        transposes(g + 1, 1 - par, 0)
                    pe.wait_ge(ff_mul, g + 1)
                    project(g, par, 0, ff_gate)
                    if not last:
                        transposes(g + 1, 1 - par, 1)
                    project(g, par, 1, ff_up)
                    if before:
                        down(g - 1, 1 - par, first=before == "first")
                    if not last:
                        transposes(g + 1, 1 - par, 2)

                for k in range(3):
                    transposes(half * NI, 0, k)
                step(0, 0, before="")
                pe.wait_ge(ff_x, 4 * half + 1)
                step(1, 1, before="first")
                with pe.Fori(2, NI - 2, 2) as s:
                    step(s, 0)
                    step(s + 1, 1)
                step(NI - 2, 0)
                step(NI - 1, 1, last=True)
                down(half * NI + NI - 1, 1, last=True)
            meet(pe, 2)
            norm_tr(2)
            pe.wait_ge(lt_w, 1)
            for t in range(NT):
                if t >= 2:
                    pe.wait_ge(lt_ev, t - 1)
                for k in range(NK):
                    last = mm3(pe, ps[:, 2 + t % 2, 0:LATW], xn_h[:, k, tile(t)], xn_l[:, k, tile(t)],
                               wlat_h[:, k, :], wlat_l[:, k, :], k == 0, k == NK - 1)
                last.then_inc(lt_mm, 1)

            def index_project(ready):
                pe.wait_ge(ix_w, ready)
                for b in range(2):
                    c = slice(512 * b, 512 * b + 512)
                    for k in range(NK):
                        last = mm3(pe, ps[:, b, :], iwq_h[:, k, :], iwq_l[:, k, :], xn_h[:, k, c], xn_l[:, k, c],
                                   k == 0, k == NK - 1)
                    last.then_inc(ix_q, 1)

            index_project(1)
            pe.wait_ge(lt_norm, 1)
            for t in range(NT):
                if t >= 2:
                    pe.wait_ge(lt_lo, t - 1)
                b = 4 + t % 2
                pe.transpose(ps[:, b, 0:P], latn[:, t, 0:P], ident[:])
                pe.transpose(ps[0:QR - P, b, P:2 * P], latn[:, t, P:QR], ident[:])
                pe.transpose(ps[:, b, 2 * P:3 * P], latn[:, t, QR:QR + P], ident[:])
                pe.transpose(ps[:, b, 3 * P:4 * P], latn[:, t, QR + KR:QR + KR + P], ident[:]).then_inc(lt_tr, 1)
            pe.wait_ge(lt_lo, NT)
            with pe.Fori(0, IDXH) as n:
                pe.wait_ge(ix_qlo, 2 * n + 2)
                index_project(n + 2)
                for t in range(1, NT):
                    w = (t + 1) * P
                    pe.wait_ge(ix_qlo, 2 * n + (3 if t < 4 else 4))
                    pe.wait_ge(ix_r, (NT - 1) * n + max(t - 2, 0) + 1)
                    for b in range(1 if t < 4 else 2):
                        c = slice(512 * b, min(w, 512 * b + 512))
                        last = mm3(pe, ps[:, 2 + 2 * (t % 2) + b, 0:c.stop - c.start], iqT_h[:, tile(t)],
                                   iqT_l[:, tile(t)], ikT_h[:, c], ikT_l[:, c], True, True)
                    last.then_inc(ix_s, 1)
            with pe.Fori(0, PAIRS) as j:
                wait_apart(pe, pr_ldq, 48 * j + 48)
                for a in range(4):
                    last = pe.transpose(ps[:, 0, a * KR:(a + 1) * KR], kvb_raw[:, tile(a)], ident[0:KR, 0:KR])
                last.then_inc(pr_t, 1)
                for h in range(2):
                    pe.transpose(ps[:, 1, h * QR:h * QR + P], qb_raw[:, 0, h * QKD:h * QKD + NOPE], ident[:])
                    last = pe.transpose(ps[:, 1, h * QR + P:(h + 1) * QR],
                                        qb_raw[0:QR - P, 1, h * QKD:h * QKD + NOPE], ident[0:QR - P, 0:QR - P])
                last.then_inc(pr_t, 1)
                pe.wait_ge(pr_tev, 2 * j + 2)
                for h in range(2):
                    c = slice(h * KR, (h + 1) * KR)
                    pe.matmul(ps[:, 6, c], qbT[:, h, 0:P], kvbT[:, 2 * h, :], start=True, stop=True)
                    pe.matmul(ps[0:QR - P, 6, P + h * KR:P + (h + 1) * KR], qbT[:, h, P:QR], kvbT[:, 2 * h, :],
                              start=True, stop=True)
                pe.wait_ge(pr_ldo, 16 * j + 16)
                for h in range(2):
                    last = pe.matmul(ps[h * KR:(h + 1) * KR, 7, :], kvbT[:, 2 * h + 1, :], ow_raw[:, h, :],
                                     start=True, stop=True)
                last.then_inc(pr_mm, 1)
            meet(pe, 3)

            def query_project(pair, n):
                c = slice(512 * n, 512 * n + 512)
                for w, bank in zip((1, 2, 0), Q_BANKS[n][1:] + Q_BANKS[n][:1]):
                    for k in range(2):
                        last = mm3(pe, ps[:, bank, :], wq_h[:, k, tile(w)], wq_l[:, k, tile(w)],
                                   latT_h[:, k, c], latT_l[:, k, c], k == 0, k == 1)
                    last.then_inc(hd_q, 1)

            def pair_work(j, last_pair):
                for kind, i in HEAD_ORDER:
                    if kind == "S":
                        h, t = divmod(i, NT)
                        w = (t + 1) * P
                        if i < 2:
                            pe.wait_ge(hd_qlo, 2 * j + i + 1)
                        if i == 4:
                            pe.wait_ge(hd_yc, 4 * j + 1)
                        if i >= 2:
                            pe.wait_ge(hd_max, 16 * j + i - 1)
                        for b in range(1 if t < 4 else 2):
                            c = slice(512 * b, min(w, 512 * b + 512))
                            last = mm3(pe, ps[:, 2 * (i % 2) + b, 0:c.stop - c.start], qc_h[:, h, tile(t)],
                                       qc_l[:, h, tile(t)], latT_h[:, 2 + h, c], latT_l[:, 2 + h, c], True, True)
                        last.then_inc(hd_s, 1)
                    elif kind == "T":
                        t = i % NT
                        pe.wait_ge(hd_p, 16 * j + i + 1)
                        for c, g in GROUPS[i]:
                            pe.wait_ge(hd_lo, NG * j + g + 1)
                            for k in range(min(4, t + 1 - 4 * c)):
                                last = pe.transpose(ps[:, 4 + g % 2, tile(k)], pm[:, i % 4, tile(4 * c + k)], ident[:])
                            last.then_inc(hd_tr, 1)
                    elif kind == "V":
                        h, b = divmod(i, 2)
                        end = GROUPS[4 * i + 3][-1][1]
                        ph, pl = (pTa_h, pTa_l) if b == 0 else (pTx_h, pTx_l)
                        pe.wait_ge(hd_lo, NG * j + end + 3)
                        pe.wait_ge(hd_of, 4 * j + i + 1)
                        nk = 4 * b + 4
                        for k in range(nk):
                            q = slice(max(0, k - 4 * b) * P, 512)
                            v = v3[:, k, h * KR:h * KR + P]
                            pe.matmul(ps[:, 6, q], v, pl[:, k, q], start=k == 0, stop=False)
                            last = pe.matmul(ps[:, 6, q], v, ph[:, k, q], start=False, stop=k == nk - 1)
                        last.then_inc(hd_o, 1)
                    elif kind == "Q":
                        if last_pair:
                            continue
                        if i == 0:
                            pe.wait_ge(hd_wq, j + 2)
                            pe.wait_ge(hd_max, 16 * j + 16)
                        else:
                            pe.wait_ge(hd_qlo, 2 * j + 3)
                        query_project(j + 1, i)
                    elif kind == "Y":
                        pe.wait_ge(hd_olo, 4 * j + (3 if i < 4 else 4))
                        pe.wait_ge(hd_wu, j + 1)
                        if i % 2 == 0:
                            pe.wait_ge(hd_x, 4 * j + i // 2 + 1)
                        else:
                            pe.wait_ge(hd_yc, 4 * j + i // 2 + 1)
                        if i == 1 and not last_pair:
                            pe.wait_ge(hd_rot, 2 * j + 3)
                        mm3(pe, ps[:, 1 if i % 2 else 7, :], ol_h[:, tile(i)], ol_l[:, tile(i)], wuvo_h[:], wuvo_l[:],
                            True, True).then_inc(hd_y, 1)

            pe.wait_ge(hd_wq, 1)
            query_project(0, 0)
            pe.wait_ge(hd_qlo, 1)
            query_project(0, 1)
            with pe.Fori(0, PAIRS - 1) as j:
                pair_work(j, False)
            pair_work(PAIRS - 1, True)
            meet(pe, 4)
            norm_tr(3)
            pe.wait_ge(ld_e, 16 * (3 + NK + LORA_N))
            for k in range(NK):
                last = pe.transpose(ps[:, 0, tile(k)], lB_sb[:, k, :], ident[:])
            last.then_inc(en_tb, 1)
            for k in range(NK):
                for c in range(NK):
                    last = pe.transpose(ps[:, 1 + k, tile(c)], lW_sb[:, c, tile(k)], ident[:])
                last.then_inc(en_tw, 1)
            pe.wait_ge(en_bt, 1)
            for k in range(NK):
                pe.matmul(ps[:, (5, 6, 7, 0)[k], :], lA_sb[:, tile(k)], lBT[:], start=True, stop=True).then_inc(en_mm, 1)
            pe.wait_ge(en_w, NK)
            for t in range(NT):
                if t >= 2:
                    pe.wait_ge(en_o, t - 1)
                for k in range(NK):
                    last = mm3(pe, ps[:, 1 + t % 2, :], xn_h[:, k, tile(t)], xn_l[:, k, tile(t)],
                               wfin_h[:, k, :], wfin_l[:, k, :], k == 0, k == NK - 1)
                last.then_inc(en_y, 1)


_INS = ['L0_attn_x', 'L0_attn_Wqkv', 'L0_attn_bqkv', 'L0_attn_Wo', 'L0_attn_bo', 'L0_ffn_w1', 'L0_ffn_mean_w1',
        'L0_ffn_w2', 'L0_ffn_mean_w2', 'L0_ffn_w3', 'L0_ffn_mean_w3', 'L1_attn_q_a_w', 'L1_attn_q_a_norm_w',
        'L1_attn_q_b_w', 'L1_attn_kv_a_w', 'L1_attn_kv_a_norm_w', 'L1_attn_kv_b_w', 'L1_attn_o_w',
        'L1_attn_idx_wq_w', 'L1_attn_idx_wk_w', 'L1_attn_idx_weights_w', 'L1_ffn_lora_A', 'L1_ffn_lora_B',
        'L1_ffn_W', 'L1_ffn_bias', 'L1_ffn_lora_weights']


def rope_tables():
    inv = (np.float32(1.0) / np.float32(10000.0) ** (np.arange(0, ROPE, 2, dtype=np.float32) / np.float32(ROPE)))
    ang = np.arange(S, dtype=np.float32)[:, None] * inv.astype(np.float32)[None, :]
    cos, sin = np.cos(ang).astype(np.float32), np.sin(ang).astype(np.float32)
    sign = np.where(np.arange(ROPE) % 2 == 0, -1.0, 1.0).astype(np.float32)
    scale = np.float32(-float(QKD) ** -0.5)
    cos_q = np.tile(np.repeat(cos, 2, axis=1).T, (2, 1)) * scale
    sin_q = np.tile((np.repeat(sin, 2, axis=1) * sign).T, (2, 1)) * scale
    cos_k, sin_k = (np.ascontiguousarray(a.reshape(NT, P, ROPE // 2).transpose(1, 0, 2)) for a in (cos, sin))
    return {"cos_q": np.ascontiguousarray(cos_q), "sin_q": np.ascontiguousarray(sin_q), "cos_k": cos_k, "sin_k": sin_k}


def kernel(**inputs):
    import concourse.bacc as _bacc
    from concourse.bass_utils import run_bass_kernel_spmd as _run

    nc = _bacc.Bacc("TRN2", target_bir_lowering=False, num_devices=1)
    arrays, args = {}, []
    for name, a in [(n, inputs[n]) for n in _INS] + list(rope_tables().items()):
        a = np.ascontiguousarray(a)
        arrays[f"in_{name}"] = a
        args.append(nc.dram_tensor(f"in_{name}", a.shape, F32, kind="ExternalInput").ap())
    args.append(nc.dram_tensor("out", (1, S, HID), F32, kind="ExternalOutput").ap())
    for name, shape in (("wabs", (P, PAIRS * P)), ("wabs_rem", (QR - P, PAIRS * P)), ("wuvo", (PAIRS * P, HID))):
        args.append(nc.dram_tensor(name, shape, F32).ap())
    build(nc, *args)
    return _run(nc, [arrays], core_ids=[0]).results[0]["out"]
```

```python
from contextlib import ExitStack

import numpy as np

import concourse.bass as bass
from concourse import mybir

F32 = mybir.dt.float32
F32R = mybir.dt.float32r
BF16 = mybir.dt.bfloat16
I8 = mybir.dt.int8
ALU = mybir.AluOpType
ACT = mybir.ActivationFunctionType
AXX = mybir.AxisListType.X

P = 128
S = 1024
HID = 512
NT = S // P
NK = HID // P
D0 = 128
INTER = 1792
NI = INTER // P
HEADS, NOPE, ROPE, VD = 32, 128, 64, 128
QKD = NOPE + ROPE
QR, KR = 192, 64
IDXH, IDXD, TOPK = 16, 128, 128
PAIRS = HEADS // 2
LATW = QR + KR + ROPE + IDXH
LORA_N, LORA_R, LORA_SCALE = 8, 16, 2.0
EPS = 1e-5
BIG = 1.0e30
FUTURE = -3.0e38
TAKEN = -3.3e38
WCHUNKS = 2 * NI + 16
TRI = [P * (t * (t + 1) // 2) for t in range(NT + 1)]


def ds(start, size):
    return bass.ds(start, size)


ATT_ORDER = [("S", 0), ("S", 1), ("T", 0), ("S", 2), ("T", 1), ("S", 3), ("T", 2), ("S", 4), ("T", 3), ("S", 5),
             ("O", 0), ("T", 4), ("Y", 0), ("Y", 1), ("Y", 2), ("Y", 3), ("S", 6), ("T", 5), ("S", 7), ("T", 6),
             ("T", 7), ("O", 1), ("Y", 4), ("Y", 5), ("Y", 6), ("Y", 7)]

PE_ORDER = """T0 Q0 S4 T1 S5 T2 S6 Q1 T3 S7 T4 Q2 T5 S8 T6 S9 V0 T7 S10 S11 Q3 T8 T9 S12 S13 V1 T10 S14 T11 T12
    S15 V2 S16 T13 T14 S17 Y0 T15 Y1 Y2 S18 V3 Q4 Y3 Q5 S19 Y4 Y5 Y6 Y7"""
DVE_ORDER = """T0 S4 C3 S5 T1 Q0 C4 S6 T2 C5 Q1 T3 C6 T4 S7 T5 S8 Q2 C7 T6 S9 C8 V0 T7 C9 S10 S11 Q3 S12 C10 S13
    C11 T8 C12 W0 T9 V1 T10 S14 C13 T11 T12 S15 C14 W1 V2 T13 W2 C15 S16 T14 Y0 T15 S17 Y1 C16 Y2 S18 V3 Q4 Y3
    C17 W3 S19 Y4 Y5 Y6 Q5 Y7 C18"""
ACT_ORDER = """T0 T1 S4 T2 S5 T3 S6 T4 T5 Q2 S7 T6 S8 V0 T7 S9 R0 W0 T8 S10 S11 S12 T9 V1 T10 S13 W1 T11 T12 S14
    V2 T13 W2 S15 T14 S16 T15 S17 V3 W3 S18 Q5 R1 S19"""
POOL_ORDER = """S4 S5 S6 G0 S7 S8 S9 S10 S11 S12 R0 S13 S14 S15 G1 S16 R1 S17 S18 S19"""

def steps(order, pair, last):
    for step in order.split():
        kind, i = step[0], int(step[1:])
        ahead = kind in "QGR" or i >= 16
        if not (ahead and last):
            yield kind, i % 16, pair + 1 if ahead else pair


Q_BANKS = (7, 6, 7, 7, 4, 6)
Y_BANKS = (7, 1, 3, 5, 7, 1, 3, 5)

GROUPS = []
for _i in range(16):
    GROUPS.append([])
    for _c in range(1 if _i % NT < 4 else 2):
        GROUPS[_i].append((_c, sum(map(len, GROUPS))))
NG = sum(map(len, GROUPS))


def build(nc, x_in, wqkv, bqkv, wo, bo, w1, m1, w2, m2, w3, m3, qa, qan, qb, kva, kvan, kvb, ow,
          iwq, iwk, iww, lA, lB, lW, lbias, lcoef, cos_q, sin_q, cos_k, sin_k, out,
          wq_d, wuvo_d):
    ctx = ExitStack()
    with ctx:
        def sem(name):
            return ctx.enter_context(nc.semaphore(name))

        def sbin(scope, name, shape, dt=F32):
            return scope.enter_context(nc.sbuf_tensor(name, shape, dt))

        def sb(name, shape, dt=F32):
            return sbin(ctx, name, shape, dt)

        x = sb("x", [P, NT * HID])
        xn_h = sb("xn_h", [P, NK, S], F32R)
        xn_l = sb("xn_l", [P, NK, S], F32R)
        ident = sb("ident", [P, P])
        ones = sb("ones", [P, P])
        stats = sb("stats", [P, NT * 6])
        mv = sb("mv", [P, NT, 2])
        rs_var = sb("rs_var", [P, 16])
        rs_sqrt = sb("rs_sqrt", [P, 16])
        rs_out = sb("rs_out", [P, 16])
        rs_tmp = sb("rs_tmp", [P, 16])
        row_bc = sb("row_bc", [P, HID])
        xn_t = sb("xn_t", [P, 2, HID])
        ps = ctx.enter_context(nc.psum_tensor("ps", [P, 8, 512], F32))

        pTx_h = xn_h[:].rearrange("p k s -> p (k s)").rearrange("p (b q) -> p b q", q=512)
        pTx_l = xn_l[:].rearrange("p k s -> p (k s)").rearrange("p (b q) -> p b q", q=512)

        w_scope = ExitStack()
        base = [sbin(w_scope, f"base{m}", [P, NI * 512]) for m in range(3)]
        sgn = [sbin(w_scope, f"sgn{m}", [P, NI * 512], I8) for m in range(3)]
        absum = sbin(w_scope, "absum", [P, WCHUNKS])
        coef = sbin(w_scope, "coef", [P, 3])
        a_scope = ExitStack()
        qkT_h = sbin(a_scope, "qkT_h", [P, 2, S], F32R)
        qkT_l = sbin(a_scope, "qkT_l", [P, 2, S], F32R)
        v_h = sbin(a_scope, "v_h", [P, NT, D0], F32R)
        v_l = sbin(a_scope, "v_l", [P, NT, D0], F32R)
        bq_col = sbin(a_scope, "bq_col", [P, 2])
        bv_bc = sbin(a_scope, "bv_bc", [P, D0])
        wo_h = sbin(a_scope, "wo_h", [P, HID], F32R)
        wo_l = sbin(a_scope, "wo_l", [P, HID], F32R)
        sm0 = sbin(a_scope, "sm0", [P, 4 * NT])
        wring = sbin(a_scope, "wring", [P, 3, 512])
        q_scope = ExitStack()
        wqkv_h = sbin(q_scope, "wqkv_h", [P, NK, 3 * D0], F32R)
        wqkv_l = sbin(q_scope, "wqkv_l", [P, NK, 3 * D0], F32R)
        q_scope.close()
        p0 = sbin(a_scope, "p0", [P, 2, S])
        oT_h = sbin(a_scope, "oT_h", [P, 512], F32R)
        oT_l = sbin(a_scope, "oT_l", [P, 512], F32R)
        a_scope.close()
        f_scope = ExitStack()
        weff = sbin(f_scope, "weff", [P, 3, 512])
        wc_h = sbin(f_scope, "wc_h", [P, 2, 3, 512], F32R)
        wc_l = sbin(f_scope, "wc_l", [P, 2, 3, 512], F32R)
        silu = sbin(f_scope, "silu", [P, 512])
        hf = sbin(f_scope, "hf", [P, 512])
        hT_h = sbin(f_scope, "hT_h", [P, 2, 512], F32R)
        hT_l = sbin(f_scope, "hT_l", [P, 2, 512], F32R)
        f_scope.close()
        w_scope.close()

        l_scope = ExitStack()
        latT_h = sbin(l_scope, "latT_h", [P, 4, S], F32R)
        latT_l = sbin(l_scope, "latT_l", [P, 4, S], F32R)
        v3 = sbin(l_scope, "v3", [P, NT, 3 * KR], F32R)
        mbias = sbin(l_scope, "mbias", [P, TRI[NT]], BF16)
        cosq = sbin(l_scope, "cosq", [P, S])
        sinq = sbin(l_scope, "sinq", [P, S])
        i_scope = ExitStack()
        iw = sbin(i_scope, "iw", [P, NT, IDXH])
        ikT_h = sbin(i_scope, "ikT_h", [P, S], F32R)
        ikT_l = sbin(i_scope, "ikT_l", [P, S], F32R)
        iqT_h = sbin(i_scope, "iqT_h", [P, S], F32R)
        iqT_l = sbin(i_scope, "iqT_l", [P, S], F32R)
        iwq_raw = sbin(i_scope, "iwq_raw", [P, NK, IDXD])
        iwq_h = sbin(i_scope, "iwq_h", [P, NK, IDXD], F32R)
        iwq_l = sbin(i_scope, "iwq_l", [P, NK, IDXD], F32R)
        relu = sbin(i_scope, "relu", [P, 2, S])
        acc = sbin(i_scope, "acc", [P, TRI[NT] - P])
        top8 = sbin(i_scope, "top8", [P, 8])
        t_scope = ExitStack()
        lat = sbin(t_scope, "lat", [P, NT, LATW])
        latn = sbin(t_scope, "latn", [P, NT, 384])
        lat_sq = sbin(t_scope, "lat_sq", [P, NT, QR])
        norm_bc = sbin(t_scope, "norm_bc", [P, QR + KR])
        cosk = sbin(t_scope, "cosk", [P, NT, ROPE // 2])
        sink = sbin(t_scope, "sink", [P, NT, ROPE // 2])
        rope_t = sbin(t_scope, "rope_t", [P, 2, NT, ROPE // 2])
        wlat_h = sbin(t_scope, "wlat_h", [P, NK, LATW], F32R)
        wlat_l = sbin(t_scope, "wlat_l", [P, NK, LATW], F32R)
        wlat_raw = sbin(t_scope, "wlat_raw", [P, NK, LATW])
        t_scope.close()
        r_scope = ExitStack()
        qb_raw = sbin(r_scope, "qb_raw", [P, 2, 2 * QKD])
        kvb_raw = sbin(r_scope, "kvb_raw", [KR, 512])
        ow_raw = sbin(r_scope, "ow_raw", [P, 2, HID])
        qbT = sbin(r_scope, "qbT", [P, 2, QR])
        kvbT = sbin(r_scope, "kvbT", [P, 4, KR])
        pr_out = sbin(r_scope, "pr_out", [P, 256 + 512])
        pq = [sbin(r_scope, f"pq{m}", [P, 2, 384], F32R) for m in range(2)]
        pu = [sbin(r_scope, f"pu{m}", [P, HID], F32R) for m in range(2)]
        r_scope.close()
        i_scope.close()
        h_scope = ExitStack()
        wq_h = sbin(h_scope, "wq_h", [P, 2, 384], F32R)
        wq_l = sbin(h_scope, "wq_l", [P, 2, 384], F32R)
        wuvo_h = sbin(h_scope, "wuvo_h", [P, HID], F32R)
        wuvo_l = sbin(h_scope, "wuvo_l", [P, HID], F32R)
        rop = sbin(h_scope, "rop", [P, 2, 2, 512])
        qc_h = [sbin(h_scope, f"qc_h{m}", [P, 2, S], F32R) for m in range(2)]
        qc_l = [sbin(h_scope, f"qc_l{m}", [P, 2, S], F32R) for m in range(2)]
        pm = sbin(h_scope, "pm", [P, 4, S])
        smx = sbin(h_scope, "smx", [P, 48])
        pTa_h = sbin(h_scope, "pTa_h", [P, 4, 512], F32R)
        pTa_l = sbin(h_scope, "pTa_l", [P, 4, 512], F32R)
        ol_half = sbin(h_scope, "ol_half", [P, 512])
        ol_f = sbin(h_scope, "ol_f", [P, 512])
        ol_h = sbin(h_scope, "ol_h", [P, S], F32R)
        ol_l = sbin(h_scope, "ol_l", [P, S], F32R)
        h_scope.close()
        l_scope.close()

        e_scope = ExitStack()
        lA_sb = sbin(e_scope, "lA_sb", [P, HID])
        lB_sb = sbin(e_scope, "lB_sb", [P, NK, P])
        lBT = sbin(e_scope, "lBT", [P, HID])
        lc_col = sbin(e_scope, "lc_col", [P, 1])
        lc2_col = sbin(e_scope, "lc2_col", [P, 1])
        lW_sb = sbin(e_scope, "lW_sb", [P, NK, HID])
        lWT = sbin(e_scope, "lWT", [P, NK, HID])
        wfin_f = sbin(e_scope, "wfin_f", [P, NK, HID])
        wfin_h = sbin(e_scope, "wfin_h", [P, NK, HID], F32R)
        wfin_l = sbin(e_scope, "wfin_l", [P, NK, HID], F32R)
        e_scope.close()

        def sems(prefix, names):
            return [sem(prefix + n) for n in names.split()]

        ld_x, ld_a, ld_l, ld_e = sems("ld_", "x a l e")
        ld_w = sems("ld_w", "0 1 2")
        consts, phase, st_out, passed = sem("consts"), sem("phase"), sem("st_out"), sem("passed")
        ln_xn, ln_tr, ln_hi, ln_lo = sems("ln_", "xn tr hi lo")
        rs_v, rs_s = sems("rs_", "v s")
        at_w, at_proj, at_q, at_qkv, at_v = sems("at_", "w proj q qkv v")
        at_s, at_max, at_exp, at_tr, at_hi, at_lo = sems("at_", "s max exp tr hi lo")
        at_o, at_ohi, at_ot, at_y, at_x = sems("at_", "o ohi ot y x")
        wt_d, wt_abs, wt_tot, wt_coef = sems("wt_", "d abs tot coef")
        ff_we, ff_tr, ff_hi, ff_lo = sems("ff_", "we tr hi lo")
        ff_gate, ff_up, ff_silu, ff_mul, ff_hhi, ff_h, ff_y, ff_x = sems("ff_", "gate up silu mul hhi h y x")
        lt_w, lt_mm, lt_ev, lt_norm, lt_tr, lt_hi, lt_lo = sems("lt_", "w mm ev norm tr hi lo")
        ix_ld, ix_w, ix_q, ix_qhi, ix_qlo, ix_s, ix_r, ix_acc, ix_mask = sems("ix_", "ld w q qhi qlo s r acc mask")
        pr_ldq, pr_ldo, pr_t, pr_tev, pr_mm, pr_ev, pr_raw, pr_sp, pr_st = sems("pr_", "ldq ldo t tev mm ev raw sp st")
        hd_ldq, hd_ldu, hd_q, hd_rm, hd_rot = sems("hd_", "ldq ldu q rm rot")
        hd_qhi, hd_qlo, hd_qalo = sems("hd_", "qhi qlo qalo")
        hd_s, hd_max, hd_exp, hd_rec, hd_p, hd_tr, hd_hi, hd_lo = sems("hd_", "s max exp rec p tr hi lo")
        hd_o, hd_ocp, hd_of, hd_ohi, hd_olo = sems("hd_", "o ocp of ohi olo")
        hd_y, hd_x, hd_wz = sems("hd_", "y x wz")
        en_tb, en_tw, en_bt, en_wt, en_c, en_mm, en_w, en_y, en_o = sems("en_", "tb tw bt wt c mm w y o")

        block = ctx.enter_context(nc.Block())

        def meet(e, n):
            e.drain().then_inc(phase, 1)
            e.wait_ge(phase, 5 * n)

        def wait_apart(e, s, value):
            e.wait_ge(s, value)
            e.sem_inc(passed, 1)

        def f(ap):
            return ap.bitcast(F32)

        def mm3(pe, dst, lh, ll, rh, rl, start, stop):
            pe.matmul(dst, lh, rl, start=start, stop=False)
            pe.matmul(dst, ll, rh, start=False, stop=False)
            return pe.matmul(dst, lh, rh, start=False, stop=stop)

        def tile(t):
            return slice(t * P, (t + 1) * P)

        def xt(t):
            return x[:, t * HID:(t + 1) * HID]

        def two_banks(b, w=1024):
            return ps[:, b:b + 2, :].rearrange("p a n -> p (a n)")[:, 0:w]

        def wt_chunk(chunk):
            m = min(chunk // NI, 2)
            return m, chunk - NI * m, 512 if m < 2 else 448

        def row(v, n, parts=P):
            return v.rearrange("(a n) -> a n", a=1).broadcast_to([parts, n])

        @block.sync
        def _(sp):
            for t in range(NT):
                sp.dma_start(xt(t), x_in[0, tile(t), :]).then_inc(ld_x, 16)
            sp.dma_start(base[2][:, 0:NK * 3 * D0].rearrange("p (k n) -> p k n", k=NK),
                         wqkv.rearrange("(k p) n -> p k n", p=P)).then_inc(ld_a, 16)
            sp.dma_start(base[2][:, 2048:2048 + HID], wo).then_inc(ld_a, 16)
            with nc.allow_non_contiguous_dma(reason="a small bias column"):
                sp.dma_start(bq_col[:], bqkv[0:2 * D0].rearrange("(a p) -> p a", p=P)).then_inc(ld_a, 16)
            sp.dma_start(bv_bc[:], row(bqkv[2 * D0:3 * D0], D0)).then_inc(ld_a, 16)
            sp.dma_start(row_bc[:], row(bo, HID)).then_inc(ld_a, 16)
            pairs = ((w1, m1), (w3, m3), (w2, m2))
            for chunk in range(WCHUNKS):
                m, s, width = wt_chunk(chunk)
                rows, mrows = (a.rearrange("(c p) n -> p c n", p=P) for a in pairs[m])
                dst = base[m][:, s * width:(s + 1) * width]
                slot = wring[:, chunk % 3, 0:width]
                if m < 2:
                    ws, ms = rows[:, s, :], mrows[:, s, :]
                else:
                    c = slice((s % 4) * 448, (s % 4) * 448 + 448)
                    ws, ms = rows[:, s // 4, c], mrows[:, s // 4, c]
                if chunk == 2 * NI:
                    sp.wait_ge(at_w, 1)
                if chunk >= 3:
                    sp.wait_ge(wt_abs, chunk - 2)
                sp.dma_start(dst, ms).then_inc(ld_w[chunk % 3], 16)
                sp.dma_start(slot, ws).then_inc(ld_w[chunk % 3], 16)
            meet(sp, 1)
            meet(sp, 2)
            for k in range(NK):
                sp.dma_start(wlat_raw[:, k, 0:QR], qa[tile(k), :]).then_inc(ld_l, 16)
                sp.dma_start(wlat_raw[:, k, QR:QR + KR + ROPE], kva[tile(k), :]).then_inc(ld_l, 16)
                sp.dma_start(wlat_raw[:, k, QR + KR + ROPE:LATW], iww[tile(k), :]).then_inc(ld_l, 16)
            sp.dma_start(norm_bc[:, 0:QR], row(qan, QR)).then_inc(ld_l, 16)
            sp.dma_start(norm_bc[:, QR:QR + KR], row(kvan, KR)).then_inc(ld_l, 16)
            sp.dma_start(cosk[:], cos_k).then_inc(ld_l, 16)
            sp.dma_start(sink[:], sin_k).then_inc(ld_l, 16)
            sp.dma_start(cosq[:], cos_q).then_inc(ld_l, 16)
            sp.dma_start(sinq[:], sin_q).then_inc(ld_l, 16)
            sp.dma_start(iwq_raw[:], iwk.rearrange("(k p) n -> p k n", p=P)).then_inc(ix_ld, 16)
            with sp.Fori(0, IDXH) as n:
                sp.wait_ge(ix_w, n + 1)
                sp.dma_start(iwq_raw[:], iwq.rearrange("(k p) n -> p k n", p=P)[:, :, ds(n * IDXD, IDXD)])\
                    .then_inc(ix_ld, 16)
            sp.wait_ge(lt_lo, NT)
            with sp.Fori(0, PAIRS) as j:
                wait_apart(sp, pr_t, 2 * j + 1)
                wait_apart(sp, pr_raw, j + 1)
                sp.dma_start(qb_raw[:, 0, :], qb[0:P, ds(j * 2 * QKD, 2 * QKD)]).then_inc(pr_ldq, 16)
                sp.dma_start(qb_raw[0:QR - P, 1, :], qb[P:QR, ds(j * 2 * QKD, 2 * QKD)]).then_inc(pr_ldq, 16)
                sp.dma_start(kvb_raw[:], kvb[:, ds(j * 512, 512)]).then_inc(pr_ldq, 16)
                sp.wait_ge(pr_mm, j + 1)
                sp.dma_start(ow_raw[:], ow[ds(j * 256, 256), :].rearrange("(a p) n -> p a n", p=P)).then_inc(pr_ldo, 16)
            meet(sp, 3)

            def load_wq(pair):
                for m, dst in enumerate((wq_h, wq_l)):
                    sp.dma_start(f(dst[:, 0, :]), wq_d[m, 0:P, ds(pair * 384, 384)]).then_inc(hd_ldq, 16)
                    sp.dma_start(f(dst[0:QR - P, 1, :]), wq_d[m, P:QR, ds(pair * 384, 384)]).then_inc(hd_ldq, 16)

            def load_wuvo(pair):
                for m, dst in enumerate((wuvo_h, wuvo_l)):
                    sp.dma_start(f(dst[:]), wuvo_d[m, ds(pair * P, P), :]).then_inc(hd_ldu, 16)

            load_wq(0)
            load_wuvo(0)
            wait_apart(sp, hd_q, 6)
            load_wq(1)
            with sp.Fori(1, PAIRS - 1) as j:
                wait_apart(sp, hd_q, 6 * j + 6)
                load_wq(j + 1)
                wait_apart(sp, hd_y, NT * j + 1)
                load_wuvo(j)
            wait_apart(sp, hd_y, NT * (PAIRS - 1) + 1)
            load_wuvo(PAIRS - 1)
            meet(sp, 4)
            sp.dma_start(lA_sb[:], lA.rearrange("n r d -> (n r) d")).then_inc(ld_e, 16)
            for k in range(NK):
                sp.dma_start(lB_sb[:, k, :].rearrange("p (n r) -> p n r", n=LORA_N),
                             lB[:, tile(k), :].rearrange("n p r -> p n r")).then_inc(ld_e, 16)
            for n in range(LORA_N):
                sp.dma_start(lc_col[n * LORA_R:(n + 1) * LORA_R, :], row(lcoef[n:n + 1], 1, LORA_R)).then_inc(ld_e, 16)
            sp.dma_start(lW_sb[:], lW.rearrange("(k p) n -> p k n", p=P)).then_inc(ld_e, 16)
            sp.dma_start(row_bc[:], row(lbias, HID)).then_inc(ld_e, 16)
            for t in range(NT):
                sp.wait_ge(en_o, t + 1)
                sp.dma_start(out[0, tile(t), :], xt(t)).then_inc(st_out, 16)
            sp.wait_ge(st_out, 16 * NT)

        @block.gpsimd
        def _(pool):
            pool.memset(ident[:], 0.0)
            pool.memset(ones[:], 1.0)
            pool.drain()
            pool.affine_select(out=ident[:], in_=ident[:], compare_op=ALU.not_equal, fill=1.0, base=0,
                               pattern=[[-1, P]], channel_multiplier=1)
            pool.drain().then_inc(consts, 1)
            for chunk in range(WCHUNKS):
                m, s, width = wt_chunk(chunk)
                slot = wring[:, chunk % 3, 0:width]
                pool.wait_ge(ld_w[chunk % 3], 32 * (chunk // 3 + 1))
                pool.tensor_tensor(slot, slot, base[m][:, s * width:(s + 1) * width], ALU.subtract).then_inc(wt_d, 1)
            meet(pool, 1)
            meet(pool, 2)
            pool.memset(mbias[:, 0:P], 0.0)
            pool.drain()
            pool.affine_select(out=mbias[:, 0:P], in_=mbias[:, 0:P], compare_op=ALU.is_ge, fill=BIG, base=0,
                               pattern=[[-1, P]], channel_multiplier=1).then_inc(ix_mask, 1)

            def split_index():
                pool.tensor_copy(iwq_h[:], iwq_raw[:])
                pool.drain()
                pool.tensor_tensor(iwq_l[:], iwq_raw[:], f(iwq_h[:]), ALU.subtract).then_inc(ix_w, 1)

            pool.wait_ge(ix_ld, 16)
            split_index()
            with pool.Fori(0, IDXH) as n:
                pool.drain()
                pool.wait_ge(ix_ld, 16 * n + 32)
                wait_apart(pool, ix_q, 2 * n + 2)
                split_index()
            pool.wait_ge(ix_acc, IDXH * (NT - 1) + 1)
            for t in range(1, NT):
                d = acc[:, TRI[t] - P + t * P:TRI[t] + t * P]
                pool.affine_select(out=d, in_=d, compare_op=ALU.is_ge, fill=FUTURE, base=0,
                                   pattern=[[-1, P]], channel_multiplier=1).then_inc(ix_mask, 1)
            rem = slice(0, QR - P)
            pool.wait_ge(lt_lo, NT)
            with pool.Fori(0, PAIRS) as j:
                wait_apart(pool, pr_ldq, 48 * j + 48)
                wait_apart(pool, pr_st, 96 * j + 1)
                for k, r in ((0, slice(0, P)), (1, rem)):
                    raw = qb_raw[r, k, :].rearrange("p (h n) -> p h n", h=2)
                    for a in range(2):
                        src = raw[:, 1 - a, NOPE:QKD]
                        pool.tensor_copy(pq[0][r, k, P + a * ROPE:P + (a + 1) * ROPE], src)
                    pool.drain()
                    for a in range(2):
                        src = raw[:, 1 - a, NOPE:QKD]
                        c = slice(P + a * ROPE, P + (a + 1) * ROPE)
                        pool.tensor_tensor(pq[1][r, k, c], src, f(pq[0][r, k, c]), ALU.subtract)
                    pool.drain()
                    for part in pq:
                        src = f(part[r, k, P:256]).rearrange("p (i two) -> p i two", two=2)
                        dst = part[r, k, 256:384].rearrange("p (i two) -> p i two", two=2)
                        for o in range(2):
                            pool.tensor_copy(dst[:, :, o:o + 1], src[:, :, 1 - o:2 - o])
                    pool.drain()
                pool.drain().then_inc(pr_raw, 1)
                wait_apart(pool, pr_ev, j + 2)
                pool.tensor_copy(pq[0][:, 0, 0:P], pr_out[:, 0:P])
                pool.tensor_copy(pu[0][:], pr_out[:, 256:768])
                pool.drain()
                pool.tensor_tensor(pq[1][:, 0, 0:P], pr_out[:, 0:P], f(pq[0][:, 0, 0:P]), ALU.subtract)
                pool.tensor_tensor(pu[1][:], pr_out[:, 256:768], f(pu[0][:]), ALU.subtract)
                pool.drain()
                pool.tensor_copy(pq[0][rem, 1, 0:P], pr_out[rem, P:256])
                pool.drain()
                pool.tensor_tensor(pq[1][rem, 1, 0:P], pr_out[rem, P:256], f(pq[0][rem, 1, 0:P]), ALU.subtract)
                pool.drain().then_inc(pr_sp, 1)
            meet(pool, 3)

            pool.memset(f(wq_h[QR - P:P, 1, :]), 0.0)
            pool.memset(f(wq_l[QR - P:P, 1, :]), 0.0)
            pool.drain().then_inc(hd_wz, 1)

            def pair_work(j, par, last, order=POOL_ORDER):
                for kind, i, p in steps(order, j, last):
                    if kind == "S":
                        w = (i % NT + 1) * P
                        wait_apart(pool, hd_rec, 16 * p + i + 1)
                        pool.tensor_scalar(pm[:, i % 4, 0:w], pm[:, i % 4, 0:w], smx[:, 32 + i:33 + i], 0.0,
                                           ALU.mult, ALU.add).then_inc(hd_p, 1)
                    elif kind == "G":
                        wait_apart(pool, hd_rm, 4 * p + 2 * i + 2)
                        pool.tensor_tensor(rop[:, i, 0, :], rop[:, i, 0, :], rop[:, i, 1, :], ALU.add)
                        pool.drain().then_inc(hd_rot, 1)
                    else:
                        c = slice(512 * i, 512 * i + 512)
                        qh, ql = qc_h[1 - par], qc_l[1 - par]
                        pool.drain()
                        wait_apart(pool, hd_qhi, 4 * p + 2 * i + 2)
                        pool.tensor_tensor(ql[KR:P, 0, c], rop[KR:P, i, 0, :], f(qh[KR:P, 0, c]), ALU.subtract)
                        pool.tensor_tensor(ql[0:KR, 1, c], rop[0:KR, i, 0, :], f(qh[0:KR, 1, c]), ALU.subtract)
                        pool.drain().then_inc(hd_qlo, 1)

            pair_work(-1, 1, False, "G0 R0 G1 R1 S16 S17 S18 S19")
            with pool.Fori(0, PAIRS // 2 - 1) as q:
                pair_work(2 * q, 0, False)
                pair_work(2 * q + 1, 1, False)
            pair_work(PAIRS - 2, 0, False)
            pair_work(PAIRS - 1, 1, True)
            meet(pool, 4)

        @block.scalar
        def _(act):
            COPY = ACT.Copy

            def sqrt(k, n):
                act.wait_ge(rs_v, k + 1)
                act.activation(rs_sqrt[:, 0:n], rs_var[:, 0:n], ACT.Sqrt).then_inc(rs_s, 1)

            def norm_hi(l):
                for t in range(NT):
                    act.wait_ge(ln_tr, NT * l + t + 1)
                    act.activation(xn_h[:, :, tile(t)], ps[:, t % 2, :].rearrange("p (k s) -> p k s", k=NK),
                                   COPY).then_inc(ln_hi, 1)

            chunks = list(range(WCHUNKS))

            def weight_chunk():
                chunk = chunks.pop(0)
                m, s, width = wt_chunk(chunk)
                slot = wring[:, chunk % 3, 0:width]
                act.wait_ge(wt_d, chunk + 1)
                act.activation(sgn[m][:, s * width:(s + 1) * width], slot, ACT.Sign)
                act.drain()
                act.activation(slot, slot, ACT.Abs, accum_out=absum[:, chunk:chunk + 1])
                act.drain().then_inc(wt_abs, 1)

            sqrt(0, NT)
            norm_hi(0)
            for u in range(4):
                act.wait_ge(at_proj, u + 1)
                if u >= 2:
                    act.wait_ge(at_qkv, u - 1)
                act.activation(xn_t[:, u % 2, :], ps[:, u, :], ACT.Identity,
                               bias=bq_col[:, u // 2:u // 2 + 1]).then_inc(at_q, 1)
            for kind, i in ATT_ORDER:
                if kind == "S":
                    act.wait_ge(at_max, i + 1)
                    act.activation(p0[:, i % 2, :], two_banks(2 * (i % 2)), ACT.Exp,
                                   bias=sm0[:, NT + i:NT + i + 1], scale=float(D0) ** -0.5,
                                   accum_out=sm0[:, 2 * NT + i:2 * NT + i + 1])
                    act.drain().then_inc(at_exp, 1)
                    weight_chunk()
                elif kind == "T":
                    for c in range(2):
                        act.wait_ge(at_tr, 2 * i + c + 1)
                        act.activation(pTx_h[:, 4 * c:4 * c + 4, tile(i % 4)],
                                       ps[:, 4 + c, :].rearrange("p (k s) -> p k s", k=4), COPY).then_inc(at_hi, 1)
                elif kind == "O":
                    act.wait_ge(at_o, i + 1)
                    act.activation(oT_h[:], ps[:, 6, :], COPY).then_inc(at_ohi, 1)
            while chunks:
                weight_chunk()
            act.drain().then_inc(wt_tot, 1)
            sqrt(1, NT)
            norm_hi(1)
            meet(act, 1)

            def weight_hi(g, par, k):
                act.wait_ge(ff_tr, 3 * g + k + 1)
                act.activation(wc_h[:, par, k, :], ps[:, 6 + (3 * par + k) % 2, :], COPY).then_inc(ff_hi, 1)

            with act.Fori(0, 2) as half:
                for k in range(3):
                    weight_hi(half * NI, 0, k)

                def step(s, par, last=False):
                    g = half * NI + s
                    if not last:
                        weight_hi(g + 1, 1 - par, 0)
                        weight_hi(g + 1, 1 - par, 1)
                    act.wait_ge(ff_gate, g + 1)
                    act.wait_ge(ff_mul, g + 1)
                    act.activation(silu[:], ps[:, 4, :], ACT.Silu).then_inc(ff_silu, 1)
                    act.wait_ge(ff_mul, g + 2)
                    act.activation(hT_h[:, par, :], hf[:], COPY).then_inc(ff_hhi, 1)
                    if not last:
                        weight_hi(g + 1, 1 - par, 2)

                with act.Fori(0, NI - 2, 2) as s:
                    step(s, 0)
                    step(s + 1, 1)
                step(NI - 2, 0)
                step(NI - 1, 1, last=True)
            meet(act, 2)
            sqrt(2, NT)
            norm_hi(2)
            for t in range(NT):
                act.wait_ge(lt_mm, t + 1)
                act.activation(lat[:, t, :], ps[:, 2 + t % 2, 0:LATW], COPY).then_inc(lt_ev, 1)
            sqrt(3, 16)
            for t in range(NT):
                act.wait_ge(lt_tr, t + 1)
                src = ps[:, 4 + t % 2, :]
                act.activation(latT_h[:, 0, tile(t)], src[:, 0:P], COPY)
                act.activation(latT_h[0:QR - P, 1, tile(t)], ps[0:QR - P, 4 + t % 2, P:2 * P], COPY)
                act.activation(latT_h[:, 2:4, tile(t)], src[:, 2 * P:4 * P].rearrange("p (k s) -> p k s", k=2), COPY)
                act.drain().then_inc(lt_hi, 1)
            for b in range(2):
                act.wait_ge(ix_q, b + 1)
                act.activation(ikT_h[:, b * 512:(b + 1) * 512], ps[:, b, :], COPY).then_inc(ix_qhi, 1)
            with act.Fori(0, IDXH) as n:
                for b in range(2):
                    act.wait_ge(ix_q, 2 * n + b + 3)
                    act.activation(iqT_h[:, b * 512:(b + 1) * 512], ps[:, b, :], COPY).then_inc(ix_qhi, 1)
                for t in range(1, NT):
                    w = (t + 1) * P
                    act.wait_ge(ix_s, (NT - 1) * n + t)
                    act.wait_ge(ix_acc, (NT - 1) * n + max(t - 2, 0) + 1)
                    act.activation(relu[:, t % 2, 0:w], two_banks(2 + 2 * (t % 2), w), ACT.Relu).then_inc(ix_r, 1)
            act.wait_ge(lt_lo, NT)
            with act.Fori(0, PAIRS) as j:
                act.wait_ge(pr_t, 2 * j + 2)
                act.activation(kvbT[:].rearrange("p a n -> p (a n)"), ps[:, 0, 0:4 * KR], COPY).then_inc(pr_tev, 1)
                act.wait_ge(pr_t, 2 * j + 3)
                act.activation(qbT[:].rearrange("p a n -> p (a n)"), ps[:, 1, 0:2 * QR], COPY).then_inc(pr_tev, 1)
                act.wait_ge(pr_mm, j + 2)
                act.wait_ge(pr_sp, j + 1)
                act.activation(pr_out[:, 0:P], ps[:, 6, 0:P], COPY, scale=-float(QKD) ** -0.5)
                act.activation(pr_out[0:QR - P, P:256], ps[0:QR - P, 6, P:256], COPY,
                               scale=-float(QKD) ** -0.5)
                act.activation(pr_out[:, 256:768], ps[:, 7, :], COPY)
                act.drain().then_inc(pr_ev, 1)
                wait_apart(act, pr_sp, j + 2)
                for m in range(2):
                    act.dma_start(wq_d[m, 0:P, ds(j * 384, 384)], f(pq[m][:, 0, :])).then_inc(pr_st, 16)
                    act.dma_start(wq_d[m, P:QR, ds(j * 384, 384)], f(pq[m][0:QR - P, 1, :])).then_inc(pr_st, 16)
                    act.dma_start(wuvo_d[m, ds(j * P, P), :], f(pu[m][:])).then_inc(pr_st, 16)
            act.wait_ge(pr_st, 96 * PAIRS + 1)
            meet(act, 3)

            def pair_work(j, par, last, order=ACT_ORDER):
                for kind, i, p in steps(order, j, last):
                    if kind == "S":
                        w = (i % NT + 1) * P
                        act.wait_ge(hd_max, 16 * p + i + 1)
                        act.activation(pm[:, i % 4, 0:w], pm[:, i % 4, 0:w], ACT.Exp, bias=smx[:, i:i + 1],
                                       scale=-1.0, accum_out=smx[:, 16 + i:17 + i])
                        act.drain().then_inc(hd_exp, 1)
                    elif kind == "T":
                        t = i % NT
                        dst = pTa_h[:] if t < 4 else pTx_h
                        for c, g in GROUPS[i]:
                            nk = min(4, t + 1 - 4 * c)
                            act.wait_ge(hd_tr, NG * p + g + 1)
                            act.activation(dst[:, 4 * c:4 * c + nk, tile(t % 4)],
                                           ps[:, 4 + g % 2, 0:nk * P].rearrange("p (k s) -> p k s", k=nk),
                                           COPY).then_inc(hd_hi, 1)
                    elif kind == "V":
                        h, b = divmod(i, 2)
                        mine, other = slice(KR * h, KR * h + KR), slice(KR * (1 - h), KR * (1 - h) + KR)
                        act.wait_ge(hd_o, 4 * p + i + 1)
                        act.activation(ol_half[mine, :], ps[other, 6, :], COPY).then_inc(hd_ocp, 1)
                    elif kind == "W":
                        h, b = divmod(i, 2)
                        mine = slice(KR * h, KR * h + KR)
                        act.wait_ge(hd_of, 4 * p + i + 2)
                        act.activation(ol_h[mine, 512 * b:512 * b + 512], ol_f[mine, :], COPY).then_inc(hd_ohi, 1)
                    elif kind == "Q":
                        n, bank = i // 3, Q_BANKS[i]
                        c = slice(512 * n, 512 * n + 512)
                        act.wait_ge(hd_q, 6 * p + i + 1)
                        act.activation(qc_h[1 - par][0:KR, 0, c], ps[0:KR, bank, :], COPY)
                        act.activation(qc_h[1 - par][KR:P, 1, c], ps[KR:P, bank, :], COPY).then_inc(hd_qhi, 1)
                    else:
                        c = slice(512 * i, 512 * i + 512)
                        act.wait_ge(hd_rot, 2 * p + i + 1)
                        act.activation(qc_h[1 - par][KR:P, 0, c], rop[KR:P, i, 0, :], COPY)
                        act.activation(qc_h[1 - par][0:KR, 1, c], rop[0:KR, i, 0, :], COPY).then_inc(hd_qhi, 1)

            pair_work(-1, 1, False, "Q2 R0 Q5 R1 S16 S17 S18 S19")
            with act.Fori(0, PAIRS // 2 - 1) as q:
                pair_work(2 * q, 0, False)
                pair_work(2 * q + 1, 1, False)
            pair_work(PAIRS - 2, 0, False)
            pair_work(PAIRS - 1, 1, True)
            meet(act, 4)
            sqrt(4, NT)
            norm_hi(3)
            act.wait_ge(en_tb, 1)
            act.wait_ge(en_c, 1)
            act.activation(lBT[:], ps[:, 0, :], ACT.Identity, scale=lc2_col[:]).then_inc(en_bt, 1)
            for k in range(NK):
                act.wait_ge(en_tw, k + 1)
                act.activation(lWT[:, k, :], ps[:, 1 + k, :], COPY).then_inc(en_wt, 1)

        @block.vector
        def _(dve):
            dve.drain().then_inc(ff_lo, 2)
            dve.drain().then_inc(ff_mul, 1)
            dve.drain().then_inc(ff_x, 1)
            dve.drain().then_inc(ix_acc, 1)
            dve.drain().then_inc(hd_lo, 2)
            dve.drain().then_inc(hd_of, 1)
            dve.drain().then_inc(hd_x, NT)

            def rsqrt(k, n):
                v, r, q = rs_var[:, 0:n], rs_out[:, 0:n], rs_tmp[:, 0:n]
                dve.drain().then_inc(rs_v, 1)
                dve.wait_ge(rs_s, k + 1)
                dve.reciprocal(r, rs_sqrt[:, 0:n])
                dve.drain()
                dve.tensor_tensor(q, r, r, ALU.mult)
                dve.drain()
                dve.tensor_tensor(q, q, v, ALU.mult)
                dve.drain()
                dve.tensor_scalar(q, q, -0.5, 1.5, ALU.mult, ALU.add)
                dve.drain()
                dve.tensor_tensor(r, r, q, ALU.mult)
                dve.drain()

            def split(hi, lo, src):
                dve.tensor_copy(hi, src)
                dve.drain()
                return dve.tensor_tensor(lo, src, f(hi), ALU.subtract)

            def norm(l, k):
                for t in range(NT):
                    if l == 0:
                        dve.wait_ge(ld_x, 16 * NT)
                    dve.bn_stats(stats[:, 6 * t:6 * t + 6], xt(t))
                dve.drain()
                for t in range(NT):
                    dve.bn_aggr(mv[:, t, :], stats[:, 6 * t:6 * t + 6])
                dve.drain()
                dve.tensor_scalar(rs_var[:, 0:NT], mv[:, :, 1], EPS, None, ALU.add)
                rsqrt(k, NT)

                def lo(t):
                    dve.wait_ge(ln_hi, NT * l + t + 1)
                    dve.tensor_tensor(xn_l[:, :, tile(t)], ps[:, t % 2, :].rearrange("p (k s) -> p k s", k=NK),
                                      f(xn_h[:, :, tile(t)]), ALU.subtract).then_inc(ln_lo, 1)

                for t in range(NT):
                    if t >= 2:
                        dve.wait_ge(ln_tr, NT * l + t - 1)
                    dve.tensor_scalar(xn_t[:, t % 2, :], xt(t), mv[:, t, 0:1], rs_out[:, t:t + 1],
                                      ALU.subtract, ALU.mult).then_inc(ln_xn, 1)
                    if t >= 1:
                        lo(t - 1)
                lo(NT - 1)
                dve.drain()

            norm(0, 0)
            dve.wait_ge(ld_a, 80)
            raw = base[2][:, 0:NK * 3 * D0].rearrange("p (k n) -> p k n", k=NK)
            split(wqkv_h[:], wqkv_l[:], raw)
            split(wo_h[:], wo_l[:], base[2][:, 2048:2048 + HID])
            dve.drain().then_inc(at_w, 1)
            for t in range(NT):
                dve.tensor_tensor(xt(t), xt(t), row_bc[:], ALU.add)
            for u in range(4):
                m, n = divmod(u, 2)
                c = slice(512 * n, 512 * n + 512)
                dve.wait_ge(at_q, u + 1)
                split(qkT_h[:, m, c], qkT_l[:, m, c], xn_t[:, u % 2, :])
                dve.drain().then_inc(at_qkv, 1)
            for b in range(2):
                dve.wait_ge(at_proj, 5 + b)
                tmp = xn_t[:, b, :].rearrange("p (k s) -> p k s", k=4)
                for i in range(4):
                    dve.tensor_tensor(tmp[:, i, :], ps[:, 4 + b, tile(i)], bv_bc[:], ALU.add)
                dve.drain()
                split(v_h[:, 4 * b:4 * b + 4, :], v_l[:, 4 * b:4 * b + 4, :], tmp)
                dve.drain().then_inc(at_v, 1)
            for kind, i in ATT_ORDER:
                if kind == "S":
                    dve.wait_ge(at_s, i + 1)
                    dve.tensor_reduce(sm0[:, i:i + 1], two_banks(2 * (i % 2)), AXX, ALU.max)
                    dve.drain()
                    dve.tensor_scalar(sm0[:, NT + i:NT + i + 1], sm0[:, i:i + 1], -float(D0) ** -0.5, None, ALU.mult)\
                        .then_inc(at_max, 1)
                elif kind == "T":
                    for c in range(2):
                        dve.wait_ge(at_hi, 2 * i + c + 1)
                        dst = (slice(None), slice(4 * c, 4 * c + 4), tile(i % 4))
                        dve.tensor_tensor(pTx_l[dst], ps[:, 4 + c, :].rearrange("p (k s) -> p k s", k=4),
                                          f(pTx_h[dst]), ALU.subtract).then_inc(at_lo, 1)
                elif kind == "O":
                    dve.wait_ge(at_ohi, i + 1)
                    dve.tensor_tensor(oT_l[:], ps[:, 6, :], f(oT_h[:]), ALU.subtract).then_inc(at_ot, 1)
                    dve.reciprocal(sm0[:, 3 * NT + 4 * i:3 * NT + 4 * i + 4], sm0[:, 2 * NT + 4 * i:2 * NT + 4 * i + 4])
                    dve.drain()
                else:
                    dve.wait_ge(at_y, i + 1)
                    dve.scalar_tensor_tensor(xt(i), ps[:, 7, :], sm0[:, 3 * NT + i:3 * NT + i + 1], xt(i),
                                             ALU.mult, ALU.add).then_inc(at_x, 1)
            dve.drain()
            norm(1, 1)
            dve.wait_ge(wt_tot, 2)
            for m, (a, b) in enumerate(((0, NI), (NI, 2 * NI), (2 * NI, WCHUNKS))):
                dve.tensor_reduce(coef[:, m:m + 1], ps[:, 7, a:b], AXX, ALU.add)
            dve.drain()
            dve.tensor_scalar(coef[:], coef[:], 1.0 / (INTER * HID), None, ALU.mult)
            meet(dve, 1)

            def effective(s, k):
                dst = weff[:, k, :]
                if k < 2:
                    sg, bs = sgn[k][:, ds(s * 512, 512)], base[k][:, ds(s * 512, 512)]
                else:
                    sg, bs = (a[:].rearrange("p (c n) -> p c n", c=NK)[:, :, ds(s * P, P)]
                              for a in (sgn[2], base[2]))
                    dst = dst.rearrange("p (c n) -> p c n", c=NK)
                dve.scalar_tensor_tensor(dst, sg, coef[:, k:k + 1], bs, ALU.mult, ALU.add).then_inc(ff_we, 1)

            def weight_lo(g, par, k):
                dve.wait_ge(ff_hi, 3 * g + k + 1)
                dve.tensor_tensor(wc_l[:, par, k, :], ps[:, 6 + (3 * par + k) % 2, :], f(wc_h[:, par, k, :]),
                                  ALU.subtract).then_inc(ff_lo, 1)

            with dve.Fori(0, 2) as half:
                for k in range(3):
                    effective(0, k)
                for k in range(3):
                    weight_lo(half * NI, 0, k)
                    effective(1, k)

                def step(s, par, ahead=True, last=False):
                    g = half * NI + s
                    for k in range(0 if last else 2):
                        weight_lo(g + 1, 1 - par, k)
                        if ahead:
                            effective(s + 2, k)
                    dve.wait_ge(ff_silu, g + 1)
                    dve.wait_ge(ff_up, g + 1)
                    dve.tensor_tensor(hf[:], ps[:, 5, :], silu[:], ALU.mult).then_inc(ff_mul, 1)
                    dve.drain()
                    dve.wait_ge(ff_hhi, g + 1)
                    dve.tensor_tensor(hT_l[:, par, :], hf[:], f(hT_h[:, par, :]), ALU.subtract).then_inc(ff_h, 1)
                    dve.drain()
                    if not last:
                        weight_lo(g + 1, 1 - par, 2)
                        if ahead:
                            effective(s + 2, 2)

                with dve.Fori(0, (NI - 2) // 2) as q:
                    step(2 * q, 0)
                    step(2 * q + 1, 1)
                step(NI - 2, 0, ahead=False)
                step(NI - 1, 1, last=True)
                for i in range(4):
                    xs = x[:, ds((half * 4 + i) * HID, HID)]
                    dve.wait_ge(ff_y, 4 * half + i + 1)
                    dve.tensor_tensor(xs, xs, ps[:, i, :], ALU.add).then_inc(ff_x, 1)
                dve.drain()
            meet(dve, 2)
            norm(2, 2)
            dve.memset(f(latT_h[QR - P:P, 1, :]), 0.0)
            dve.memset(f(latT_l[QR - P:P, 1, :]), 0.0)
            dve.memset(acc[:], 0.0)
            dve.wait_ge(ld_l, 16 * 18)
            split(wlat_h[:], wlat_l[:], wlat_raw[:])
            dve.drain().then_inc(lt_w, 1)
            dve.wait_ge(lt_ev, NT)
            for c, (a, w) in enumerate(((0, QR), (QR, KR))):
                sq = lat_sq[:, :, 0:w]
                dve.tensor_tensor(sq, lat[:, :, a:a + w], lat[:, :, a:a + w], ALU.mult)
                dve.drain()
                dve.tensor_reduce(rs_var[:, NT * c:NT * c + NT], sq, AXX, ALU.add)
                dve.drain()
                dve.tensor_scalar(rs_var[:, NT * c:NT * c + NT], rs_var[:, NT * c:NT * c + NT], 1.0 / w, EPS,
                                  ALU.mult, ALU.add)
                dve.drain()
            rsqrt(3, 16)
            for t in range(NT):
                for c, (a, w) in enumerate(((0, QR), (QR, KR))):
                    dve.scalar_tensor_tensor(latn[:, t, a:a + w], lat[:, t, a:a + w],
                                             rs_out[:, NT * c + t:NT * c + t + 1], norm_bc[:, a:a + w],
                                             ALU.mult, ALU.mult)
            kp = lat[:, :, QR + KR:QR + KR + ROPE].rearrange("p t (i two) -> p t i two", two=2)
            ko = latn[:, :, QR + KR:QR + KR + ROPE].rearrange("p t (i two) -> p t i two", two=2)
            for o in range(2):
                own, partner = kp[:, :, :, o], kp[:, :, :, 1 - o]
                dve.tensor_tensor(rope_t[:, 0], own, cosk[:], ALU.mult)
                dve.tensor_tensor(rope_t[:, 1], partner, sink[:], ALU.mult)
                dve.drain()
                dve.tensor_tensor(ko[:, :, :, o], rope_t[:, 0], rope_t[:, 1], ALU.add if o else ALU.subtract)
                dve.drain()
            lv = latn[:, :, QR:QR + KR]
            dve.tensor_copy(latn[:, :, QR + KR + ROPE:384], lv)
            dve.tensor_copy(v3[:, :, 0:KR], lv)
            dve.tensor_copy(v3[:, :, 2 * KR:3 * KR], lv)
            dve.drain()
            dve.tensor_tensor(v3[:, :, KR:2 * KR], lv, f(v3[:, :, 0:KR]), ALU.subtract)
            dve.tensor_scalar(iw[:], lat[:, :, QR + KR + ROPE:LATW], float(IDXH) ** -0.5 * float(IDXD) ** -0.5, None,
                              ALU.mult)
            dve.drain().then_inc(lt_norm, 1)
            for t in range(NT):
                dve.wait_ge(lt_hi, t + 1)
                src = ps[:, 4 + t % 2, :]
                dve.tensor_tensor(latT_l[:, 0, tile(t)], src[:, 0:P], f(latT_h[:, 0, tile(t)]), ALU.subtract)
                dve.tensor_tensor(latT_l[0:QR - P, 1, tile(t)], ps[0:QR - P, 4 + t % 2, P:2 * P],
                                  f(latT_h[0:QR - P, 1, tile(t)]), ALU.subtract)
                dve.tensor_tensor(latT_l[:, 2:4, tile(t)], src[:, 2 * P:4 * P].rearrange("p (k s) -> p k s", k=2),
                                  f(latT_h[:, 2:4, tile(t)]), ALU.subtract)
                dve.drain().then_inc(lt_lo, 1)

            def index_lo(hi, lo, b, count):
                c = slice(512 * b, 512 * b + 512)
                dve.wait_ge(ix_qhi, count)
                dve.tensor_tensor(lo[:, c], ps[:, b, :], f(hi[:, c]), ALU.subtract).then_inc(ix_qlo, 1)

            for b in range(2):
                index_lo(ikT_h, ikT_l, b, b + 1)
            with dve.Fori(0, IDXH) as n:
                for b in range(2):
                    index_lo(iqT_h, iqT_l, b, 2 * n + b + 3)
                dve.drain()
                for t in range(1, NT):
                    w = (t + 1) * P
                    at = acc[:, TRI[t] - P:TRI[t] - P + w]
                    dve.wait_ge(ix_r, (NT - 1) * n + t + 1)
                    dve.scalar_tensor_tensor(at, relu[:, t % 2, 0:w], iw[:, t, ds(n, 1)], at, ALU.mult, ALU.add)\
                        .then_inc(ix_acc, 1)
                dve.drain()
            for t in range(1, NT):
                at = acc[:, TRI[t] - P:TRI[t + 1] - P]
                dve.wait_ge(ix_mask, t + 1)
                with dve.Fori(0, TOPK // 8):
                    dve.max(top8[:], at)
                    dve.drain()
                    dve.match_replace(at, top8[:], at, TAKEN)
                    dve.drain()
                dve.tensor_scalar(mbias[:, TRI[t]:TRI[t + 1]], at, TAKEN, BIG, ALU.not_equal, ALU.mult)
            meet(dve, 3)

            def reciprocal(count, i):
                dve.wait_ge(hd_exp, count)
                dve.reciprocal(smx[:, 32 + i:33 + i], smx[:, 16 + i:17 + i]).then_inc(hd_rec, 1)

            def pair_work(j, par, last, order=DVE_ORDER):
                for kind, i, p in steps(order, j, last):
                    if kind == "S":
                        t = i % NT
                        w = (t + 1) * P
                        if i >= 4:
                            dve.wait_ge(hd_tr, NG * p + GROUPS[i - 4][-1][1] + 1)
                        wait_apart(dve, hd_s, 16 * p + i + 1)
                        dve.tensor_tensor_reduce(out=pm[:, i % 4, 0:w], in0=two_banks(2 * (i % 2), w),
                                                 in1=mbias[:, TRI[t]:TRI[t + 1]], scale=1.0, scalar=3.0 * BIG,
                                                 op0=ALU.add, op1=ALU.min, accum_out=smx[:, i:i + 1])
                        dve.drain().then_inc(hd_max, 1)
                    elif kind == "C":
                        reciprocal(16 * p + i + 1, i)
                    elif kind == "T":
                        t = i % NT
                        dh, dl = (pTa_h[:], pTa_l[:]) if t < 4 else (pTx_h, pTx_l)
                        for c, g in GROUPS[i]:
                            nk = min(4, t + 1 - 4 * c)
                            at = (slice(None), slice(4 * c, 4 * c + nk), tile(t % 4))
                            dve.wait_ge(hd_hi, NG * p + g + 1)
                            dve.tensor_tensor(dl[at], ps[:, 4 + g % 2, 0:nk * P].rearrange("p (k s) -> p k s", k=nk),
                                              f(dh[at]), ALU.subtract).then_inc(hd_lo, 1)
                    elif kind == "V":
                        h, b = divmod(i, 2)
                        r, c = slice(KR * h, KR * h + KR), slice(512 * b, 512 * b + 512)
                        dve.wait_ge(hd_ocp, 4 * p + i + 1)
                        dve.tensor_tensor(ol_f[r, :], ps[r, 6, :], ol_half[r, :], ALU.add)
                        dve.drain().then_inc(hd_of, 1)
                    elif kind == "W":
                        h, b = divmod(i, 2)
                        r, c = slice(KR * h, KR * h + KR), slice(512 * b, 512 * b + 512)
                        dve.wait_ge(hd_ohi, 4 * p + i + 1)
                        dve.tensor_tensor(ol_l[r, c], ol_f[r, :], f(ol_h[r, c]), ALU.subtract).then_inc(hd_olo, 1)
                        dve.drain()
                    elif kind == "Q":
                        (n, piece), bank = divmod(i, 3), Q_BANKS[i]
                        c = slice(512 * n, 512 * n + 512)
                        if piece < 2:
                            dve.wait_ge(hd_q, 6 * p + i + 1)
                            dve.tensor_tensor(rop[:, n, piece, :], ps[:, bank, :], (cosq, sinq)[piece][:, c], ALU.mult)\
                                .then_inc(hd_rm, 1)
                        else:
                            qh, ql = qc_h[1 - par], qc_l[1 - par]
                            dve.wait_ge(hd_qhi, 4 * p + (1 if n == 0 else 3))
                            dve.tensor_tensor(ql[0:KR, 0, c], ps[0:KR, bank, :], f(qh[0:KR, 0, c]), ALU.subtract)
                            dve.tensor_tensor(ql[KR:P, 1, c], ps[KR:P, bank, :], f(qh[KR:P, 1, c]), ALU.subtract)\
                                .then_inc(hd_qalo, 1)
                    else:
                        dve.wait_ge(hd_y, NT * p + i + 2)
                        dve.tensor_tensor(xt(i), xt(i), ps[:, Y_BANKS[i], :], ALU.add).then_inc(hd_x, 1)
                dve.drain()

            pair_work(-1, 1, False, "Q0 Q1 Q2 Q3 Q4 Q5 S16 S17 C16 S18 C17 S19 C18")
            with dve.Fori(0, PAIRS // 2 - 1) as q:
                pair_work(2 * q, 0, False)
                pair_work(2 * q + 1, 1, False)
            pair_work(PAIRS - 2, 0, False)
            pair_work(PAIRS - 1, 1, True)
            meet(dve, 4)
            norm(3, 4)
            dve.wait_ge(ld_e, 16 * (3 + NK + LORA_N))
            dve.tensor_scalar(lc2_col[:], lc_col[:], LORA_SCALE, None, ALU.mult).then_inc(en_c, 1)
            for t in range(NT):
                dve.tensor_tensor(xt(t), xt(t), row_bc[:], ALU.add)
            for k in range(NK):
                dve.wait_ge(en_wt, k + 1)
                dve.wait_ge(en_mm, k + 1)
                dve.tensor_tensor(wfin_f[:, k, :], ps[:, (5, 6, 7, 0)[k], :], lWT[:, k, :], ALU.add)
                dve.drain()
                split(wfin_h[:, k, :], wfin_l[:, k, :], wfin_f[:, k, :])
                dve.drain().then_inc(en_w, 1)
            for t in range(NT):
                dve.wait_ge(en_y, t + 1)
                dve.tensor_tensor(xt(t), xt(t), ps[:, 1 + t % 2, :], ALU.add).then_inc(en_o, 1)

        @block.tensor
        def _(pe):
            pe.drain().then_inc(ix_r, 1)
            pe.drain().then_inc(pr_t, 1)
            pe.drain().then_inc(pr_mm, 1)
            pe.drain().then_inc(pr_st, 1)
            pe.drain().then_inc(pr_ev, 1)
            pe.drain().then_inc(pr_sp, 1)
            pe.drain().then_inc(pr_raw, 1)
            pe.drain().then_inc(hd_y, 1)
            pe.wait_ge(consts, 1)

            def norm_tr(l):
                for t in range(NT):
                    pe.wait_ge(ln_xn, NT * l + t + 1)
                    if t >= 2:
                        pe.wait_ge(ln_lo, NT * l + t - 1)
                    for k in range(NK):
                        last = pe.transpose(ps[:, t % 2, tile(k)], xn_t[:, t % 2, tile(k)], ident[:])
                    last.then_inc(ln_tr, 1)
                pe.wait_ge(ln_lo, NT * l + NT)

            norm_tr(0)
            pe.wait_ge(at_w, 1)
            for u in range(4):
                m, n = divmod(u, 2)
                c = slice(512 * n, 512 * n + 512)
                for k in range(NK):
                    last = mm3(pe, ps[:, u, :], wqkv_h[:, k, tile(m)], wqkv_l[:, k, tile(m)],
                               xn_h[:, k, c], xn_l[:, k, c], k == 0, k == NK - 1)
                last.then_inc(at_proj, 1)
            for t in range(NT):
                for k in range(NK):
                    last = mm3(pe, ps[:, 4 + t // 4, tile(t % 4)], xn_h[:, k, tile(t)], xn_l[:, k, tile(t)],
                               wqkv_h[:, k, tile(2)], wqkv_l[:, k, tile(2)], k == 0, k == NK - 1)
                if t % 4 == 3:
                    last.then_inc(at_proj, 1)
            pe.wait_ge(at_qkv, 4)
            for kind, i in ATT_ORDER:
                if kind == "S":
                    if i >= 2:
                        pe.wait_ge(at_exp, i - 1)
                    for n in range(2):
                        c = slice(512 * n, 512 * n + 512)
                        last = mm3(pe, ps[:, 2 * (i % 2) + n, :], qkT_h[:, 0, tile(i)], qkT_l[:, 0, tile(i)],
                                   qkT_h[:, 1, c], qkT_l[:, 1, c], True, True)
                    last.then_inc(at_s, 1)
                elif kind == "T":
                    pe.wait_ge(at_exp, i + 1)
                    for c in range(2):
                        if i == 0:
                            pe.wait_ge(at_v, c + 1)
                        else:
                            pe.wait_ge(at_lo, 2 * i + c - 1)
                        for k in range(4):
                            last = pe.transpose(ps[:, 4 + c, tile(k)], p0[:, i % 2, tile(4 * c + k)], ident[:])
                        last.then_inc(at_tr, 1)
                elif kind == "O":
                    pe.wait_ge(at_lo, 8 * (i + 1))
                    if i:
                        pe.wait_ge(at_ot, i)
                    for k in range(NT):
                        last = mm3(pe, ps[:, 6, :], v_h[:, k, :], v_l[:, k, :], pTx_h[:, k, :], pTx_l[:, k, :],
                                   k == 0, k == NT - 1)
                    last.then_inc(at_o, 1)
                else:
                    pe.wait_ge(at_ot, i // 4 + 1)
                    if i:
                        pe.wait_ge(at_x, i)
                    mm3(pe, ps[:, 7, :], oT_h[:, tile(i % 4)], oT_l[:, tile(i % 4)], wo_h[:], wo_l[:],
                        True, True).then_inc(at_y, 1)
            norm_tr(1)
            pe.wait_ge(wt_tot, 1)
            pe.matmul(ps[:, 7, 0:WCHUNKS], ones[:], absum[:], start=True, stop=True).then_inc(wt_tot, 1)
            meet(pe, 1)

            with pe.Fori(0, 2) as half:
                tokens = ds(half * 512, 512)

                def transposes(g, par, k):
                    pe.wait_ge(ff_we, 3 * g + k + 1)
                    pe.wait_ge(ff_lo, 3 * g + k + 1)
                    for c in range(NK):
                        last = pe.transpose(ps[:, 6 + (3 * par + k) % 2, tile(c)], weff[:, k, tile(c)], ident[:])
                    last.then_inc(ff_tr, 1)

                def project(g, par, k, done):
                    pe.wait_ge(ff_lo, 3 * g + k + 3)
                    for c in range(NK):
                        last = mm3(pe, ps[:, 4 + k, :], wc_h[:, par, k, tile(c)], wc_l[:, par, k, tile(c)],
                                   xn_h[:, c, tokens], xn_l[:, c, tokens], c == 0, c == NK - 1)
                    last.then_inc(done, 1)

                def down(g, par, first=False, last=False):
                    pe.wait_ge(ff_h, g + 1)
                    pe.wait_ge(ff_lo, 3 * g + 5)
                    for i in range(4):
                        one = mm3(pe, ps[:, i, :], hT_h[:, par, tile(i)], hT_l[:, par, tile(i)],
                                  wc_h[:, par, 2, :], wc_l[:, par, 2, :], first, last)
                        if last:
                            one.then_inc(ff_y, 1)

                def step(s, par, before="run", last=False):
                    g = half * NI + s
                    if not last:
                        transposes(g + 1, 1 - par, 0)
                    pe.wait_ge(ff_mul, g + 1)
                    project(g, par, 0, ff_gate)
                    if not last:
                        transposes(g + 1, 1 - par, 1)
                    project(g, par, 1, ff_up)
                    if before:
                        down(g - 1, 1 - par, first=before == "first")
                    if not last:
                        transposes(g + 1, 1 - par, 2)

                for k in range(3):
                    transposes(half * NI, 0, k)
                step(0, 0, before="")
                pe.wait_ge(ff_x, 4 * half + 1)
                step(1, 1, before="first")
                with pe.Fori(2, NI - 2, 2) as s:
                    step(s, 0)
                    step(s + 1, 1)
                step(NI - 2, 0)
                step(NI - 1, 1, last=True)
                down(half * NI + NI - 1, 1, last=True)
            meet(pe, 2)
            norm_tr(2)
            pe.wait_ge(lt_w, 1)
            for t in range(NT):
                if t >= 2:
                    pe.wait_ge(lt_ev, t - 1)
                for k in range(NK):
                    last = mm3(pe, ps[:, 2 + t % 2, 0:LATW], xn_h[:, k, tile(t)], xn_l[:, k, tile(t)],
                               wlat_h[:, k, :], wlat_l[:, k, :], k == 0, k == NK - 1)
                last.then_inc(lt_mm, 1)

            def index_project(ready):
                pe.wait_ge(ix_w, ready)
                for b in range(2):
                    c = slice(512 * b, 512 * b + 512)
                    for k in range(NK):
                        last = mm3(pe, ps[:, b, :], iwq_h[:, k, :], iwq_l[:, k, :], xn_h[:, k, c], xn_l[:, k, c],
                                   k == 0, k == NK - 1)
                    last.then_inc(ix_q, 1)

            index_project(1)
            pe.wait_ge(lt_norm, 1)
            for t in range(NT):
                if t >= 2:
                    pe.wait_ge(lt_lo, t - 1)
                b = 4 + t % 2
                pe.transpose(ps[:, b, 0:P], latn[:, t, 0:P], ident[:])
                pe.transpose(ps[0:QR - P, b, P:2 * P], latn[:, t, P:QR], ident[:])
                pe.transpose(ps[:, b, 2 * P:3 * P], latn[:, t, QR:QR + P], ident[:])
                pe.transpose(ps[:, b, 3 * P:4 * P], latn[:, t, QR + KR:QR + KR + P], ident[:]).then_inc(lt_tr, 1)
            pe.wait_ge(lt_lo, NT)
            with pe.Fori(0, IDXH) as n:
                pe.wait_ge(ix_qlo, 2 * n + 2)
                index_project(n + 2)
                for t in range(1, NT):
                    w = (t + 1) * P
                    pe.wait_ge(ix_qlo, 2 * n + (3 if t < 4 else 4))
                    pe.wait_ge(ix_r, (NT - 1) * n + max(t - 2, 0) + 1)
                    for b in range(1 if t < 4 else 2):
                        c = slice(512 * b, min(w, 512 * b + 512))
                        last = mm3(pe, ps[:, 2 + 2 * (t % 2) + b, 0:c.stop - c.start], iqT_h[:, tile(t)],
                                   iqT_l[:, tile(t)], ikT_h[:, c], ikT_l[:, c], True, True)
                    last.then_inc(ix_s, 1)
            with pe.Fori(0, PAIRS) as j:
                wait_apart(pe, pr_ldq, 48 * j + 48)
                for a in range(4):
                    last = pe.transpose(ps[:, 0, a * KR:(a + 1) * KR], kvb_raw[:, tile(a)], ident[0:KR, 0:KR])
                last.then_inc(pr_t, 1)
                for h in range(2):
                    pe.transpose(ps[:, 1, h * QR:h * QR + P], qb_raw[:, 0, h * QKD:h * QKD + NOPE], ident[:])
                    last = pe.transpose(ps[:, 1, h * QR + P:(h + 1) * QR],
                                        qb_raw[0:QR - P, 1, h * QKD:h * QKD + NOPE], ident[0:QR - P, 0:QR - P])
                last.then_inc(pr_t, 1)
                pe.wait_ge(pr_tev, 2 * j + 2)
                for h in range(2):
                    c = slice(h * KR, (h + 1) * KR)
                    pe.matmul(ps[:, 6, c], qbT[:, h, 0:P], kvbT[:, 2 * h, :], start=True, stop=True)
                    pe.matmul(ps[0:QR - P, 6, P + h * KR:P + (h + 1) * KR], qbT[:, h, P:QR], kvbT[:, 2 * h, :],
                              start=True, stop=True)
                pe.wait_ge(pr_ldo, 16 * j + 16)
                for h in range(2):
                    last = pe.matmul(ps[h * KR:(h + 1) * KR, 7, :], kvbT[:, 2 * h + 1, :], ow_raw[:, h, :],
                                     start=True, stop=True)
                last.then_inc(pr_mm, 1)
            meet(pe, 3)

            def pair_work(j, par, last, order=PE_ORDER):
                for kind, i, p in steps(order, j, last):
                    if kind == "S":
                        h, t = divmod(i, NT)
                        w = (t + 1) * P
                        q = par if i >= 4 else 1 - par
                        if i in (0, 4):
                            pe.wait_ge(hd_qlo, 2 * p + i // 4 + 1)
                            pe.wait_ge(hd_qalo, 2 * p + i // 4 + 1)
                        if i in (4, 5):
                            pe.wait_ge(hd_x, NT * p + i + 2)
                        if i >= 2 or order == PE_ORDER:
                            pe.wait_ge(hd_max, 16 * p + i - 1)
                        for b in range(1 if t < 4 else 2):
                            c = slice(512 * b, min(w, 512 * b + 512))
                            done = mm3(pe, ps[:, 2 * (i % 2) + b, 0:c.stop - c.start], qc_h[q][:, h, tile(t)],
                                       qc_l[q][:, h, tile(t)], latT_h[:, 2 + h, c], latT_l[:, 2 + h, c], True, True)
                        done.then_inc(hd_s, 1)
                    elif kind == "T":
                        t = i % NT
                        pe.wait_ge(hd_p, 16 * p + i + 1)
                        for c, g in GROUPS[i]:
                            pe.wait_ge(hd_lo, NG * p + g + 1)
                            if g == 0:
                                pe.wait_ge(hd_rm, 4 * p + 4)
                            if g == 1:
                                pe.wait_ge(hd_x, NT * p + NT)
                            for k in range(min(4, t + 1 - 4 * c)):
                                done = pe.transpose(ps[:, 4 + g % 2, tile(k)], pm[:, i % 4, tile(4 * c + k)], ident[:])
                            done.then_inc(hd_tr, 1)
                    elif kind == "V":
                        h, b = divmod(i, 2)
                        end = GROUPS[4 * i + 3][-1][1]
                        ph, pl = (pTa_h, pTa_l) if b == 0 else (pTx_h, pTx_l)
                        pe.wait_ge(hd_lo, NG * p + end + 3)
                        pe.wait_ge(hd_of, 4 * p + i + 1)
                        if i == 0 and not last:
                            pe.wait_ge(hd_rm, 4 * p + 6)
                        elif i == 0:
                            pe.wait_ge(hd_qalo, 2 * p + 2)
                        nk = 4 * b + 4
                        for k in range(nk):
                            q = slice(max(0, k - 4 * b) * P, 512)
                            v = v3[:, k, h * KR:h * KR + P]
                            pe.matmul(ps[:, 6, q], v, pl[:, k, q], start=k == 0, stop=False)
                            done = pe.matmul(ps[:, 6, q], v, ph[:, k, q], start=False, stop=k == nk - 1)
                        done.then_inc(hd_o, 1)
                    elif kind == "Q":
                        if i == 0:
                            pe.wait_ge(hd_ldq, 64 * p + 64)
                            if order == PE_ORDER:
                                pe.wait_ge(hd_x, NT * p - 3)
                        elif i == 1:
                            if order == PE_ORDER:
                                pe.wait_ge(hd_qalo, 2 * p)
                        elif i == 2:
                            pe.wait_ge(hd_rm, 4 * p + 1)
                        elif i == 3:
                            pe.wait_ge(hd_qalo, 2 * p + 1)
                        elif i == 4:
                            if order == PE_ORDER:
                                pe.wait_ge(hd_lo, NG * p + 1)
                        elif i == 5:
                            pe.wait_ge(hd_rm, 4 * p + 2)
                            pe.wait_ge(hd_of, 4 * p + 1)
                        w, c = (1, 2, 0)[i % 3], slice(512 * (i // 3), 512 * (i // 3) + 512)
                        for k in range(2):
                            done = mm3(pe, ps[:, Q_BANKS[i], :], wq_h[:, k, tile(w)], wq_l[:, k, tile(w)],
                                       latT_h[:, k, c], latT_l[:, k, c], k == 0, k == 1)
                        done.then_inc(hd_q, 1)
                    elif kind == "Y":
                        pe.wait_ge(hd_olo, 4 * p + (3 if i < 4 else 4))
                        pe.wait_ge(hd_ldu, 32 * p + 32)
                        if i == 0 and not last:
                            pe.wait_ge(hd_rm, 4 * p + 7)
                        elif i in (1, 2):
                            pe.wait_ge(hd_max, 16 * p + 16)
                        elif i == 3:
                            pe.wait_ge(hd_lo, NG * (p + 1) + 2)
                        elif i >= 4:
                            pe.wait_ge(hd_x, NT * p + NT + i - 3)
                        mm3(pe, ps[:, Y_BANKS[i], :], ol_h[:, tile(i)], ol_l[:, tile(i)], wuvo_h[:], wuvo_l[:],
                            True, True).then_inc(hd_y, 1)

            pe.wait_ge(hd_wz, 1)
            pair_work(-1, 1, False, "Q0 Q1 Q2 Q3 Q4 Q5 S16 S17 S18 S19")
            with pe.Fori(0, PAIRS // 2 - 1) as q:
                pair_work(2 * q, 0, False)
                pair_work(2 * q + 1, 1, False)
            pair_work(PAIRS - 2, 0, False)
            pair_work(PAIRS - 1, 1, True)
            meet(pe, 4)
            norm_tr(3)
            pe.wait_ge(ld_e, 16 * (3 + NK + LORA_N))
            for k in range(NK):
                last = pe.transpose(ps[:, 0, tile(k)], lB_sb[:, k, :], ident[:])
            last.then_inc(en_tb, 1)
            for k in range(NK):
                for c in range(NK):
                    last = pe.transpose(ps[:, 1 + k, tile(c)], lW_sb[:, c, tile(k)], ident[:])
                last.then_inc(en_tw, 1)
            pe.wait_ge(en_bt, 1)
            for k in range(NK):
                pe.matmul(ps[:, (5, 6, 7, 0)[k], :], lA_sb[:, tile(k)], lBT[:], start=True, stop=True).then_inc(en_mm, 1)
            pe.wait_ge(en_w, NK)
            for t in range(NT):
                if t >= 2:
                    pe.wait_ge(en_o, t - 1)
                for k in range(NK):
                    last = mm3(pe, ps[:, 1 + t % 2, :], xn_h[:, k, tile(t)], xn_l[:, k, tile(t)],
                               wfin_h[:, k, :], wfin_l[:, k, :], k == 0, k == NK - 1)
                last.then_inc(en_y, 1)


_INS = ['L0_attn_x', 'L0_attn_Wqkv', 'L0_attn_bqkv', 'L0_attn_Wo', 'L0_attn_bo', 'L0_ffn_w1', 'L0_ffn_mean_w1',
        'L0_ffn_w2', 'L0_ffn_mean_w2', 'L0_ffn_w3', 'L0_ffn_mean_w3', 'L1_attn_q_a_w', 'L1_attn_q_a_norm_w',
        'L1_attn_q_b_w', 'L1_attn_kv_a_w', 'L1_attn_kv_a_norm_w', 'L1_attn_kv_b_w', 'L1_attn_o_w',
        'L1_attn_idx_wq_w', 'L1_attn_idx_wk_w', 'L1_attn_idx_weights_w', 'L1_ffn_lora_A', 'L1_ffn_lora_B',
        'L1_ffn_W', 'L1_ffn_bias', 'L1_ffn_lora_weights']


def rope_tables():
    inv = (np.float32(1.0) / np.float32(10000.0) ** (np.arange(0, ROPE, 2, dtype=np.float32) / np.float32(ROPE)))
    ang = np.arange(S, dtype=np.float32)[:, None] * inv.astype(np.float32)[None, :]
    cos, sin = np.cos(ang).astype(np.float32), np.sin(ang).astype(np.float32)
    sign = np.where(np.arange(ROPE) % 2 == 0, -1.0, 1.0).astype(np.float32)
    scale = np.float32(-float(QKD) ** -0.5)
    cos_q = np.tile(np.repeat(cos, 2, axis=1).T, (2, 1)) * scale
    sin_q = np.tile((np.repeat(sin, 2, axis=1) * sign).T, (2, 1)) * scale
    cos_k, sin_k = (np.ascontiguousarray(a.reshape(NT, P, ROPE // 2).transpose(1, 0, 2)) for a in (cos, sin))
    return {"cos_q": np.ascontiguousarray(cos_q), "sin_q": np.ascontiguousarray(sin_q), "cos_k": cos_k, "sin_k": sin_k}


def kernel(**inputs):
    import concourse.bacc as _bacc
    from concourse.bass_utils import run_bass_kernel_spmd as _run

    nc = _bacc.Bacc("TRN2", target_bir_lowering=False, num_devices=1)
    arrays, args = {}, []
    for name, a in [(n, inputs[n]) for n in _INS] + list(rope_tables().items()):
        a = np.ascontiguousarray(a)
        arrays[f"in_{name}"] = a
        args.append(nc.dram_tensor(f"in_{name}", a.shape, F32, kind="ExternalInput").ap())
    args.append(nc.dram_tensor("out", (1, S, HID), F32, kind="ExternalOutput").ap())
    for name, shape in (("wq", (2, QR, PAIRS * 384)), ("wuvo", (2, PAIRS * P, HID))):
        args.append(nc.dram_tensor(name, shape, F32).ap())
    build(nc, *args)
    return _run(nc, [arrays], core_ids=[0]).results[0]["out"]
```

```python
from contextlib import ExitStack

import numpy as np

import concourse.bass as bass
from concourse import mybir

F32 = mybir.dt.float32
F32R = mybir.dt.float32r
BF16 = mybir.dt.bfloat16
I8 = mybir.dt.int8
ALU = mybir.AluOpType
ACT = mybir.ActivationFunctionType
AXX = mybir.AxisListType.X

P = 128
S = 1024
HID = 512
NT = S // P
NK = HID // P
D0 = 128
INTER = 1792
NI = INTER // P
HEADS, NOPE, ROPE, VD = 32, 128, 64, 128
QKD = NOPE + ROPE
QR, KR = 192, 64
IDXH, IDXD, TOPK = 16, 128, 128
PAIRS = HEADS // 2
LATW = QR + KR + ROPE + IDXH
LORA_N, LORA_R, LORA_SCALE = 8, 16, 2.0
EPS = 1e-5
BIG = 1.0e30
FUTURE = -3.0e38
TAKEN = -3.3e38
WCHUNKS = 2 * NI + 16
ROW_FREE = 9
RING = []
for _c in range(WCHUNKS):
    _slot = _c % 3 if _c < ROW_FREE else (_c - ROW_FREE) % 4
    _users = [_n for _n in range(_c) if RING[_n][0] == _slot]
    RING.append((_slot, _users[-1] if _users else None, len(_users)))
TRI = [P * (t * (t + 1) // 2) for t in range(NT + 1)]


def ds(start, size):
    return bass.ds(start, size)


ATT_ORDER = [(_step[0], int(_step[1:])) for _step in
             "S0 S1 S2 T0 S3 T1 S4 T2 S5 T3 S6 O0 T4 Y0 Y1 S7 Y2 T5 Y3 T6 T7 O1 Y4 Y5 Y6 Y7".split()]

PE_ORDER = """T0 Q0 S4 T1 S5 T2 Q1 S6 T3 S7 T4 S8 V0 Q2 T5 S9 T6 S10 Q3 T7 S11 T8 S12 T9 S13 T10 S14 V1 T11 S15
    T12 V2 T13 S16 S17 T14 S18 Y0 T15 Y1 Y2 V3 Q4 Y3 Q5 Y4 Y5 Y6 S19 Y7"""
DVE_ORDER = """T0 Q0 S4 S5 C3 C4 T1 T2 Q1 S6 T3 C5 S7 T4 C6 S8 C7 T5 S9 Q2 C8 T6 V0 S10 T7 C9 S11 Q3 C10 T8 S12
    C11 S13 S14 C12 T9 T10 W0 C13 V1 T11 S15 T12 W1 C14 V2 T13 W2 S16 C15 T14 T15 C16 S17 Y0 Y1 Y2 S18 V3 C17
    C18 Q4 W3 Y3 Y4 Y5 Y6 S19 Q5 Y7"""
ACT_ORDER = """T0 S4 T1 T2 T3 S5 T4 S6 S7 T5 Q2 S8 V0 T6 S9 T7 R0 W0 S10 T8 S11 T9 S12 T10 S13 S14 V1 T11 W1 T12
    V2 T13 W2 S15 T14 T15 S16 S17 V3 S18 W3 Q5 R1 S19"""
POOL_ORDER = """S4 S5 S6 S7 S8 G0 S9 S10 S11 S12 S13 R0 S14 S15 S16 S17 G1 R1 S18 S19"""

def steps(order, pair, last):
    for step in order.split():
        kind, i = step[0], int(step[1:])
        ahead = kind in "QGR" or i >= 16
        if not (ahead and last):
            yield kind, i % 16, pair + 1 if ahead else pair


Q_BANKS = (7, 6, 7, 7, 4, 6)
Y_BANKS = (7, 1, 3, 5, 7, 1, 3, 5)

GROUPS = []
for _i in range(16):
    GROUPS.append([])
    for _c in range(1 if _i % NT < 4 else 2):
        GROUPS[_i].append((_c, sum(map(len, GROUPS))))
NG = sum(map(len, GROUPS))


def build(nc, x_in, wqkv, bqkv, wo, bo, w1, m1, w2, m2, w3, m3, qa, qan, qb, kva, kvan, kvb, ow,
          iwq, iwk, iww, lA, lB, lW, lbias, lcoef, cos_q, sin_q, cos_k, sin_k, out,
          wq_d, wuvo_d):
    ctx = ExitStack()
    with ctx:
        def sem(name):
            return ctx.enter_context(nc.semaphore(name))

        def sbin(scope, name, shape, dt=F32):
            return scope.enter_context(nc.sbuf_tensor(name, shape, dt))

        def sb(name, shape, dt=F32):
            return sbin(ctx, name, shape, dt)

        x = sb("x", [P, NT * HID])
        xn_h = sb("xn_h", [P, NK, S], F32R)
        xn_l = sb("xn_l", [P, NK, S], F32R)
        ident = sb("ident", [P, P])
        ones = sb("ones", [P, P])
        stats = sb("stats", [P, NT * 6])
        mv = sb("mv", [P, NT, 2])
        rs_var = sb("rs_var", [P, 16])
        rs_sqrt = sb("rs_sqrt", [P, 16])
        rs_out = sb("rs_out", [P, 16])
        rs_tmp = sb("rs_tmp", [P, 16])
        row_bc = sb("row_bc", [P, HID])
        n_scope = ExitStack()
        xn_t = sbin(n_scope, "xn_t", [P, 2, HID])
        n_scope.close()
        oT = sb("oT", [P, 2, HID], F32R)
        ps = ctx.enter_context(nc.psum_tensor("ps", [P, 8, 512], F32))

        pTx_h = xn_h[:].rearrange("p k s -> p (k s)").rearrange("p (b q) -> p b q", q=512)
        pTx_l = xn_l[:].rearrange("p k s -> p (k s)").rearrange("p (b q) -> p b q", q=512)

        w_scope = ExitStack()
        base = [sbin(w_scope, f"base{m}", [P, NI * 512]) for m in range(3)]
        sgn = [sbin(w_scope, f"sgn{m}", [P, NI * 512], I8) for m in range(3)]
        absum = sbin(w_scope, "absum", [P, WCHUNKS])
        coef = sbin(w_scope, "coef", [P, 3])
        a_scope = ExitStack()
        qkT_h = sbin(a_scope, "qkT_h", [P, 2, S], F32R)
        qkT_l = sbin(a_scope, "qkT_l", [P, 2, S], F32R)
        v_h = sbin(a_scope, "v_h", [P, NT, D0], F32R)
        v_l = sbin(a_scope, "v_l", [P, NT, D0], F32R)
        bq_col = sbin(a_scope, "bq_col", [P, 2])
        bv_bc = sbin(a_scope, "bv_bc", [P, D0])
        wo_h = sbin(a_scope, "wo_h", [P, HID], F32R)
        wo_l = sbin(a_scope, "wo_l", [P, HID], F32R)
        sm0 = sbin(a_scope, "sm0", [P, 4 * NT])
        wring = sbin(a_scope, "wring", [P, 3, 512])
        q_scope = ExitStack()
        wqkv_h = sbin(q_scope, "wqkv_h", [P, NK, 3 * D0], F32R)
        wqkv_l = sbin(q_scope, "wqkv_l", [P, NK, 3 * D0], F32R)
        q_scope.close()
        p0 = sbin(a_scope, "p0", [P, 3, S])
        a_scope.close()
        f_scope = ExitStack()
        weff = sbin(f_scope, "weff", [P, 3, 512])
        wc_h = sbin(f_scope, "wc_h", [P, 2, 3, 512], F32R)
        wc_l = sbin(f_scope, "wc_l", [P, 2, 3, 512], F32R)
        silu = sbin(f_scope, "silu", [P, 512])
        hf = sbin(f_scope, "hf", [P, 512])
        hT_h = sbin(f_scope, "hT_h", [P, 2, 512], F32R)
        hT_l = sbin(f_scope, "hT_l", [P, 2, 512], F32R)
        f_scope.close()
        w_scope.close()

        l_scope = ExitStack()
        latT_h = sbin(l_scope, "latT_h", [P, 4, S], F32R)
        latT_l = sbin(l_scope, "latT_l", [P, 4, S], F32R)
        v3 = sbin(l_scope, "v3", [P, NT, 3 * KR], F32R)
        mbias = sbin(l_scope, "mbias", [P, TRI[NT]], BF16)
        cosq = sbin(l_scope, "cosq", [P, S])
        sinq = sbin(l_scope, "sinq", [P, S])
        i_scope = ExitStack()
        iw = sbin(i_scope, "iw", [P, NT, IDXH])
        ikT_h = sbin(i_scope, "ikT_h", [P, S], F32R)
        ikT_l = sbin(i_scope, "ikT_l", [P, S], F32R)
        iqT_h = sbin(i_scope, "iqT_h", [P, 2, 512], F32R)
        iqT_l = sbin(i_scope, "iqT_l", [P, 2, 512], F32R)
        iwq_raw = sbin(i_scope, "iwq_raw", [P, NK, IDXD])
        iwq_h = sbin(i_scope, "iwq_h", [P, NK, IDXD], F32R)
        iwq_l = sbin(i_scope, "iwq_l", [P, NK, IDXD], F32R)
        relu = sbin(i_scope, "relu", [P, 2, S])
        acc = sbin(i_scope, "acc", [P, TRI[NT] - P])
        t_scope = ExitStack()
        lat = sbin(t_scope, "lat", [P, NT, LATW])
        latn = sbin(t_scope, "latn", [P, NT, 384])
        lat_sq = sbin(t_scope, "lat_sq", [P, NT, QR])
        norm_bc = sbin(t_scope, "norm_bc", [P, QR + KR])
        cosk = sbin(t_scope, "cosk", [P, NT, ROPE // 2])
        sink = sbin(t_scope, "sink", [P, NT, ROPE // 2])
        rope_t = sbin(t_scope, "rope_t", [P, 2, NT, ROPE // 2])
        wlat_h = sbin(t_scope, "wlat_h", [P, NK, LATW], F32R)
        wlat_l = sbin(t_scope, "wlat_l", [P, NK, LATW], F32R)
        wlat_raw = sbin(t_scope, "wlat_raw", [P, NK, LATW])
        t_scope.close()
        r_scope = ExitStack()
        top8 = sbin(r_scope, "top8", [P, 4, 8])
        qb_raw = sbin(r_scope, "qb_raw", [P, 2, 2 * QKD])
        kvb_raw = sbin(r_scope, "kvb_raw", [KR, 512])
        ow_raw = sbin(r_scope, "ow_raw", [P, 2, HID])
        qbT = sbin(r_scope, "qbT", [P, 2, QR])
        kvbT = sbin(r_scope, "kvbT", [P, 4, KR])
        pr_out = sbin(r_scope, "pr_out", [P, 256 + HID])
        pr_hl = sbin(r_scope, "pr_hl", [P, 2, 256 + HID], F32R)
        r_scope.close()
        i_scope.close()
        h_scope = ExitStack()
        wq_h = sbin(h_scope, "wq_h", [P, 2, 384], F32R)
        wq_l = sbin(h_scope, "wq_l", [P, 2, 384], F32R)
        wuvo_h = sbin(h_scope, "wuvo_h", [P, HID], F32R)
        wuvo_l = sbin(h_scope, "wuvo_l", [P, HID], F32R)
        rop = sbin(h_scope, "rop", [P, 2, 2, 512])
        qc_h = [sbin(h_scope, f"qc_h{m}", [P, 2, S], F32R) for m in range(2)]
        qc_l = [sbin(h_scope, f"qc_l{m}", [P, 2, S], F32R) for m in range(2)]
        pm = sbin(h_scope, "pm", [P, 4, S])
        smx = sbin(h_scope, "smx", [P, 48])
        pTa_h = sbin(h_scope, "pTa_h", [P, 4, 512], F32R)
        pTa_l = sbin(h_scope, "pTa_l", [P, 4, 512], F32R)
        ol_half = sbin(h_scope, "ol_half", [P, 512])
        ol_f = sbin(h_scope, "ol_f", [P, 512])
        ol_h = sbin(h_scope, "ol_h", [P, S], F32R)
        ol_l = sbin(h_scope, "ol_l", [P, S], F32R)
        h_scope.close()
        l_scope.close()

        e_scope = ExitStack()
        lA_sb = sbin(e_scope, "lA_sb", [P, HID])
        lB_sb = sbin(e_scope, "lB_sb", [P, NK, P])
        lBT = sbin(e_scope, "lBT", [P, HID])
        lc_col = sbin(e_scope, "lc_col", [P, 1])
        lc2_col = sbin(e_scope, "lc2_col", [P, 1])
        lW_sb = sbin(e_scope, "lW_sb", [P, NK, HID])
        lWT = sbin(e_scope, "lWT", [P, NK, HID])
        wfin_f = sbin(e_scope, "wfin_f", [P, NK, HID])
        wfin_h = sbin(e_scope, "wfin_h", [P, NK, HID], F32R)
        wfin_l = sbin(e_scope, "wfin_l", [P, NK, HID], F32R)
        e_scope.close()

        def sems(prefix, names):
            return [sem(prefix + n) for n in names.split()]

        ld_x, ld_a, ld_l, ld_e = sems("ld_", "x a l e")
        ix_slot = sems("ix_", "ld0 ld1")
        ld_w, row_free = sems("ld_w", "0 1 2 3"), sem("row_free")
        consts, phase, st_out, passed = sem("consts"), sem("phase"), sem("st_out"), sem("passed")
        ln_xn, ln_tr, ln_hi, ln_lo = sems("ln_", "xn tr hi lo")
        rs_v, rs_s = sems("rs_", "v s")
        at_w, at_proj, at_q, at_qkv, at_v = sems("at_", "w proj q qkv v")
        at_s, at_max, at_exp, at_tr, at_hi, at_lo = sems("at_", "s max exp tr hi lo")
        at_o, at_ohi, at_ot, at_y, at_x = sems("at_", "o ohi ot y x")
        wt_d, wt_abs, wt_tot = sems("wt_", "d abs tot")
        ff_we, ff_tr, ff_hi, ff_lo = sems("ff_", "we tr hi lo")
        ff_gate, ff_up, ff_silu, ff_mul, ff_hhi, ff_h, ff_y, ff_x = sems("ff_", "gate up silu mul hhi h y x")
        lt_w, lt_mm, lt_ev, lt_norm, lt_tr, lt_hi, lt_lo = sems("lt_", "w mm ev norm tr hi lo")
        ix_ld, ix_wh, ix_w, ix_q, ix_qhi, ix_qlo, ix_s, ix_r, ix_acc, ix_mask = sems("ix_", "ld wh w q qhi qlo s r acc mask")
        pr_ldq, pr_ldo, pr_t, pr_tev, pr_mm, pr_ev, pr_z, pr_sp, pr_st = sems("pr_", "ldq ldo t tev mm ev z sp st")
        rp_ld, rp_sp, rp_st = sems("rp_", "ld sp st")
        hd_ldq, hd_ldu, hd_q, hd_rm, hd_rot = sems("hd_", "ldq ldu q rm rot")
        hd_qhi, hd_qlo, hd_qalo = sems("hd_", "qhi qlo qalo")
        hd_s, hd_max, hd_exp, hd_rec, hd_p, hd_tr, hd_hi, hd_lo = sems("hd_", "s max exp rec p tr hi lo")
        hd_o, hd_ocp, hd_of, hd_ohi, hd_olo = sems("hd_", "o ocp of ohi olo")
        hd_y, hd_x, hd_wz = sems("hd_", "y x wz")
        en_tb, en_tw, en_bt, en_wt, en_c, en_mm, en_w, en_y, en_o = sems("en_", "tb tw bt wt c mm w y o")

        block = ctx.enter_context(nc.Block())

        def meet(e, n):
            e.drain().then_inc(phase, 1)
            e.wait_ge(phase, 5 * n)

        def wait_apart(e, s, value):
            e.wait_ge(s, value)
            e.sem_inc(passed, 1)

        def f(ap):
            return ap.bitcast(F32)

        def mm3(pe, dst, lh, ll, rh, rl, start, stop):
            pe.matmul(dst, lh, rl, start=start, stop=False)
            pe.matmul(dst, ll, rh, start=False, stop=False)
            return pe.matmul(dst, lh, rh, start=False, stop=stop)

        def tile(t):
            return slice(t * P, (t + 1) * P)

        def xt(t):
            return x[:, t * HID:(t + 1) * HID]

        def two_banks(b, w=1024):
            return ps[:, b:b + 2, :].rearrange("p a n -> p (a n)")[:, 0:w]

        LATE, EARLY = (4, 5, 6, 7), (1, 2, 3)

        def index_tiles(step, late, par):
            if late:
                return step * 4, [(k, t, k % 2) for k, t in enumerate(LATE)]
            return IDXH * 4 + (step - IDXH) * 3, [(k, t, (k + par) % 2) for k, t in enumerate(EARLY)]

        def late_steps(e, work):
            with e.Fori(0, IDXH // 2 - 1) as q:
                work(2 * q, True, True, 0)
                work(2 * q + 1, True, True, 1)
            work(IDXH - 2, True, True, 0)
            work(IDXH - 1, True, False, 1)

        def early_steps(e, work):
            with e.Fori(0, IDXH // 2 - 1) as q:
                work(2 * q + IDXH, False, False, 0)
                work(2 * q + IDXH + 1, False, False, 1)
            work(2 * IDXH - 2, False, False, 0)
            work(2 * IDXH - 1, False, None, 1)

        def wt_chunk(chunk):
            m = min(chunk // NI, 2)
            return m, chunk - NI * m, 512 if m < 2 else 448

        def ring(chunk):
            slot, width = RING[chunk][0], wt_chunk(chunk)[2]
            return wring[:, slot, 0:width] if slot < 3 else row_bc[:, 0:width]

        def row(v, n, parts=P):
            return v.rearrange("(a n) -> a n", a=1).broadcast_to([parts, n])

        @block.sync
        def _(sp):
            for t in range(NT):
                sp.dma_start(xt(t), x_in[0, tile(t), :]).then_inc(ld_x, 16)
            sp.dma_start(base[2][:, 0:NK * 3 * D0].rearrange("p (k n) -> p k n", k=NK),
                         wqkv.rearrange("(k p) n -> p k n", p=P)).then_inc(ld_a, 16)
            sp.dma_start(base[2][:, 2048:2048 + HID], wo).then_inc(ld_a, 16)
            with nc.allow_non_contiguous_dma(reason="a small bias column"):
                sp.dma_start(bq_col[:], bqkv[0:2 * D0].rearrange("(a p) -> p a", p=P)).then_inc(ld_a, 16)
            sp.dma_start(bv_bc[:], row(bqkv[2 * D0:3 * D0], D0)).then_inc(ld_a, 16)
            sp.dma_start(row_bc[:], row(bo, HID)).then_inc(ld_a, 16)
            pairs = ((w1, m1), (w3, m3), (w2, m2))
            for chunk in range(WCHUNKS):
                m, s, width = wt_chunk(chunk)
                rows, mrows = (a.rearrange("(c p) n -> p c n", p=P) for a in pairs[m])
                dst = base[m][:, s * width:(s + 1) * width]
                slot = ring(chunk)
                if m < 2:
                    ws, ms = rows[:, s, :], mrows[:, s, :]
                else:
                    c = slice((s % 4) * 448, (s % 4) * 448 + 448)
                    ws, ms = rows[:, s // 4, c], mrows[:, s // 4, c]
                if chunk == 2 * NI:
                    sp.wait_ge(at_w, 1)
                number, last, _ = RING[chunk]
                if last is not None:
                    sp.wait_ge(wt_abs, last + 1)
                elif number == 3:
                    sp.wait_ge(row_free, 1)
                sp.dma_start(dst, ms).then_inc(ld_w[number], 16)
                sp.dma_start(slot, ws).then_inc(ld_w[number], 16)
            meet(sp, 1)
            rp_raw = row_bc[:, 0:256].rearrange("p (k n) -> p k n", k=2)
            with sp.Fori(0, PAIRS) as j:
                wait_apart(sp, rp_sp, j + 1)
                for a in range(2):
                    c = slice(a * ROPE, (a + 1) * ROPE)
                    src = ds(j * 2 * QKD + (1 - a) * QKD + NOPE, ROPE)
                    sp.dma_start(rp_raw[:, 0, c], qb[0:P, src]).then_inc(rp_ld, 16)
                    sp.dma_start(rp_raw[0:QR - P, 1, c], qb[P:QR, src]).then_inc(rp_ld, 16)
                wait_apart(sp, rp_sp, j + 2)
                for m in range(2):
                    cols = ds(j * 384 + P, 256)
                    sp.dma_start(wq_d[m, 0:P, cols], xn_t[:, m, 0:256]).then_inc(rp_st, 16)
                    sp.dma_start(wq_d[m, P:QR, cols], xn_t[0:QR - P, m, 256:512]).then_inc(rp_st, 16)
            sp.wait_ge(rp_st, 64 * PAIRS)
            meet(sp, 2)
            for k in range(NK):
                sp.dma_start(wlat_raw[:, k, 0:QR], qa[tile(k), :]).then_inc(ld_l, 16)
                sp.dma_start(wlat_raw[:, k, QR:QR + KR + ROPE], kva[tile(k), :]).then_inc(ld_l, 16)
                sp.dma_start(wlat_raw[:, k, QR + KR + ROPE:LATW], iww[tile(k), :]).then_inc(ld_l, 16)
            sp.dma_start(norm_bc[:, 0:QR], row(qan, QR)).then_inc(ld_l, 16)
            sp.dma_start(norm_bc[:, QR:QR + KR], row(kvan, KR)).then_inc(ld_l, 16)
            sp.dma_start(cosk[:], cos_k).then_inc(ld_l, 16)
            sp.dma_start(sink[:], sin_k).then_inc(ld_l, 16)
            sp.dma_start(cosq[:], cos_q).then_inc(ld_l, 16)
            sp.dma_start(sinq[:], sin_q).then_inc(ld_l, 16)
            def load_index(item, head, slot):
                wait_apart(sp, ix_w, item - 1)
                sp.dma_start(xn_t[:, slot, :].rearrange("p (k n) -> p k n", k=NK),
                             iwq.rearrange("(k p) n -> p k n", p=P)[:, :, ds(head * IDXD, IDXD)])\
                    .then_inc(ix_slot[slot], 16)

            def load_pair(j):
                wait_apart(sp, pr_t, 2 * j + 1)
                sp.dma_start(qb_raw[:, 0, :], qb[0:P, ds(j * 2 * QKD, 2 * QKD)]).then_inc(pr_ldq, 16)
                sp.dma_start(qb_raw[0:QR - P, 1, :], qb[P:QR, ds(j * 2 * QKD, 2 * QKD)]).then_inc(pr_ldq, 16)
                sp.dma_start(kvb_raw[:], kvb[:, ds(j * 512, 512)]).then_inc(pr_ldq, 16)
                wait_apart(sp, pr_mm, j + 1)
                sp.dma_start(ow_raw[:], ow[ds(j * 256, 256), :].rearrange("(a p) n -> p a n", p=P)).then_inc(pr_ldo, 16)

            sp.dma_start(iwq_raw[:], iwk.rearrange("(k p) n -> p k n", p=P)).then_inc(ix_ld, 16)
            sp.wait_ge(ln_lo, 3 * NT)
            with sp.Fori(0, IDXH // 2) as q:
                load_index(2 * q + 1, 2 * q, 1)
                load_index(2 * q + 2, 2 * q + 1, 0)
            load_index(17, 0, 1)
            load_index(18, 1, 0)
            load_pair(0)
            def store_pair(j):
                wait_apart(sp, pr_sp, j + 2)
                part = f(pr_hl[:])
                sp.dma_start(wq_d[:, 0:P, ds(j * 384, P)].rearrange("m p n -> p m n"), part[:, :, 0:P])\
                    .then_inc(pr_st, 16)
                sp.dma_start(wq_d[:, P:QR, ds(j * 384, P)].rearrange("m p n -> p m n"), part[0:QR - P, :, P:256])\
                    .then_inc(pr_st, 16)
                sp.dma_start(wuvo_d[:, ds(j * P, P), :].rearrange("m p n -> p m n"), part[:, :, 256:768])\
                    .then_inc(pr_st, 16)

            load_index(19, 2, 1)
            load_pair(1)

            def follow(b, slot):
                load_index(b + 19, b + 2, slot)
                store_pair(b - 1)
                load_pair(b + 1)

            with sp.Fori(0, IDXH // 2 - 2) as c:
                follow(2 * c + 1, 0)
                follow(2 * c + 2, 1)
            follow(IDXH - 3, 0)
            store_pair(PAIRS - 3)
            load_pair(PAIRS - 1)
            store_pair(PAIRS - 2)
            store_pair(PAIRS - 1)
            sp.wait_ge(pr_st, 48 * PAIRS + 1)
            meet(sp, 3)

            def load_wq(pair):
                for m, dst in enumerate((wq_h, wq_l)):
                    sp.dma_start(f(dst[:, 0, :]), wq_d[m, 0:P, ds(pair * 384, 384)]).then_inc(hd_ldq, 16)
                    sp.dma_start(f(dst[0:QR - P, 1, :]), wq_d[m, P:QR, ds(pair * 384, 384)]).then_inc(hd_ldq, 16)

            def load_wuvo(pair):
                for m, dst in enumerate((wuvo_h, wuvo_l)):
                    sp.dma_start(f(dst[:]), wuvo_d[m, ds(pair * P, P), :]).then_inc(hd_ldu, 16)

            load_wq(0)
            load_wuvo(0)
            wait_apart(sp, hd_q, 6)
            load_wq(1)
            with sp.Fori(1, PAIRS - 1) as j:
                wait_apart(sp, hd_q, 6 * j + 6)
                load_wq(j + 1)
                wait_apart(sp, hd_y, NT * j + 1)
                load_wuvo(j)
            wait_apart(sp, hd_y, NT * (PAIRS - 1) + 1)
            load_wuvo(PAIRS - 1)
            meet(sp, 4)
            sp.dma_start(lA_sb[:], lA.rearrange("n r d -> (n r) d")).then_inc(ld_e, 16)
            for k in range(NK):
                sp.dma_start(lB_sb[:, k, :].rearrange("p (n r) -> p n r", n=LORA_N),
                             lB[:, tile(k), :].rearrange("n p r -> p n r")).then_inc(ld_e, 16)
            for n in range(LORA_N):
                sp.dma_start(lc_col[n * LORA_R:(n + 1) * LORA_R, :], row(lcoef[n:n + 1], 1, LORA_R)).then_inc(ld_e, 16)
            sp.dma_start(lW_sb[:], lW.rearrange("(k p) n -> p k n", p=P)).then_inc(ld_e, 16)
            sp.dma_start(row_bc[:], row(lbias, HID)).then_inc(ld_e, 16)
            for t in range(NT):
                sp.wait_ge(en_o, t + 1)
                sp.dma_start(out[0, tile(t), :], xt(t)).then_inc(st_out, 16)
            sp.wait_ge(st_out, 16 * NT)

        @block.gpsimd
        def _(pool):
            pool.memset(ident[:], 0.0)
            pool.memset(ones[:], 1.0)
            pool.drain()
            pool.affine_select(out=ident[:], in_=ident[:], compare_op=ALU.not_equal, fill=1.0, base=0,
                               pattern=[[-1, P]], channel_multiplier=1)
            pool.drain().then_inc(consts, 1)
            for chunk in range(WCHUNKS):
                m, s, width = wt_chunk(chunk)
                slot = ring(chunk)
                pool.wait_ge(ld_w[RING[chunk][0]], 32 * (RING[chunk][2] + 1))
                pool.tensor_tensor(slot, slot, base[m][:, s * width:(s + 1) * width], ALU.subtract).then_inc(wt_d, 1)
            meet(pool, 1)
            rp_raw = row_bc[:, 0:256].rearrange("p (k n) -> p k n", k=2)
            rp_out = xn_t[:].rearrange("p m (k n) -> p m k n", k=2)
            pool.memset(row_bc[:], 0.0)
            pool.drain().then_inc(rp_sp, 1)
            with pool.Fori(0, PAIRS) as j:
                wait_apart(pool, rp_ld, 64 * j + 64)
                wait_apart(pool, rp_st, 64 * j)
                pool.tensor_copy(rp_out[:, 0, :, 0:P].bitcast(F32R), rp_raw[:])
                pool.drain()
                pool.tensor_tensor(rp_out[:, 1, :, 0:P].bitcast(F32R), rp_raw[:], rp_out[:, 0, :, 0:P], ALU.subtract)
                pool.drain()
                for m in range(2):
                    for k in range(2):
                        src = rp_out[:, m, k, 0:P].rearrange("p (i two) -> p i two", two=2)
                        dst = rp_out[:, m, k, P:256].rearrange("p (i two) -> p i two", two=2)
                        for o in range(2):
                            pool.tensor_copy(dst[:, :, o:o + 1], src[:, :, 1 - o:2 - o])
                pool.drain().then_inc(rp_sp, 1)
            meet(pool, 2)
            pool.memset(mbias[:, 0:P], 0.0)
            pool.drain()
            pool.affine_select(out=mbias[:, 0:P], in_=mbias[:, 0:P], compare_op=ALU.is_ge, fill=BIG, base=0,
                               pattern=[[-1, P]], channel_multiplier=1).then_inc(ix_mask, 1)

            def split_index():
                pool.tensor_copy(iwq_h[:], iwq_raw[:])
                pool.drain()
                pool.tensor_tensor(iwq_l[:], iwq_raw[:], f(iwq_h[:]), ALU.subtract).then_inc(ix_w, 1)

            def index_weights_lo(item, slot):
                wait_apart(pool, ix_wh, item)
                pool.tensor_tensor(iwq_l[:], xn_t[:, slot, :].rearrange("p (k n) -> p k n", k=NK), f(iwq_h[:]),
                                   ALU.subtract).then_inc(ix_w, 1)

            def drop_later(tiles):
                for t in tiles:
                    d = acc[:, TRI[t] - P + t * P:TRI[t] + t * P]
                    pool.affine_select(out=d, in_=d, compare_op=ALU.is_ge, fill=FUTURE, base=0,
                                       pattern=[[-1, P]], channel_multiplier=1).then_inc(ix_mask, 1)

            def split_pair(j):
                wait_apart(pool, pr_ev, j + 2)
                pool.tensor_tensor(pr_hl[:, 1, :], pr_out[:], f(pr_hl[:, 0, :]), ALU.subtract)
                pool.drain().then_inc(pr_sp, 1)

            pool.wait_ge(ix_ld, 16)
            split_index()
            pool.drain()
            with pool.Fori(0, IDXH // 2 + 1) as q:
                index_weights_lo(2 * q + 1, 1)
                index_weights_lo(2 * q + 2, 0)
            pool.wait_ge(ix_acc, 4 * IDXH + 1)
            drop_later(LATE)
            pool.wait_ge(lt_lo, NT)
            pool.memset(pr_out[:], 0.0)
            pool.drain().then_inc(pr_z, 1)
            with pool.Fori(0, IDXH // 2 - 1) as c:
                index_weights_lo(2 * c + 19, 1)
                split_pair(2 * c)
                index_weights_lo(2 * c + 20, 0)
                split_pair(2 * c + 1)
            split_pair(PAIRS - 2)
            split_pair(PAIRS - 1)
            pool.wait_ge(ix_acc, 7 * IDXH + 1)
            drop_later(EARLY)
            meet(pool, 3)

            pool.memset(f(wq_h[QR - P:P, 1, :]), 0.0)
            pool.memset(f(wq_l[QR - P:P, 1, :]), 0.0)
            pool.drain().then_inc(hd_wz, 1)

            def pair_work(j, par, last, order=POOL_ORDER):
                for kind, i, p in steps(order, j, last):
                    if kind == "S":
                        w = (i % NT + 1) * P
                        wait_apart(pool, hd_rec, 16 * p + i + 1)
                        pool.tensor_scalar(pm[:, i % 4, 0:w], pm[:, i % 4, 0:w], smx[:, 32 + i:33 + i], 0.0,
                                           ALU.mult, ALU.add).then_inc(hd_p, 1)
                    elif kind == "G":
                        wait_apart(pool, hd_rm, 4 * p + 2 * i + 2)
                        pool.tensor_tensor(rop[:, i, 0, :], rop[:, i, 0, :], rop[:, i, 1, :], ALU.add)
                        pool.drain().then_inc(hd_rot, 1)
                    else:
                        c = slice(512 * i, 512 * i + 512)
                        qh, ql = qc_h[1 - par], qc_l[1 - par]
                        pool.drain()
                        wait_apart(pool, hd_qhi, 4 * p + 2 * i + 2)
                        pool.tensor_tensor(ql[KR:P, 0, c], rop[KR:P, i, 0, :], f(qh[KR:P, 0, c]), ALU.subtract)
                        pool.tensor_tensor(ql[0:KR, 1, c], rop[0:KR, i, 0, :], f(qh[0:KR, 1, c]), ALU.subtract)
                        pool.drain().then_inc(hd_qlo, 1)

            pair_work(-1, 1, False, "G0 R0 G1 R1 S16 S17 S18 S19")
            with pool.Fori(0, PAIRS // 2 - 1) as q:
                pair_work(2 * q, 0, False)
                pair_work(2 * q + 1, 1, False)
            pair_work(PAIRS - 2, 0, False)
            pair_work(PAIRS - 1, 1, True)
            meet(pool, 4)

        @block.scalar
        def _(act):
            COPY = ACT.Copy

            def sqrt(k, n):
                act.wait_ge(rs_v, k + 1)
                act.activation(rs_sqrt[:, 0:n], rs_var[:, 0:n], ACT.Sqrt).then_inc(rs_s, 1)

            def norm_hi(l, after=None):
                for t in range(NT):
                    act.wait_ge(ln_tr, NT * l + t + 1)
                    act.activation(xn_h[:, :, tile(t)], ps[:, t % 2, :].rearrange("p (k s) -> p k s", k=NK),
                                   COPY).then_inc(ln_hi, 1)
                    if after and t >= 1:
                        after()

            chunks = list(range(WCHUNKS))

            def weight_chunk():
                if not chunks:
                    return
                chunk = chunks.pop(0)
                m, s, width = wt_chunk(chunk)
                slot = ring(chunk)
                act.wait_ge(wt_d, chunk + 1)
                act.activation(sgn[m][:, s * width:(s + 1) * width], slot, ACT.Sign)
                act.drain()
                act.activation(slot, slot, ACT.Abs, accum_out=absum[:, chunk:chunk + 1])
                act.drain().then_inc(wt_abs, 1)

            sqrt(0, NT)
            norm_hi(0, weight_chunk)
            for u in range(4):
                act.wait_ge(at_proj, u + 1)
                if u >= 2:
                    act.wait_ge(at_qkv, u - 1)
                act.activation(xn_t[:, u % 2, :], ps[:, u, :], ACT.Identity,
                               bias=bq_col[:, u // 2:u // 2 + 1]).then_inc(at_q, 1)
                weight_chunk()
            for _ in range(6):
                weight_chunk()
            for kind, i in ATT_ORDER:
                if kind == "S":
                    act.wait_ge(at_max, i + 1)
                    act.activation(p0[:, i % 3, :], two_banks(2 * (i % 2)), ACT.Exp,
                                   bias=sm0[:, NT + i:NT + i + 1], scale=float(D0) ** -0.5,
                                   accum_out=sm0[:, 2 * NT + i:2 * NT + i + 1])
                    act.drain().then_inc(at_exp, 1)
                    weight_chunk()
                elif kind == "T":
                    for c in range(2):
                        act.wait_ge(at_tr, 2 * i + c + 1)
                        act.activation(pTx_h[:, 4 * c:4 * c + 4, tile(i % 4)],
                                       ps[:, 4 + c, :].rearrange("p (k s) -> p k s", k=4), COPY).then_inc(at_hi, 1)
                    weight_chunk()
                elif kind == "O":
                    act.wait_ge(at_o, i + 1)
                    act.activation(oT[:, 0, :], ps[:, 6, :], COPY).then_inc(at_ohi, 1)
                else:
                    weight_chunk()
            sqrt(1, NT)
            norm_hi(1, weight_chunk)
            while chunks:
                weight_chunk()
            act.drain().then_inc(wt_tot, 1)
            meet(act, 1)

            def weight_hi(g, par, k):
                act.wait_ge(ff_tr, 3 * g + k + 1)
                act.activation(wc_h[:, par, k, :], ps[:, 6 + (3 * par + k) % 2, :], COPY).then_inc(ff_hi, 1)

            with act.Fori(0, 2) as half:
                for k in range(3):
                    weight_hi(half * NI, 0, k)

                def step(s, par, last=False):
                    g = half * NI + s
                    if not last:
                        weight_hi(g + 1, 1 - par, 0)
                        weight_hi(g + 1, 1 - par, 1)
                    act.wait_ge(ff_gate, g + 1)
                    act.wait_ge(ff_mul, g + 1)
                    act.activation(silu[:], ps[:, 4, :], ACT.Silu).then_inc(ff_silu, 1)
                    act.wait_ge(ff_mul, g + 2)
                    act.activation(hT_h[:, par, :], hf[:], COPY).then_inc(ff_hhi, 1)
                    if not last:
                        weight_hi(g + 1, 1 - par, 2)

                with act.Fori(0, NI - 2, 2) as s:
                    step(s, 0)
                    step(s + 1, 1)
                step(NI - 2, 0)
                step(NI - 1, 1, last=True)
            meet(act, 2)
            sqrt(2, NT)
            norm_hi(2)
            for t in range(NT):
                act.wait_ge(lt_mm, t + 1)
                act.activation(lat[:, t, :], ps[:, 2 + t % 2, 0:LATW], COPY).then_inc(lt_ev, 1)
            sqrt(3, 16)
            for t in range(NT):
                act.wait_ge(lt_tr, t + 1)
                src = ps[:, 4 + t % 2, :]
                act.activation(latT_h[:, 0, tile(t)], src[:, 0:P], COPY)
                act.activation(latT_h[0:QR - P, 1, tile(t)], ps[0:QR - P, 4 + t % 2, P:2 * P], COPY)
                act.activation(latT_h[:, 2:4, tile(t)], src[:, 2 * P:4 * P].rearrange("p (k s) -> p k s", k=2), COPY)
                act.drain().then_inc(lt_hi, 1)
            for b in range(2):
                act.wait_ge(ix_q, b + 1)
                act.activation(ikT_h[:, b * 512:(b + 1) * 512], ps[:, b, :], COPY).then_inc(ix_qhi, 1)

            def index_hi(step, par):
                act.wait_ge(ix_q, step + 3)
                act.activation(iqT_h[:, par, :], ps[:, par, :], COPY).then_inc(ix_qhi, 1)

            def index_weights_hi(item, slot, loads):
                act.wait_ge(ix_slot[slot], 16 * loads)
                wait_apart(act, ix_q, item + 1)
                wait_apart(act, ix_w, item)
                act.activation(iwq_h[:], xn_t[:, slot, :].rearrange("p (k n) -> p k n", k=NK), COPY)\
                    .then_inc(ix_wh, 1)

            def index_relu(step, late, par):
                base_tile, tiles = index_tiles(step, late, par)
                for k, t, slot in tiles:
                    w = (t + 1) * P
                    act.wait_ge(ix_s, base_tile + k + 1)
                    act.wait_ge(ix_acc, base_tile + k)
                    act.activation(relu[:, slot, 0:w], two_banks(2 + 2 * slot, w), ACT.Relu).then_inc(ix_r, 1)

            def late_work(step, late, late_next, par):
                index_hi(step + 1, 1 - par)
                index_weights_hi(step + 3, 1 - par, (step - par) // 2 + 2)
                index_relu(step, late, par)

            def early_work(step, late, late_next, par):
                j = step - IDXH
                if late_next is not None:
                    index_hi(step + 1, 1 - par)
                if not isinstance(step, int):
                    index_weights_hi(step + 3, 1 - par, (step - par) // 2 + 2)
                act.wait_ge(pr_t, 2 * j + 2)
                act.activation(kvbT[:].rearrange("p a n -> p (a n)"), ps[:, 6, 0:4 * KR], COPY).then_inc(pr_tev, 1)
                act.wait_ge(pr_t, 2 * j + 3)
                act.activation(qbT[:].rearrange("p a n -> p (a n)"), ps[:, 7, 0:2 * QR], COPY).then_inc(pr_tev, 1)
                index_relu(step, late, par)
                act.wait_ge(pr_mm, j + 2)
                act.wait_ge(pr_sp, j + 1)
                act.wait_ge(pr_st, 48 * j + 1)
                act.activation(pr_out[:, 0:P], ps[:, 6, 256:384], COPY, scale=-float(QKD) ** -0.5)
                act.activation(pr_out[0:QR - P, P:256], ps[0:QR - P, 6, 384:512], COPY, scale=-float(QKD) ** -0.5)
                act.activation(pr_out[:, 256:768], ps[:, 7, :], COPY)
                act.drain()
                act.activation(pr_hl[:, 0, :], pr_out[:], COPY)
                act.drain().then_inc(pr_ev, 1)

            index_weights_hi(1, 1, 1)
            index_hi(0, 0)
            index_weights_hi(2, 0, 1)
            late_steps(act, late_work)
            act.wait_ge(pr_z, 1)
            early_steps(act, early_work)
            meet(act, 3)

            def pair_work(j, par, last, order=ACT_ORDER):
                for kind, i, p in steps(order, j, last):
                    if kind == "S":
                        w = (i % NT + 1) * P
                        act.wait_ge(hd_max, 16 * p + i + 1)
                        act.activation(pm[:, i % 4, 0:w], pm[:, i % 4, 0:w], ACT.Exp, bias=smx[:, i:i + 1],
                                       scale=-1.0, accum_out=smx[:, 16 + i:17 + i])
                        act.drain().then_inc(hd_exp, 1)
                    elif kind == "T":
                        t = i % NT
                        dst = pTa_h[:] if t < 4 else pTx_h
                        for c, g in GROUPS[i]:
                            nk = min(4, t + 1 - 4 * c)
                            act.wait_ge(hd_tr, NG * p + g + 1)
                            act.activation(dst[:, 4 * c:4 * c + nk, tile(t % 4)],
                                           ps[:, 4 + g % 2, 0:nk * P].rearrange("p (k s) -> p k s", k=nk),
                                           COPY).then_inc(hd_hi, 1)
                    elif kind == "V":
                        h, b = divmod(i, 2)
                        mine, other = slice(KR * h, KR * h + KR), slice(KR * (1 - h), KR * (1 - h) + KR)
                        act.wait_ge(hd_o, 4 * p + i + 1)
                        act.activation(ol_half[mine, :], ps[other, 6, :], COPY).then_inc(hd_ocp, 1)
                    elif kind == "W":
                        h, b = divmod(i, 2)
                        mine = slice(KR * h, KR * h + KR)
                        act.wait_ge(hd_of, 4 * p + i + 2)
                        act.activation(ol_h[mine, 512 * b:512 * b + 512], ol_f[mine, :], COPY).then_inc(hd_ohi, 1)
                    elif kind == "Q":
                        n, bank = i // 3, Q_BANKS[i]
                        c = slice(512 * n, 512 * n + 512)
                        act.wait_ge(hd_q, 6 * p + i + 1)
                        act.activation(qc_h[1 - par][0:KR, 0, c], ps[0:KR, bank, :], COPY)
                        act.activation(qc_h[1 - par][KR:P, 1, c], ps[KR:P, bank, :], COPY).then_inc(hd_qhi, 1)
                    else:
                        c = slice(512 * i, 512 * i + 512)
                        act.wait_ge(hd_rot, 2 * p + i + 1)
                        act.activation(qc_h[1 - par][KR:P, 0, c], rop[KR:P, i, 0, :], COPY)
                        act.activation(qc_h[1 - par][0:KR, 1, c], rop[0:KR, i, 0, :], COPY).then_inc(hd_qhi, 1)

            pair_work(-1, 1, False, "Q2 R0 Q5 R1 S16 S17 S18 S19")
            with act.Fori(0, PAIRS // 2 - 1) as q:
                pair_work(2 * q, 0, False)
                pair_work(2 * q + 1, 1, False)
            pair_work(PAIRS - 2, 0, False)
            pair_work(PAIRS - 1, 1, True)
            meet(act, 4)
            sqrt(4, NT)
            norm_hi(3)
            act.wait_ge(en_tb, 1)
            act.wait_ge(en_c, 1)
            act.activation(lBT[:], ps[:, 0, :], ACT.Identity, scale=lc2_col[:]).then_inc(en_bt, 1)
            for k in range(NK):
                act.wait_ge(en_tw, k + 1)
                act.activation(lWT[:, k, :], ps[:, 1 + k, :], COPY).then_inc(en_wt, 1)

        @block.vector
        def _(dve):
            dve.drain().then_inc(ff_lo, 2)
            dve.drain().then_inc(ff_mul, 1)
            dve.drain().then_inc(ff_x, 1)
            dve.drain().then_inc(ix_acc, 1)
            dve.drain().then_inc(hd_lo, 2)
            dve.drain().then_inc(hd_of, 1)
            dve.drain().then_inc(hd_x, NT)

            def rsqrt(k, n):
                v, r, q = rs_var[:, 0:n], rs_out[:, 0:n], rs_tmp[:, 0:n]
                dve.drain().then_inc(rs_v, 1)
                dve.wait_ge(rs_s, k + 1)
                dve.reciprocal(r, rs_sqrt[:, 0:n])
                dve.drain()
                dve.tensor_tensor(q, r, r, ALU.mult)
                dve.drain()
                dve.tensor_tensor(q, q, v, ALU.mult)
                dve.drain()
                dve.tensor_scalar(q, q, -0.5, 1.5, ALU.mult, ALU.add)
                dve.drain()
                dve.tensor_tensor(r, r, q, ALU.mult)
                dve.drain()

            def split(hi, lo, src):
                dve.tensor_copy(hi, src)
                dve.drain()
                return dve.tensor_tensor(lo, src, f(hi), ALU.subtract)

            def norm(l, k):
                for t in range(NT if l < 3 else 0):
                    if l == 0:
                        dve.wait_ge(ld_x, 16 * NT)
                    dve.bn_stats(stats[:, 6 * t:6 * t + 6], xt(t))
                dve.drain()
                for t in range(NT):
                    dve.bn_aggr(mv[:, t, :], stats[:, 6 * t:6 * t + 6])
                dve.drain()
                dve.tensor_scalar(rs_var[:, 0:NT], mv[:, :, 1], EPS, None, ALU.add)
                rsqrt(k, NT)

                def lo(t):
                    dve.wait_ge(ln_hi, NT * l + t + 1)
                    dve.tensor_tensor(xn_l[:, :, tile(t)], ps[:, t % 2, :].rearrange("p (k s) -> p k s", k=NK),
                                      f(xn_h[:, :, tile(t)]), ALU.subtract).then_inc(ln_lo, 1)

                for t in range(NT):
                    if t >= 2:
                        dve.wait_ge(ln_tr, NT * l + t - 1)
                    dve.tensor_scalar(xn_t[:, t % 2, :], xt(t), mv[:, t, 0:1], rs_out[:, t:t + 1],
                                      ALU.subtract, ALU.mult).then_inc(ln_xn, 1)
                    if t >= 1:
                        lo(t - 1)
                lo(NT - 1)
                dve.drain()

            norm(0, 0)
            dve.wait_ge(ld_a, 80)
            raw = base[2][:, 0:NK * 3 * D0].rearrange("p (k n) -> p k n", k=NK)
            split(wqkv_h[:], wqkv_l[:], raw)
            split(wo_h[:], wo_l[:], base[2][:, 2048:2048 + HID])
            dve.drain().then_inc(at_w, 1)
            for t in range(NT):
                dve.tensor_tensor(xt(t), xt(t), row_bc[:], ALU.add)
            dve.drain().then_inc(row_free, 1)
            for u in range(4):
                m, n = divmod(u, 2)
                c = slice(512 * n, 512 * n + 512)
                dve.wait_ge(at_q, u + 1)
                split(qkT_h[:, m, c], qkT_l[:, m, c], xn_t[:, u % 2, :])
                dve.drain().then_inc(at_qkv, 1)
            for b in range(2):
                dve.wait_ge(at_proj, 5 + b)
                tmp = xn_t[:, b, :].rearrange("p (k s) -> p k s", k=4)
                for i in range(4):
                    dve.tensor_tensor(tmp[:, i, :], ps[:, 4 + b, tile(i)], bv_bc[:], ALU.add)
                dve.drain()
                split(v_h[:, 4 * b:4 * b + 4, :], v_l[:, 4 * b:4 * b + 4, :], tmp)
                dve.drain().then_inc(at_v, 1)
            for kind, i in ATT_ORDER:
                if kind == "S":
                    dve.wait_ge(at_s, i + 1)
                    dve.tensor_reduce(sm0[:, i:i + 1], two_banks(2 * (i % 2)), AXX, ALU.max)
                    dve.drain()
                    dve.tensor_scalar(sm0[:, NT + i:NT + i + 1], sm0[:, i:i + 1], -float(D0) ** -0.5, None, ALU.mult)\
                        .then_inc(at_max, 1)
                elif kind == "T":
                    for c in range(2):
                        dve.wait_ge(at_hi, 2 * i + c + 1)
                        dst = (slice(None), slice(4 * c, 4 * c + 4), tile(i % 4))
                        dve.tensor_tensor(pTx_l[dst], ps[:, 4 + c, :].rearrange("p (k s) -> p k s", k=4),
                                          f(pTx_h[dst]), ALU.subtract).then_inc(at_lo, 1)
                elif kind == "O":
                    dve.wait_ge(at_ohi, i + 1)
                    dve.tensor_tensor(oT[:, 1, :], ps[:, 6, :], f(oT[:, 0, :]), ALU.subtract).then_inc(at_ot, 1)
                    dve.reciprocal(sm0[:, 3 * NT + 4 * i:3 * NT + 4 * i + 4], sm0[:, 2 * NT + 4 * i:2 * NT + 4 * i + 4])
                    dve.drain()
                else:
                    dve.wait_ge(at_y, i + 1)
                    dve.scalar_tensor_tensor(xt(i), ps[:, 7 - i % 2, :], sm0[:, 3 * NT + i:3 * NT + i + 1], xt(i),
                                             ALU.mult, ALU.add).then_inc(at_x, 1)
            dve.drain()
            norm(1, 1)
            dve.wait_ge(wt_tot, 2)
            for m, (a, b) in enumerate(((0, NI), (NI, 2 * NI), (2 * NI, WCHUNKS))):
                dve.tensor_reduce(coef[:, m:m + 1], ps[:, 7, a:b], AXX, ALU.add)
            dve.drain()
            dve.tensor_scalar(coef[:], coef[:], 1.0 / (INTER * HID), None, ALU.mult)
            meet(dve, 1)

            def effective(s, k):
                dst = weff[:, k, :]
                if k < 2:
                    sg, bs = sgn[k][:, ds(s * 512, 512)], base[k][:, ds(s * 512, 512)]
                else:
                    sg, bs = (a[:].rearrange("p (c n) -> p c n", c=NK)[:, :, ds(s * P, P)]
                              for a in (sgn[2], base[2]))
                    dst = dst.rearrange("p (c n) -> p c n", c=NK)
                dve.scalar_tensor_tensor(dst, sg, coef[:, k:k + 1], bs, ALU.mult, ALU.add).then_inc(ff_we, 1)

            def weight_lo(g, par, k):
                dve.wait_ge(ff_hi, 3 * g + k + 1)
                dve.tensor_tensor(wc_l[:, par, k, :], ps[:, 6 + (3 * par + k) % 2, :], f(wc_h[:, par, k, :]),
                                  ALU.subtract).then_inc(ff_lo, 1)

            with dve.Fori(0, 2) as half:
                for k in range(3):
                    effective(0, k)
                for k in range(3):
                    weight_lo(half * NI, 0, k)
                    effective(1, k)

                def step(s, par, ahead=True, last=False):
                    g = half * NI + s
                    for k in range(0 if last else 2):
                        weight_lo(g + 1, 1 - par, k)
                        if ahead:
                            effective(s + 2, k)
                    dve.wait_ge(ff_silu, g + 1)
                    dve.wait_ge(ff_up, g + 1)
                    dve.tensor_tensor(hf[:], ps[:, 5, :], silu[:], ALU.mult).then_inc(ff_mul, 1)
                    dve.drain()
                    dve.wait_ge(ff_hhi, g + 1)
                    dve.tensor_tensor(hT_l[:, par, :], hf[:], f(hT_h[:, par, :]), ALU.subtract).then_inc(ff_h, 1)
                    dve.drain()
                    if not last:
                        weight_lo(g + 1, 1 - par, 2)
                        if ahead:
                            effective(s + 2, 2)

                with dve.Fori(0, (NI - 2) // 2) as q:
                    step(2 * q, 0)
                    step(2 * q + 1, 1)
                step(NI - 2, 0, ahead=False)
                step(NI - 1, 1, last=True)
                for i in range(4):
                    xs = x[:, ds((half * 4 + i) * HID, HID)]
                    dve.wait_ge(ff_y, 4 * half + i + 1)
                    dve.tensor_tensor(xs, xs, ps[:, i, :], ALU.add).then_inc(ff_x, 1)
                dve.drain()
            meet(dve, 2)
            norm(2, 2)
            dve.memset(f(latT_h[QR - P:P, 1, :]), 0.0)
            dve.memset(f(latT_l[QR - P:P, 1, :]), 0.0)
            dve.memset(acc[:], 0.0)
            dve.wait_ge(ld_l, 16 * 18)
            split(wlat_h[:], wlat_l[:], wlat_raw[:])
            dve.drain().then_inc(lt_w, 1)
            dve.wait_ge(lt_ev, NT)
            for c, (a, w) in enumerate(((0, QR), (QR, KR))):
                sq = lat_sq[:, :, 0:w]
                dve.tensor_tensor(sq, lat[:, :, a:a + w], lat[:, :, a:a + w], ALU.mult)
                dve.drain()
                dve.tensor_reduce(rs_var[:, NT * c:NT * c + NT], sq, AXX, ALU.add)
                dve.drain()
                dve.tensor_scalar(rs_var[:, NT * c:NT * c + NT], rs_var[:, NT * c:NT * c + NT], 1.0 / w, EPS,
                                  ALU.mult, ALU.add)
                dve.drain()
            rsqrt(3, 16)
            for t in range(NT):
                for c, (a, w) in enumerate(((0, QR), (QR, KR))):
                    dve.scalar_tensor_tensor(latn[:, t, a:a + w], lat[:, t, a:a + w],
                                             rs_out[:, NT * c + t:NT * c + t + 1], norm_bc[:, a:a + w],
                                             ALU.mult, ALU.mult)
            kp = lat[:, :, QR + KR:QR + KR + ROPE].rearrange("p t (i two) -> p t i two", two=2)
            ko = latn[:, :, QR + KR:QR + KR + ROPE].rearrange("p t (i two) -> p t i two", two=2)
            for o in range(2):
                own, partner = kp[:, :, :, o], kp[:, :, :, 1 - o]
                dve.tensor_tensor(rope_t[:, 0], own, cosk[:], ALU.mult)
                dve.tensor_tensor(rope_t[:, 1], partner, sink[:], ALU.mult)
                dve.drain()
                dve.tensor_tensor(ko[:, :, :, o], rope_t[:, 0], rope_t[:, 1], ALU.add if o else ALU.subtract)
                dve.drain()
            lv = latn[:, :, QR:QR + KR]
            dve.tensor_copy(latn[:, :, QR + KR + ROPE:384], lv)
            dve.tensor_copy(v3[:, :, 0:KR], lv)
            dve.tensor_copy(v3[:, :, 2 * KR:3 * KR], lv)
            dve.drain()
            dve.tensor_tensor(v3[:, :, KR:2 * KR], lv, f(v3[:, :, 0:KR]), ALU.subtract)
            dve.tensor_scalar(iw[:], lat[:, :, QR + KR + ROPE:LATW], float(IDXH) ** -0.5 * float(IDXD) ** -0.5, None,
                              ALU.mult)
            dve.drain().then_inc(lt_norm, 1)
            for t in range(NT):
                dve.wait_ge(lt_hi, t + 1)
                src = ps[:, 4 + t % 2, :]
                dve.tensor_tensor(latT_l[:, 0, tile(t)], src[:, 0:P], f(latT_h[:, 0, tile(t)]), ALU.subtract)
                dve.tensor_tensor(latT_l[0:QR - P, 1, tile(t)], ps[0:QR - P, 4 + t % 2, P:2 * P],
                                  f(latT_h[0:QR - P, 1, tile(t)]), ALU.subtract)
                dve.tensor_tensor(latT_l[:, 2:4, tile(t)], src[:, 2 * P:4 * P].rearrange("p (k s) -> p k s", k=2),
                                  f(latT_h[:, 2:4, tile(t)]), ALU.subtract)
                dve.drain().then_inc(lt_lo, 1)

            for b in range(2):
                c = slice(512 * b, 512 * b + 512)
                dve.wait_ge(ix_qhi, b + 1)
                dve.tensor_tensor(ikT_l[:, c], ps[:, b, :], f(ikT_h[:, c]), ALU.subtract).then_inc(ix_qlo, 1)

            def index_lo(step, par):
                dve.wait_ge(ix_qhi, step + 3)
                dve.tensor_tensor(iqT_l[:, par, :], ps[:, par, :], f(iqT_h[:, par, :]), ALU.subtract)\
                    .then_inc(ix_qlo, 1)

            def index_work(step, late, late_next, par):
                if late_next is not None:
                    index_lo(step + 1, 1 - par)
                base_tile, tiles = index_tiles(step, late, par)
                for k, t, slot in tiles:
                    w = (t + 1) * P
                    at = acc[:, TRI[t] - P:TRI[t] - P + w]
                    dve.wait_ge(ix_r, base_tile + k + 2)
                    head = step if late else step - IDXH
                    dve.scalar_tensor_tensor(at, relu[:, slot, 0:w], iw[:, t, ds(head, 1)], at, ALU.mult, ALU.add)\
                        .then_inc(ix_acc, 1)
                dve.drain()

            def topk_round(tiles):
                for k, t in enumerate(tiles):
                    dve.max(top8[:, k, :], acc[:, TRI[t] - P:TRI[t + 1] - P])
                dve.drain()
                for k, t in enumerate(tiles):
                    at = acc[:, TRI[t] - P:TRI[t + 1] - P]
                    dve.match_replace(at, top8[:, k, :], at, TAKEN)
                dve.drain()

            def topk_mask(tiles):
                for t in tiles:
                    dve.tensor_scalar(mbias[:, TRI[t]:TRI[t + 1]], acc[:, TRI[t] - P:TRI[t + 1] - P],
                                      TAKEN, BIG, ALU.not_equal, ALU.mult)

            def early_work(step, late, late_next, par):
                index_work(step, late, late_next, par)
                topk_round(LATE)

            index_lo(0, 0)
            late_steps(dve, index_work)
            dve.wait_ge(ix_mask, 1 + len(LATE))
            early_steps(dve, early_work)
            topk_mask(LATE)
            dve.wait_ge(ix_mask, NT)
            with dve.Fori(0, TOPK // 32):
                for _ in range(4):
                    topk_round(EARLY)
            topk_mask(EARLY)
            meet(dve, 3)

            def reciprocal(count, i):
                dve.wait_ge(hd_exp, count)
                dve.reciprocal(smx[:, 32 + i:33 + i], smx[:, 16 + i:17 + i]).then_inc(hd_rec, 1)

            def pair_work(j, par, last, order=DVE_ORDER):
                for kind, i, p in steps(order, j, last):
                    if kind == "S":
                        t = i % NT
                        w = (t + 1) * P
                        if i >= 4:
                            dve.wait_ge(hd_tr, NG * p + GROUPS[i - 4][-1][1] + 1)
                        wait_apart(dve, hd_s, 16 * p + i + 1)
                        dve.tensor_tensor_reduce(out=pm[:, i % 4, 0:w], in0=two_banks(2 * (i % 2), w),
                                                 in1=mbias[:, TRI[t]:TRI[t + 1]], scale=1.0, scalar=3.0 * BIG,
                                                 op0=ALU.add, op1=ALU.min, accum_out=smx[:, i:i + 1])
                        dve.drain().then_inc(hd_max, 1)
                    elif kind == "C":
                        reciprocal(16 * p + i + 1, i)
                    elif kind == "T":
                        t = i % NT
                        dh, dl = (pTa_h[:], pTa_l[:]) if t < 4 else (pTx_h, pTx_l)
                        for c, g in GROUPS[i]:
                            nk = min(4, t + 1 - 4 * c)
                            at = (slice(None), slice(4 * c, 4 * c + nk), tile(t % 4))
                            dve.wait_ge(hd_hi, NG * p + g + 1)
                            dve.tensor_tensor(dl[at], ps[:, 4 + g % 2, 0:nk * P].rearrange("p (k s) -> p k s", k=nk),
                                              f(dh[at]), ALU.subtract).then_inc(hd_lo, 1)
                    elif kind == "V":
                        h, b = divmod(i, 2)
                        r, c = slice(KR * h, KR * h + KR), slice(512 * b, 512 * b + 512)
                        dve.wait_ge(hd_ocp, 4 * p + i + 1)
                        dve.tensor_tensor(ol_f[r, :], ps[r, 6, :], ol_half[r, :], ALU.add)
                        dve.drain().then_inc(hd_of, 1)
                    elif kind == "W":
                        h, b = divmod(i, 2)
                        r, c = slice(KR * h, KR * h + KR), slice(512 * b, 512 * b + 512)
                        dve.wait_ge(hd_ohi, 4 * p + i + 1)
                        dve.tensor_tensor(ol_l[r, c], ol_f[r, :], f(ol_h[r, c]), ALU.subtract).then_inc(hd_olo, 1)
                        dve.drain()
                    elif kind == "Q":
                        (n, piece), bank = divmod(i, 3), Q_BANKS[i]
                        c = slice(512 * n, 512 * n + 512)
                        if piece < 2:
                            dve.wait_ge(hd_q, 6 * p + i + 1)
                            dve.tensor_tensor(rop[:, n, piece, :], ps[:, bank, :], (cosq, sinq)[piece][:, c], ALU.mult)\
                                .then_inc(hd_rm, 1)
                        else:
                            qh, ql = qc_h[1 - par], qc_l[1 - par]
                            dve.wait_ge(hd_qhi, 4 * p + (1 if n == 0 else 3))
                            dve.tensor_tensor(ql[0:KR, 0, c], ps[0:KR, bank, :], f(qh[0:KR, 0, c]), ALU.subtract)
                            dve.tensor_tensor(ql[KR:P, 1, c], ps[KR:P, bank, :], f(qh[KR:P, 1, c]), ALU.subtract)\
                                .then_inc(hd_qalo, 1)
                    else:
                        dve.wait_ge(hd_y, NT * p + i + 2)
                        dve.tensor_tensor(xt(i), xt(i), ps[:, Y_BANKS[i], :], ALU.add).then_inc(hd_x, 1)
                        if last:
                            dve.drain()
                            dve.bn_stats(stats[:, 6 * i:6 * i + 6], xt(i))
                dve.drain()

            pair_work(-1, 1, False, "Q0 Q1 Q2 Q3 Q4 Q5 S16 S17 C16 S18 C17 S19 C18")
            with dve.Fori(0, PAIRS // 2 - 1) as q:
                pair_work(2 * q, 0, False)
                pair_work(2 * q + 1, 1, False)
            pair_work(PAIRS - 2, 0, False)
            pair_work(PAIRS - 1, 1, True)
            meet(dve, 4)
            norm(3, 4)
            dve.wait_ge(ld_e, 16 * (3 + NK + LORA_N))
            dve.tensor_scalar(lc2_col[:], lc_col[:], LORA_SCALE, None, ALU.mult).then_inc(en_c, 1)
            for t in range(NT):
                dve.tensor_tensor(xt(t), xt(t), row_bc[:], ALU.add)
            for k in range(NK):
                dve.wait_ge(en_wt, k + 1)
                dve.wait_ge(en_mm, k + 1)
                dve.tensor_tensor(wfin_f[:, k, :], ps[:, (5, 6, 7, 0)[k], :], lWT[:, k, :], ALU.add)
                dve.drain()
                split(wfin_h[:, k, :], wfin_l[:, k, :], wfin_f[:, k, :])
                dve.drain().then_inc(en_w, 1)
            for t in range(NT):
                dve.wait_ge(en_y, t + 1)
                dve.tensor_tensor(xt(t), xt(t), ps[:, 1 + t % 2, :], ALU.add).then_inc(en_o, 1)

        @block.tensor
        def _(pe):
            pe.drain().then_inc(ix_r, 1)
            pe.drain().then_inc(pr_t, 1)
            pe.drain().then_inc(pr_mm, 1)
            pe.drain().then_inc(pr_st, 1)
            pe.drain().then_inc(pr_ev, 1)
            pe.drain().then_inc(pr_sp, 1)
            pe.drain().then_inc(hd_y, 1)
            pe.wait_ge(consts, 1)

            def norm_tr(l):
                for t in range(NT):
                    pe.wait_ge(ln_xn, NT * l + t + 1)
                    if t >= 2:
                        pe.wait_ge(ln_lo, NT * l + t - 1)
                    for k in range(NK):
                        last = pe.transpose(ps[:, t % 2, tile(k)], xn_t[:, t % 2, tile(k)], ident[:])
                    last.then_inc(ln_tr, 1)
                pe.wait_ge(ln_lo, NT * l + NT)

            norm_tr(0)
            pe.wait_ge(at_w, 1)
            for u in range(4):
                m, n = divmod(u, 2)
                c = slice(512 * n, 512 * n + 512)
                for k in range(NK):
                    last = mm3(pe, ps[:, u, :], wqkv_h[:, k, tile(m)], wqkv_l[:, k, tile(m)],
                               xn_h[:, k, c], xn_l[:, k, c], k == 0, k == NK - 1)
                last.then_inc(at_proj, 1)
            for t in range(NT):
                for k in range(NK):
                    last = mm3(pe, ps[:, 4 + t // 4, tile(t % 4)], xn_h[:, k, tile(t)], xn_l[:, k, tile(t)],
                               wqkv_h[:, k, tile(2)], wqkv_l[:, k, tile(2)], k == 0, k == NK - 1)
                if t % 4 == 3:
                    last.then_inc(at_proj, 1)
            pe.wait_ge(at_qkv, 4)
            for kind, i in ATT_ORDER:
                if kind == "S":
                    if i >= 2:
                        pe.wait_ge(at_exp, i - 1)
                    for n in range(2):
                        c = slice(512 * n, 512 * n + 512)
                        last = mm3(pe, ps[:, 2 * (i % 2) + n, :], qkT_h[:, 0, tile(i)], qkT_l[:, 0, tile(i)],
                                   qkT_h[:, 1, c], qkT_l[:, 1, c], True, True)
                    last.then_inc(at_s, 1)
                elif kind == "T":
                    pe.wait_ge(at_exp, i + 1)
                    for c in range(2):
                        if i == 0:
                            pe.wait_ge(at_v, c + 1)
                        else:
                            pe.wait_ge(at_lo, 2 * i + c - 1)
                        for k in range(4):
                            last = pe.transpose(ps[:, 4 + c, tile(k)], p0[:, i % 3, tile(4 * c + k)], ident[:])
                        last.then_inc(at_tr, 1)
                elif kind == "O":
                    pe.wait_ge(at_lo, 8 * (i + 1))
                    if i:
                        pe.wait_ge(at_ot, i)
                        pe.wait_ge(at_x, 4)
                    for k in range(NT):
                        last = mm3(pe, ps[:, 6, :], v_h[:, k, :], v_l[:, k, :], pTx_h[:, k, :], pTx_l[:, k, :],
                                   k == 0, k == NT - 1)
                    last.then_inc(at_o, 1)
                else:
                    pe.wait_ge(at_ot, i // 4 + 1)
                    if i >= 2:
                        pe.wait_ge(at_x, i - 1)
                    mm3(pe, ps[:, 7 - i % 2, :], oT[:, 0, tile(i % 4)], oT[:, 1, tile(i % 4)], wo_h[:], wo_l[:],
                        True, True).then_inc(at_y, 1)
            norm_tr(1)
            pe.wait_ge(wt_tot, 1)
            pe.matmul(ps[:, 7, 0:WCHUNKS], ones[:], absum[:], start=True, stop=True).then_inc(wt_tot, 1)
            meet(pe, 1)

            with pe.Fori(0, 2) as half:
                tokens = ds(half * 512, 512)

                def transposes(g, par, k):
                    pe.wait_ge(ff_we, 3 * g + k + 1)
                    pe.wait_ge(ff_lo, 3 * g + k + 1)
                    for c in range(NK):
                        last = pe.transpose(ps[:, 6 + (3 * par + k) % 2, tile(c)], weff[:, k, tile(c)], ident[:])
                    last.then_inc(ff_tr, 1)

                def project(g, par, k, done):
                    pe.wait_ge(ff_lo, 3 * g + k + 3)
                    for c in range(NK):
                        last = mm3(pe, ps[:, 4 + k, :], wc_h[:, par, k, tile(c)], wc_l[:, par, k, tile(c)],
                                   xn_h[:, c, tokens], xn_l[:, c, tokens], c == 0, c == NK - 1)
                    last.then_inc(done, 1)

                def down(g, par, first=False, last=False):
                    pe.wait_ge(ff_h, g + 1)
                    pe.wait_ge(ff_lo, 3 * g + 5)
                    for i in range(4):
                        one = mm3(pe, ps[:, i, :], hT_h[:, par, tile(i)], hT_l[:, par, tile(i)],
                                  wc_h[:, par, 2, :], wc_l[:, par, 2, :], first, last)
                        if last:
                            one.then_inc(ff_y, 1)

                def step(s, par, before="run", last=False):
                    g = half * NI + s
                    if not last:
                        transposes(g + 1, 1 - par, 0)
                    pe.wait_ge(ff_mul, g + 1)
                    project(g, par, 0, ff_gate)
                    if not last:
                        transposes(g + 1, 1 - par, 1)
                    project(g, par, 1, ff_up)
                    if before:
                        down(g - 1, 1 - par, first=before == "first")
                    if not last:
                        transposes(g + 1, 1 - par, 2)

                for k in range(3):
                    transposes(half * NI, 0, k)
                step(0, 0, before="")
                pe.wait_ge(ff_x, 4 * half + 1)
                step(1, 1, before="first")
                with pe.Fori(2, NI - 2, 2) as s:
                    step(s, 0)
                    step(s + 1, 1)
                step(NI - 2, 0)
                step(NI - 1, 1, last=True)
                down(half * NI + NI - 1, 1, last=True)
            meet(pe, 2)
            norm_tr(2)
            pe.wait_ge(lt_w, 1)
            for t in range(NT):
                if t >= 2:
                    pe.wait_ge(lt_ev, t - 1)
                for k in range(NK):
                    last = mm3(pe, ps[:, 2 + t % 2, 0:LATW], xn_h[:, k, tile(t)], xn_l[:, k, tile(t)],
                               wlat_h[:, k, :], wlat_l[:, k, :], k == 0, k == NK - 1)
                last.then_inc(lt_mm, 1)

            pe.wait_ge(ix_w, 1)
            for b in range(2):
                c = slice(512 * b, 512 * b + 512)
                for k in range(NK):
                    last = mm3(pe, ps[:, b, :], iwq_h[:, k, :], iwq_l[:, k, :], xn_h[:, k, c], xn_l[:, k, c],
                               k == 0, k == NK - 1)
                last.then_inc(ix_q, 1)

            def index_project(step, late, par):
                pe.wait_ge(ix_w, step + 2)
                pe.wait_ge(ix_qlo, step + 1)
                c = slice(512, 1024) if late else slice(0, 512)
                for k in range(NK):
                    last = mm3(pe, ps[:, par, :], iwq_h[:, k, :], iwq_l[:, k, :], xn_h[:, k, c], xn_l[:, k, c],
                               k == 0, k == NK - 1)
                last.then_inc(ix_q, 1)

            pe.wait_ge(lt_norm, 1)
            for t in range(NT):
                if t >= 2:
                    pe.wait_ge(lt_lo, t - 1)
                b = 4 + t % 2
                pe.transpose(ps[:, b, 0:P], latn[:, t, 0:P], ident[:])
                pe.transpose(ps[0:QR - P, b, P:2 * P], latn[:, t, P:QR], ident[:])
                pe.transpose(ps[:, b, 2 * P:3 * P], latn[:, t, QR:QR + P], ident[:])
                pe.transpose(ps[:, b, 3 * P:4 * P], latn[:, t, QR + KR:QR + KR + P], ident[:]).then_inc(lt_tr, 1)
            pe.wait_ge(lt_lo, NT)

            def index_scores(step, late, par):
                base_tile, tiles = index_tiles(step, late, par)
                pe.wait_ge(ix_qlo, step + 3)
                for k, t, slot in tiles:
                    w = (t + 1) * P
                    pe.wait_ge(ix_r, base_tile + k)
                    for b in range(1 if t < 4 else 2):
                        c = slice(512 * b, min(w, 512 * b + 512))
                        last = mm3(pe, ps[:, 2 + 2 * slot + b, 0:c.stop - c.start], iqT_h[:, par, tile(t % 4)],
                                   iqT_l[:, par, tile(t % 4)], ikT_h[:, c], ikT_l[:, c], True, True)
                    last.then_inc(ix_s, 1)

            def late_work(step, late, late_next, par):
                index_project(step + 1, late_next, 1 - par)
                index_scores(step, late, par)

            def early_work(step, late, late_next, par):
                j = step - IDXH
                if late_next is not None:
                    index_project(step + 1, late_next, 1 - par)
                wait_apart(pe, pr_ldq, 48 * j + 48)
                wait_apart(pe, pr_ev, j + 1)
                for a in range(4):
                    last = pe.transpose(ps[:, 6, a * KR:(a + 1) * KR], kvb_raw[:, tile(a)], ident[0:KR, 0:KR])
                last.then_inc(pr_t, 1)
                for h in range(2):
                    pe.transpose(ps[:, 7, h * QR:h * QR + P], qb_raw[:, 0, h * QKD:h * QKD + NOPE], ident[:])
                    last = pe.transpose(ps[:, 7, h * QR + P:(h + 1) * QR],
                                        qb_raw[0:QR - P, 1, h * QKD:h * QKD + NOPE], ident[0:QR - P, 0:QR - P])
                last.then_inc(pr_t, 1)
                index_scores(step, late, par)
                pe.wait_ge(pr_tev, 2 * j + 2)
                for h in range(2):
                    c = slice(256 + h * KR, 256 + (h + 1) * KR)
                    pe.matmul(ps[:, 6, c], qbT[:, h, 0:P], kvbT[:, 2 * h, :], start=True, stop=True)
                    c = slice(384 + h * KR, 384 + (h + 1) * KR)
                    pe.matmul(ps[0:QR - P, 6, c], qbT[:, h, P:QR], kvbT[:, 2 * h, :], start=True, stop=True)
                pe.wait_ge(pr_ldo, 16 * j + 16)
                for h in range(2):
                    last = pe.matmul(ps[h * KR:(h + 1) * KR, 7, :], kvbT[:, 2 * h + 1, :], ow_raw[:, h, :],
                                     start=True, stop=True)
                last.then_inc(pr_mm, 1)

            index_project(0, True, 0)
            late_steps(pe, late_work)
            early_steps(pe, early_work)
            meet(pe, 3)

            def pair_work(j, par, last, order=PE_ORDER):
                for kind, i, p in steps(order, j, last):
                    if kind == "S":
                        h, t = divmod(i, NT)
                        w = (t + 1) * P
                        q = par if i >= 4 else 1 - par
                        if i in (0, 4):
                            pe.wait_ge(hd_qlo, 2 * p + i // 4 + 1)
                            pe.wait_ge(hd_qalo, 2 * p + i // 4 + 1)
                        if i in (4, 5):
                            pe.wait_ge(hd_x, NT * p + i + 2)
                        if i >= 2 or order == PE_ORDER:
                            pe.wait_ge(hd_max, 16 * p + i - 1)
                        for b in range(1 if t < 4 else 2):
                            c = slice(512 * b, min(w, 512 * b + 512))
                            done = mm3(pe, ps[:, 2 * (i % 2) + b, 0:c.stop - c.start], qc_h[q][:, h, tile(t)],
                                       qc_l[q][:, h, tile(t)], latT_h[:, 2 + h, c], latT_l[:, 2 + h, c], True, True)
                        done.then_inc(hd_s, 1)
                    elif kind == "T":
                        t = i % NT
                        pe.wait_ge(hd_p, 16 * p + i + 1)
                        for c, g in GROUPS[i]:
                            pe.wait_ge(hd_lo, NG * p + g + 1)
                            if g == 0:
                                pe.wait_ge(hd_rm, 4 * p + 4)
                            if g == 1:
                                pe.wait_ge(hd_x, NT * p + NT)
                            for k in range(min(4, t + 1 - 4 * c)):
                                done = pe.transpose(ps[:, 4 + g % 2, tile(k)], pm[:, i % 4, tile(4 * c + k)], ident[:])
                            done.then_inc(hd_tr, 1)
                    elif kind == "V":
                        h, b = divmod(i, 2)
                        end = GROUPS[4 * i + 3][-1][1]
                        ph, pl = (pTa_h, pTa_l) if b == 0 else (pTx_h, pTx_l)
                        pe.wait_ge(hd_lo, NG * p + end + 3)
                        pe.wait_ge(hd_of, 4 * p + i + 1)
                        if i == 0 and not last:
                            pe.wait_ge(hd_rm, 4 * p + 6)
                        elif i == 0:
                            pe.wait_ge(hd_qalo, 2 * p + 2)
                        nk = 4 * b + 4
                        for k in range(nk):
                            q = slice(max(0, k - 4 * b) * P, 512)
                            v = v3[:, k, h * KR:h * KR + P]
                            pe.matmul(ps[:, 6, q], v, pl[:, k, q], start=k == 0, stop=False)
                            done = pe.matmul(ps[:, 6, q], v, ph[:, k, q], start=False, stop=k == nk - 1)
                        done.then_inc(hd_o, 1)
                    elif kind == "Q":
                        if i == 0:
                            pe.wait_ge(hd_ldq, 64 * p + 64)
                            if order == PE_ORDER:
                                pe.wait_ge(hd_x, NT * p - 3)
                        elif i == 1:
                            if order == PE_ORDER:
                                pe.wait_ge(hd_qalo, 2 * p)
                        elif i == 2:
                            pe.wait_ge(hd_rm, 4 * p + 1)
                        elif i == 3:
                            pe.wait_ge(hd_qalo, 2 * p + 1)
                        elif i == 4:
                            if order == PE_ORDER:
                                pe.wait_ge(hd_lo, NG * p + 1)
                        elif i == 5:
                            pe.wait_ge(hd_rm, 4 * p + 2)
                            pe.wait_ge(hd_of, 4 * p + 1)
                        w, c = (1, 2, 0)[i % 3], slice(512 * (i // 3), 512 * (i // 3) + 512)
                        for k in range(2):
                            done = mm3(pe, ps[:, Q_BANKS[i], :], wq_h[:, k, tile(w)], wq_l[:, k, tile(w)],
                                       latT_h[:, k, c], latT_l[:, k, c], k == 0, k == 1)
                        done.then_inc(hd_q, 1)
                    elif kind == "Y":
                        pe.wait_ge(hd_olo, 4 * p + (3 if i < 4 else 4))
                        pe.wait_ge(hd_ldu, 32 * p + 32)
                        if i == 0 and not last:
                            pe.wait_ge(hd_rm, 4 * p + 7)
                        elif i in (1, 2):
                            pe.wait_ge(hd_max, 16 * p + 16)
                        elif i == 3:
                            pe.wait_ge(hd_lo, NG * (p + 1) + 2)
                        elif i >= 4:
                            pe.wait_ge(hd_x, NT * p + NT + i - 3)
                        mm3(pe, ps[:, Y_BANKS[i], :], ol_h[:, tile(i)], ol_l[:, tile(i)], wuvo_h[:], wuvo_l[:],
                            True, True).then_inc(hd_y, 1)

            pe.wait_ge(hd_wz, 1)
            pair_work(-1, 1, False, "Q0 Q1 Q2 Q3 Q4 Q5 S16 S17 S18 S19")
            with pe.Fori(0, PAIRS // 2 - 1) as q:
                pair_work(2 * q, 0, False)
                pair_work(2 * q + 1, 1, False)
            pair_work(PAIRS - 2, 0, False)
            pair_work(PAIRS - 1, 1, True)
            meet(pe, 4)
            norm_tr(3)
            pe.wait_ge(ld_e, 16 * (3 + NK + LORA_N))
            for k in range(NK):
                last = pe.transpose(ps[:, 0, tile(k)], lB_sb[:, k, :], ident[:])
            last.then_inc(en_tb, 1)
            for k in range(NK):
                for c in range(NK):
                    last = pe.transpose(ps[:, 1 + k, tile(c)], lW_sb[:, c, tile(k)], ident[:])
                last.then_inc(en_tw, 1)
            pe.wait_ge(en_bt, 1)
            for k in range(NK):
                pe.matmul(ps[:, (5, 6, 7, 0)[k], :], lA_sb[:, tile(k)], lBT[:], start=True, stop=True).then_inc(en_mm, 1)
            pe.wait_ge(en_w, NK)
            for t in range(NT):
                if t >= 2:
                    pe.wait_ge(en_o, t - 1)
                for k in range(NK):
                    last = mm3(pe, ps[:, 1 + t % 2, :], xn_h[:, k, tile(t)], xn_l[:, k, tile(t)],
                               wfin_h[:, k, :], wfin_l[:, k, :], k == 0, k == NK - 1)
                last.then_inc(en_y, 1)


_INS = ['L0_attn_x', 'L0_attn_Wqkv', 'L0_attn_bqkv', 'L0_attn_Wo', 'L0_attn_bo', 'L0_ffn_w1', 'L0_ffn_mean_w1',
        'L0_ffn_w2', 'L0_ffn_mean_w2', 'L0_ffn_w3', 'L0_ffn_mean_w3', 'L1_attn_q_a_w', 'L1_attn_q_a_norm_w',
        'L1_attn_q_b_w', 'L1_attn_kv_a_w', 'L1_attn_kv_a_norm_w', 'L1_attn_kv_b_w', 'L1_attn_o_w',
        'L1_attn_idx_wq_w', 'L1_attn_idx_wk_w', 'L1_attn_idx_weights_w', 'L1_ffn_lora_A', 'L1_ffn_lora_B',
        'L1_ffn_W', 'L1_ffn_bias', 'L1_ffn_lora_weights']


def rope_tables():
    inv = (np.float32(1.0) / np.float32(10000.0) ** (np.arange(0, ROPE, 2, dtype=np.float32) / np.float32(ROPE)))
    ang = np.arange(S, dtype=np.float32)[:, None] * inv.astype(np.float32)[None, :]
    cos, sin = np.cos(ang).astype(np.float32), np.sin(ang).astype(np.float32)
    sign = np.where(np.arange(ROPE) % 2 == 0, -1.0, 1.0).astype(np.float32)
    scale = np.float32(-float(QKD) ** -0.5)
    cos_q = np.tile(np.repeat(cos, 2, axis=1).T, (2, 1)) * scale
    sin_q = np.tile((np.repeat(sin, 2, axis=1) * sign).T, (2, 1)) * scale
    cos_k, sin_k = (np.ascontiguousarray(a.reshape(NT, P, ROPE // 2).transpose(1, 0, 2)) for a in (cos, sin))
    return {"cos_q": np.ascontiguousarray(cos_q), "sin_q": np.ascontiguousarray(sin_q), "cos_k": cos_k, "sin_k": sin_k}


def kernel(**inputs):
    import concourse.bacc as _bacc
    from concourse.bass_utils import run_bass_kernel_spmd as _run

    nc = _bacc.Bacc("TRN2", target_bir_lowering=False, num_devices=1)
    arrays, args = {}, []
    for name, a in [(n, inputs[n]) for n in _INS] + list(rope_tables().items()):
        a = np.ascontiguousarray(a)
        arrays[f"in_{name}"] = a
        args.append(nc.dram_tensor(f"in_{name}", a.shape, F32, kind="ExternalInput").ap())
    args.append(nc.dram_tensor("out", (1, S, HID), F32, kind="ExternalOutput").ap())
    for name, shape in (("wq", (2, QR, PAIRS * 384)), ("wuvo", (2, PAIRS * P, HID))):
        args.append(nc.dram_tensor(name, shape, F32).ap())
    build(nc, *args)
    return _run(nc, [arrays], core_ids=[0]).results[0]["out"]
```
